# Optimizing a Trainium2 kernel written in Bass

```python
import numpy as np
import jax
import jax.numpy as jnp

def _softmax(x, axis=-1):
    return jax.nn.softmax(x, axis=axis)

def _gelu(x):
    return jax.nn.gelu(x, approximate=True)

def _silu(x):
    return jax.nn.silu(x)

def _sigmoid(x):
    return jax.nn.sigmoid(x)

def _layernorm(x, axis=-1, eps=1e-05):
    m = jnp.mean(x, axis=axis, keepdims=True)
    v = jnp.var(x, axis=axis, keepdims=True)
    return (x - m) / jnp.sqrt(v + eps)

def _scatter_add(tgt, idx, src, axis=0):
    return tgt.at[idx].add(src)

def _segment_sum(src, seg, n):
    return jax.ops.segment_sum(src, seg, n)
kernel_name = 'mk_vit_tower_d1_tok_img256_r4_248e32'

def setup_inputs(seed: int=0):
    np.random.seed(seed)
    _w = jnp.asarray

    def _rec_inputs():
        import jax
        import jax.numpy as jnp
        _rk = jax.random.key(seed)
        x = -0.000125008 + 0.999885 * jax.random.normal(jax.random.fold_in(_rk, 1), (32, 64, 64, 64), jnp.float32)
        return x
    x = _rec_inputs()

    def _L0_tok_setup():
        import jax, jax.numpy as jnp
        import numpy as np
        B, C, H, W = (32, 64, 64, 64)
        STRIDE, HEADS = (4, 8)

        def _ln(x, w, b):
            mu = x.mean(-1, keepdims=True)
            var = ((x - mu) ** 2).mean(-1, keepdims=True)
            return (x - mu) * jax.lax.rsqrt(var + 1e-05) * w + b
        key = jax.random.key(seed)
        ks = jax.random.split(key, 4)
        return {'features': jax.random.normal(ks[0], (B, C, H, W), dtype=jnp.float32), 'ln_q_w': jnp.ones((C,), jnp.float32), 'ln_q_b': jnp.zeros((C,), jnp.float32), 'Wq': jax.random.normal(ks[1], (C, C), dtype=jnp.float32) * 0.02, 'ln_kv_w': jnp.ones((C,), jnp.float32), 'ln_kv_b': jnp.zeros((C,), jnp.float32), 'Wkv': jax.random.normal(ks[2], (2 * C, C), dtype=jnp.float32) * 0.02, 'proj_w': jax.random.normal(ks[3], (C, C), dtype=jnp.float32) * 0.02, 'proj_b': jnp.zeros((C,), jnp.float32), 'conv_stride': STRIDE, 'num_heads': HEADS}
    _L0_tok_all = _L0_tok_setup()
    _L0_tok_in = {k: v for k, v in _L0_tok_all.items() if k in ('ln_q_w', 'ln_q_b', 'Wq', 'ln_kv_w', 'ln_kv_b', 'Wkv', 'proj_w', 'proj_b')}
    del _L0_tok_all

    def _L0_attn_setup():
        import jax, jax.numpy as jnp
        import numpy as np
        from jax import lax

        def _scan_combine(c1, c2):
            a1, b1 = c1
            a2, b2 = c2
            return (a1 * a2, a2 * b1 + b2)
        key = jax.random.key(seed)
        ks = jax.random.split(key, 6)
        B, L, Cin, N, Cout = (4, 1024, 64, 128, 64)
        s = 0.02
        return {'x': jax.random.normal(ks[0], (B, L, Cin), dtype=jnp.float32), 'Wx': jax.random.normal(ks[1], (Cin, N), dtype=jnp.float32) * s, 'bx': jnp.zeros((N,), dtype=jnp.float32), 'Wbc': jax.random.normal(ks[2], (Cin, 2 * N), dtype=jnp.float32) * s, 'bbc': jnp.zeros((2 * N,), dtype=jnp.float32), 'Wd': jax.random.normal(ks[3], (Cin, N), dtype=jnp.float32) * s, 'bd': jnp.zeros((N,), dtype=jnp.float32), 'Wy': jax.random.normal(ks[4], (N, Cout), dtype=jnp.float32) * s, 'by': jnp.zeros((Cout,), dtype=jnp.float32)}
    _L0_attn_all = _L0_attn_setup()
    _L0_attn_in = {k: v for k, v in _L0_attn_all.items() if k in ('Wx', 'bx', 'Wbc', 'bbc', 'Wd', 'bd', 'Wy', 'by')}
    del _L0_attn_all

    def _L0_ffn_setup():
        import jax, jax.numpy as jnp
        import numpy as np
        INPUT_WIDTH = 64
        DEPTH = 7
        OUTPUT_WIDTH = 64
        N_NODES = 2 ** (DEPTH + 1) - 1
        key = jax.random.key(seed)
        k_x, k_w1, k_w2 = jax.random.split(key, 3)
        init1 = 1.0 / np.sqrt(INPUT_WIDTH)
        x = jax.random.normal(k_x, (2, 256, INPUT_WIDTH), dtype=jnp.float32)
        w1s = jax.random.uniform(k_w1, (N_NODES, INPUT_WIDTH), jnp.float32, -init1, init1)
        b1s = jnp.zeros((N_NODES,), jnp.float32)
        w2s = jax.random.uniform(k_w2, (N_NODES, INPUT_WIDTH, OUTPUT_WIDTH), jnp.float32, -init1, init1)
        b2s = jnp.zeros((N_NODES, OUTPUT_WIDTH), jnp.float32)
        return {'x': x, 'w1s': w1s, 'b1s': b1s, 'w2s': w2s, 'b2s': b2s}
    _L0_ffn_all = _L0_ffn_setup()
    _L0_ffn_in = {k: v for k, v in _L0_ffn_all.items() if k in ('w1s', 'b1s', 'w2s', 'b2s')}
    del _L0_ffn_all
    return {'x': x, 'L0_tok_ln_q_w': _L0_tok_in['ln_q_w'], 'L0_tok_ln_q_b': _L0_tok_in['ln_q_b'], 'L0_tok_Wq': _L0_tok_in['Wq'], 'L0_tok_ln_kv_w': _L0_tok_in['ln_kv_w'], 'L0_tok_ln_kv_b': _L0_tok_in['ln_kv_b'], 'L0_tok_Wkv': _L0_tok_in['Wkv'], 'L0_tok_proj_w': _L0_tok_in['proj_w'], 'L0_tok_proj_b': _L0_tok_in['proj_b'], 'L0_attn_Wx': _L0_attn_in['Wx'], 'L0_attn_bx': _L0_attn_in['bx'], 'L0_attn_Wbc': _L0_attn_in['Wbc'], 'L0_attn_bbc': _L0_attn_in['bbc'], 'L0_attn_Wd': _L0_attn_in['Wd'], 'L0_attn_bd': _L0_attn_in['bd'], 'L0_attn_Wy': _L0_attn_in['Wy'], 'L0_attn_by': _L0_attn_in['by'], 'L0_ffn_w1s': _L0_ffn_in['w1s'], 'L0_ffn_b1s': _L0_ffn_in['b1s'], 'L0_ffn_w2s': _L0_ffn_in['w2s'], 'L0_ffn_b2s': _L0_ffn_in['b2s']}

def reference(x, L0_tok_ln_q_w, L0_tok_ln_q_b, L0_tok_Wq, L0_tok_ln_kv_w, L0_tok_ln_kv_b, L0_tok_Wkv, L0_tok_proj_w, L0_tok_proj_b, L0_attn_Wx, L0_attn_bx, L0_attn_Wbc, L0_attn_bbc, L0_attn_Wd, L0_attn_bd, L0_attn_Wy, L0_attn_by, L0_ffn_w1s, L0_ffn_b1s, L0_ffn_w2s, L0_ffn_b2s):
    import jax
    import jax.numpy as jnp

    def _L0_tok_ref(features, ln_q_w, ln_q_b, Wq, ln_kv_w, ln_kv_b, Wkv, proj_w, proj_b, conv_stride, num_heads):
        import jax, jax.numpy as jnp
        import numpy as np
        B, C, H, W = (32, 64, 64, 64)
        STRIDE, HEADS = (4, 8)

        def _ln(x, w, b):
            mu = x.mean(-1, keepdims=True)
            var = ((x - mu) ** 2).mean(-1, keepdims=True)
            return (x - mu) * jax.lax.rsqrt(var + 1e-05) * w + b
        s = conv_stride
        b, c, hh, ww = features.shape
        h, w = (hh // s, ww // s)
        hw, n, d = (h * w, s * s, c // num_heads)
        scale = c ** (-0.5)
        x = features.reshape(b, c, h, s, w, s)
        reduce_feats = x.mean((3, 5)).reshape(b, c, hw).transpose(0, 2, 1)
        unf = x.transpose(0, 1, 2, 4, 3, 5).reshape(b, c, hw, n).transpose(0, 2, 3, 1)
        q = _ln(reduce_feats, ln_q_w, ln_q_b) @ Wq.T
        q = q.reshape(b, hw, num_heads, d).transpose(0, 2, 1, 3)
        kv = _ln(unf, ln_kv_w, ln_kv_b) @ Wkv.T
        kv = kv.reshape(b, hw, n, 2, num_heads, d).transpose(3, 0, 4, 1, 2, 5)
        k, v = (kv[0], kv[1])
        attn = jax.nn.softmax(jnp.einsum('bhpd,bhpnd->bhpn', q * scale, k), axis=-1)
        aggre = jnp.einsum('bhpn,bhpnd->bhpd', attn, v)
        aggre = aggre.transpose(0, 2, 1, 3).reshape(b, hw, c)
        return reduce_feats + aggre @ proj_w.T + proj_b

    def _L0_attn_ref(x, Wx, bx, Wbc, bbc, Wd, bd, Wy, by):
        import jax, jax.numpy as jnp
        import numpy as np
        from jax import lax

        def _scan_combine(c1, c2):
            a1, b1 = c1
            a2, b2 = c2
            return (a1 * a2, a2 * b1 + b2)
        x_proj = x @ Wx + bx
        BC = x @ Wbc + bbc
        delta = x @ Wd + bd
        Bm, C = jnp.split(BC, 2, axis=-1)
        A_bar = jnp.exp(-jax.nn.softplus(delta))
        B_bar = (1.0 - A_bar) * Bm
        u = B_bar * x_proj
        _, h = lax.associative_scan(_scan_combine, (A_bar, u), axis=1)
        y = C * h
        return y @ Wy + by

    def _L0_ffn_ref(x, w1s, b1s, w2s, b2s):
        import jax, jax.numpy as jnp
        import numpy as np
        INPUT_WIDTH = 64
        DEPTH = 7
        OUTPUT_WIDTH = 64
        N_NODES = 2 ** (DEPTH + 1) - 1
        B, S, D = x.shape
        flat_x = x.reshape(B * S, D)
        T = flat_x.shape[0]
        current = jnp.zeros((T,), dtype=jnp.int32)
        all_nodes = []
        all_logits = []
        for _ in range(DEPTH + 1):
            all_nodes.append(current)
            score = jnp.einsum('td,td->t', flat_x, w1s[current]) + b1s[current]
            all_logits.append(score)
            choice = ((jnp.sign(score) + 1.0) / 2.0).astype(jnp.int32)
            current = current * 2 + choice + 1
        logits = jnp.stack(all_logits, axis=1)
        path_weights = jax.nn.gelu(jnp.abs(logits), approximate=False)
        out = jnp.zeros((T, OUTPUT_WIDTH), dtype=x.dtype)
        for i in range(DEPTH + 1):
            nodes_i = all_nodes[i]
            t_i = jnp.einsum('td,tdo->to', flat_x, w2s[nodes_i]) + b2s[nodes_i]
            out = out + t_i * path_weights[:, i][:, None]
        return out.reshape(B, S, OUTPUT_WIDTH)
    h = _L0_tok_ref(x, L0_tok_ln_q_w, L0_tok_ln_q_b, L0_tok_Wq, L0_tok_ln_kv_w, L0_tok_ln_kv_b, L0_tok_Wkv, L0_tok_proj_w, L0_tok_proj_b, 4, 8)
    h = h + _L0_attn_ref(_layernorm(h, axis=-1), L0_attn_Wx, L0_attn_bx, L0_attn_Wbc, L0_attn_bbc, L0_attn_Wd, L0_attn_bd, L0_attn_Wy, L0_attn_by)
    h = h + _L0_ffn_ref(_layernorm(h, axis=-1), L0_ffn_w1s, L0_ffn_b1s, L0_ffn_w2s, L0_ffn_b2s)
    return h

_drawn_inputs = setup_inputs


def setup_inputs(seed=0):
    import zlib

    import numpy as np

    out = dict(_drawn_inputs(seed))
    spreads = {'L0_tok_ln_q_w': (1.0, 0.6),
     'L0_tok_ln_q_b': (0.0, 2.0),
     'L0_tok_ln_kv_w': (1.0, 0.2),
     'L0_tok_ln_kv_b': (0.0, 0.1),
     'L0_tok_proj_b': (0.0, 0.1),
     'L0_attn_bx': (0.0, 0.1),
     'L0_attn_bbc': (0.0, 0.1),
     'L0_attn_bd': (0.0, 0.8),
     'L0_attn_by': (0.0, 0.1),
     'L0_ffn_b1s': (0.0, 0.1),
     'L0_ffn_b2s': (0.0, 0.1)}
    factors = {'L0_attn_Wd': 3.392, 'L0_tok_Wq': 2.701}
    for name, (base, spread) in spreads.items():
        noise = np.random.default_rng([zlib.crc32(name.encode()), seed]).standard_normal(out[name].shape)
        drawn = base * np.exp(spread * noise) if base else spread * noise
        out[name] = jnp.asarray(drawn.astype(out[name].dtype))
    for name, factor in factors.items():
        out[name] = (out[name] * factor).astype(out[name].dtype)
    return out
```

```python
import numpy as np
import concourse.bass as bass
from concourse import mybir
from contextlib import ExitStack

F32 = mybir.dt.float32
F32R = mybir.dt.float32r
ALU = mybir.AluOpType
ACT = mybir.ActivationFunctionType
AX = mybir.AxisListType

P = 128
B, C, HW = 32, 64, 64
S = 4
TH = HW // S
TOK = TH * TH
NP = S * S
HEADS = 8
HD = C // HEADS
PIX = HW * HW
TILES = B // 2
CH = 512
NCH = PIX // CH
ORDER = [0, 2, 4, 6, 1, 3, 5, 7]
EPS = 1e-5


def tokenizer(nc, ctx, A, h1):
    def sb(name, shape, dt=F32):
        return ctx.enter_context(nc.sbuf_tensor(name, shape, dt))

    def bank(name):
        return ctx.enter_context(nc.psum_tensor(name, [P, CH], F32))

    def sem(name):
        return ctx.enter_context(nc.semaphore(name))

    x_v = A["x"].rearrange("(t b) c h w -> t (b c) (h w)", b=2)

    x = sb("x_px", [P, 2, PIX])
    x_hi = sb("x_hi", [P, 2, PIX], F32R)
    x_lo = sb("x_lo", [P, 2, PIX], F32R)
    x_sq = sb("x_sq", [P, NCH // 2, CH])
    v_sb = sb("v_sb", [P, NCH, CH])
    qk = sb("qk", [P, NCH // 2, CH])
    va = sb("va", [P, NCH, CH])
    pre1 = sb("pre1", [P, 1024])
    pre2 = sb("pre2", [P, TH, HW])
    rkv = sb("rkv", [P, CH])
    sc = sb("sc", [P, CH])
    ex = sb("ex", [P, CH])
    a_hi = sb("a_hi", [P, CH], F32R)
    a_lo = sb("a_lo", [P, CH], F32R)
    mx = sb("mx", [P, 2 * TH])
    sm = sb("sm", [P, 2 * TH])
    rc = sb("rc", [P, 2 * TH])
    px_sum = sb("px_sum", [P, TOK])
    q4 = sb("q4", [P, TH, HW])
    rs2 = sb("rs2", [P, 2 * TOK])
    rq = sb("rq", [P, TOK])
    qs = sb("qs", [P, TOK])
    w_ld = sb("w_ld", [P, 4, P])
    w_sc = sb("w_sc", [P, 3, P])
    w_hi = sb("w_hi", [P, 2, P], F32R)
    w_lo = sb("w_lo", [P, 2, P], F32R)
    gq = sb("gq", [P, P])
    vec = sb("vec", [P, 8])
    avg = sb("avg", [P, P])
    cen = sb("cen", [P, P])
    sel = sb("sel", [P, 2, 32])
    msel = sb("msel", [P, 2, 32])
    e_f = sb("e_f", [P, NCH, P])
    e_r = sb("e_r", [P, NCH, P], F32R)
    eps = sb("eps", [P, 1])

    b_k = [bank(f"b_k{i}") for i in range(2)]
    b_w = [bank(f"b_w{i}") for i in range(2)]
    b_s, b_m, b_q, b_b = bank("b_s"), bank("b_m"), bank("b_q"), bank("b_b")

    with ExitStack() as wctx:
        wsem = lambda n: wctx.enter_context(nc.semaphore(n))
        zeroed, loaded, masks, scaled, prod, folded = (wsem(n) for n in
            ("w_zeroed", "w_loaded", "w_masks", "w_scaled", "w_prod", "w_folded"))
        with nc.Block() as block:
            @block.sync
            def _(sp):
                for i, n in enumerate(("ln_q_w", "ln_q_b", "ln_kv_w", "ln_kv_b", "proj_b")):
                    for b in range(2):
                        sp.dma_start(vec[C * b:C * b + C, i:i + 1], A["L0_tok_" + n].rearrange("(c o) -> c o", o=1)).then_inc(loaded, 16)
                sp.wait_ge(zeroed, 1)
                for b in range(2):
                    s = slice(C * b, C * b + C)
                    sp.dma_start(w_ld[s, 0, s], A["WqT"]).then_inc(loaded, 16)
                    sp.dma_start(w_ld[s, 1, s], A["WkvT"][:, 0:C]).then_inc(loaded, 16)
                    sp.dma_start(w_ld[s, 2, s], A["WkvT"][:, C:2 * C]).then_inc(loaded, 16)
                    sp.dma_start(w_ld[s, 3, s], A["projT"]).then_inc(loaded, 16)
                sp.wait_ge(loaded, 16 * 18)

            @block.gpsimd
            def _(pool):
                g = nc.gpsimd
                n = [0]

                def step(ins):
                    ins.then_inc(masks, 1)
                    n[0] += 1
                    pool.wait_ge(masks, n[0])

                def band(view, fill_outside, lo_base, lo_pat, lo_mul, hi_base, hi_pat, hi_mul):
                    step(g.affine_select(out=view, in_=view, compare_op=ALU.is_ge, fill=fill_outside, base=lo_base,
                                         pattern=lo_pat, channel_multiplier=lo_mul))
                    step(g.affine_select(out=view, in_=view, compare_op=ALU.is_ge, fill=fill_outside, base=hi_base,
                                         pattern=hi_pat, channel_multiplier=hi_mul))

                step(g.memset(avg[:, :], 1.0 / C))
                for m in range(2):
                    v = avg[:, C * m:C * m + C]
                    band(v, 0.0, -C * m, [[0, C]], 1, C * m + C - 1, [[0, C]], -1)
                step(g.memset(cen[:, :], 0.0))
                step(g.affine_select(out=cen[:, :], in_=cen[:, :], compare_op=ALU.not_equal, fill=1.0, base=0,
                                     pattern=[[-1, P]], channel_multiplier=1))
                step(g.tensor_tensor(cen[:, :], cen[:, :], avg[:, :], ALU.subtract))
                step(g.memset(sel[:, :, :], 0.0))
                for e in range(2):
                    v = sel[:, e, 16 * e:16 * e + 16]
                    step(g.memset(v, 1.0))
                    band(v, 0.0, 0, [[-HD, 16]], 1, HD - 1, [[HD, 16]], -1)
                step(g.memset(msel[:, :, :], 0.0))
                for e in range(2):
                    for b in range(2):
                        v = msel[:, e, 16 * e + 8 * b:16 * e + 8 * b + 8]
                        step(g.memset(v, 1.0 / C))
                        band(v, 0.0, -C * b, [[0, 8]], 1, C * b + C - 1, [[0, 8]], -1)
                step(g.memset(e_f[:, :, :], 1.0))
                band(e_f[:, :, :], 0.0, 0, [[16 * HD, NCH], [1, P]], -HD, HD - 1, [[-16 * HD, NCH], [-1, P]], HD)
                step(g.memset(eps[:, :], EPS))

            @block.vector
            def _(v):
                nc.vector.memset(w_ld[:, :, :], 0.0).then_inc(zeroed, 1)
                v.wait_ge(loaded, 16 * 18)
                v.wait_ge(masks, 32)
                for i, w in ((0, 0), (1, 2), (2, 2)):
                    nc.vector.tensor_scalar(w_sc[:, i, :], w_ld[:, i, :], vec[:, w:w + 1], None, ALU.mult).then_inc(scaled, 1)
                nc.vector.tensor_copy(e_r[:, :, :], e_f[:, :, :]).then_inc(scaled, 1)
                v.wait_ge(prod, 1)
                for i in range(2):
                    nc.vector.tensor_copy(w_hi[:, i, :], b_k[0][:, P * (i + 1):P * (i + 2)]).then_inc(folded, 1)
                nc.vector.tensor_scalar(gq[:, :], b_k[0][:, 0:P], C ** -0.5, None, ALU.mult).then_inc(folded, 1)
                nc.vector.tensor_scalar(vec[:, 5:6], b_k[1][:, 0:1], C ** -0.5, None, ALU.mult).then_inc(folded, 1)
                nc.vector.tensor_copy(vec[:, 6:7], b_k[1][:, 1:2]).then_inc(folded, 1)
                v.wait_ge(folded, 5)
                for i in range(2):
                    nc.vector.tensor_tensor(w_lo[:, i, :], b_k[0][:, P * (i + 1):P * (i + 2)], w_hi[:, i, :].bitcast(F32),
                                            ALU.subtract).then_inc(folded, 1)
                v.wait_ge(prod, 2)
                nc.vector.tensor_tensor(vec[:, 7:8], b_w[0][:, 0:1], vec[:, 4:5], ALU.add).then_inc(folded, 1)

            @block.tensor
            def _(pe):
                pe.wait_ge(scaled, 4)
                for i in range(3):
                    nc.tensor.matmul(b_k[0][:, P * i:P * (i + 1)], cen[:, :], w_sc[:, i, :], start=True, stop=True)
                nc.tensor.matmul(b_k[1][:, 0:1], w_ld[:, 0, :], vec[:, 1:2], start=True, stop=True)
                nc.tensor.matmul(b_k[1][:, 1:2], w_ld[:, 2, :], vec[:, 3:4], start=True, stop=True).then_inc(prod, 1)
                pe.wait_ge(folded, 7)
                nc.tensor.matmul(b_w[0][:, 0:1], w_ld[:, 3, :], vec[:, 6:7], start=True, stop=True).then_inc(prod, 1)

    N = "x_in0 x_in1 split_hi split_lo squared pooled pooled_copied pooled_squared pooled_biased q_moments q_mean_sq q_var q_ln q_rstd q_product q_scaled q_ready " \
        "moments square_sums kv_mean_sq kv_var kv_clamped kv_ln kv_rstd k_product qk_ready scores scores_scaled scores_max scores_shifted exps " \
        "exp_sum exp_recip exps_scaled weights weights_hi weights_lo a_spread va_ready v_product v_copied " \
        "halved quartered attn_out h1_ready"
    class Z:
        pass
    z = {n: sem(n) for n in N.split()}
    x_in = [z["x_in0"], z["x_in1"]]

    def tile(k, o):
        return 2 * k + o, o % 2

    block = ctx.enter_context(nc.Block())

    STEADY = (TILES - 2) // 2

    @block.sync
    def _(sp):
        def load(k, o):
            t, par = tile(k, o)
            sp.dma_start(x[:, par, :], x_v[t, :, :] if isinstance(t, int) else x_v[bass.ds(t, 1), :, :].rearrange("o p n -> (o p) n")).then_inc(x_in[par], 16)

        load(0, 0)
        load(0, 1)

        def reload(k, o):
            t, par = tile(k, o)
            sp.wait_ge(z["split_lo"], 2 * t - 2)
            sp.wait_ge(z["pooled"], 2 * t - 2)
            sp.wait_ge(z["square_sums"], 2 * t - 2)
            load(k, o)

        with sp.Fori(1, STEADY + 1) as k:
            reload(k, 0)
            reload(k, 1)

    @block.scalar
    def _(act):
        a = nc.scalar

        def split(k, o, half, first=False):
            t, par = tile(k, o)
            s = slice(half * PIX // 2, (half + 1) * PIX // 2)
            a.activation(x_hi[:, par, s], x[:, par, s], ACT.Copy).then_inc(z["split_hi"], 1)

        def square(k, o, half, first=False):
            t, par = tile(k, o)
            if not (first and half == 0):
                act.wait_ge(z["square_sums"], 2 * t + half)
            src = x[:, par, :].rearrange("p (j e n) -> p j e n", e=2, n=CH)[:, :, half, :]
            a.activation(x_sq[:, :, :], src, ACT.Square).then_inc(z["squared"], 1)

        def q_front(k, o):
            t, par = tile(k, o)
            act.wait_ge(z["pooled"], 2 * t + 2)
            src = px_sum[:, :]
            a.activation(rs2[:, 0:TOK], src, ACT.Copy, scale=1.0 / NP).then_inc(z["pooled_copied"], 1)
            a.activation(rs2[:, TOK:2 * TOK], src, ACT.Square, scale=1.0 / NP).then_inc(z["pooled_squared"], 1)
            a.activation(h1[:, bass.ts(t, TOK)], src, ACT.Identity, scale=1.0 / NP, bias=vec[:, 7:8]).then_inc(z["pooled_biased"], 1)

        def q_moment(k, o):
            t, par = tile(k, o)
            act.wait_ge(z["q_moments"], t + 1)
            a.activation(rq[:, :], b_b[:, 0:TOK], ACT.Square).then_inc(z["q_mean_sq"], 1)

        def q_back(k, o):
            t, par = tile(k, o)
            act.wait_ge(z["q_var"], t + 1)
            a.activation(rq[:, :], rq[:, :], ACT.Ln, bias=eps[:, :]).then_inc(z["q_ln"], 1)
            act.wait_ge(z["q_ln"], t + 1)
            a.activation(rq[:, :], rq[:, :], ACT.Exp, scale=-0.5).then_inc(z["q_rstd"], 1)

        def q_final(k, o):
            t, par = tile(k, o)
            act.wait_ge(z["q_scaled"], t + 1)
            a.activation(q4[:, :, :].rearrange("p h (w s) -> p (h w) s", s=S),
                         qs[:, :].rearrange("p (n s) -> p n s", s=1).broadcast_to([P, TOK, S]),
                         ACT.Identity, bias=vec[:, 5:6]).then_inc(z["q_ready"], 1)

        def kv_mean(k, o):
            t, par = tile(k, o)
            act.wait_ge(z["moments"], t + 1)
            a.activation(rkv[:, :], b_m[:, :], ACT.Square).then_inc(z["kv_mean_sq"], 1)

        def kv_rstd(k, o):
            t, par = tile(k, o)
            act.wait_ge(z["kv_clamped"], t + 1)
            a.activation(rkv[:, :], rkv[:, :], ACT.Ln, bias=eps[:, :]).then_inc(z["kv_ln"], 1)
            act.wait_ge(z["kv_ln"], t + 1)
            a.activation(rkv[:, :], rkv[:, :], ACT.Exp, scale=-0.5).then_inc(z["kv_rstd"], 1)

        def copy_v(k, o, n):
            t, par = tile(k, o)
            act.wait_ge(z["v_product"], NCH * t + n + 1)
            a.activation(v_sb[:, n, :], b_w[n % 2][:, :], ACT.Copy).then_inc(z["v_copied"], 1)

        def softmax_exp(k, o):
            t, par = tile(k, o)
            act.wait_ge(z["scores_shifted"], 2 * t + 2)
            a.activation(ex[:, :], sc[:, :], ACT.Exp).then_inc(z["exps"], 1)

        def prepare(k, o, first=False):
            t, par = tile(k, o)
            act.wait_ge(x_in[par], 16 * (k + o // 2 + 1))
            if not (first or isinstance(t, int) and t < 2):
                act.wait_ge(z["v_product"], NCH * (t - 1))
            split(k, o, 0)
            split(k, o, 1)

        def step(k, o, last=False):
            kv_mean(k, o)
            if not last:
                prepare(k, o + 1)
            kv_rstd(k, o)
            if not last:
                square(k, o + 1, 0)
                q_front(k, o + 1)
            for n in range(0, 3):
                copy_v(k, o, n)
            softmax_exp(k, o)
            copy_v(k, o, 3)
            if not last:
                q_moment(k, o + 1)
            copy_v(k, o, 4)
            copy_v(k, o, 5)
            if not last:
                square(k, o + 1, 1)
                q_back(k, o + 1)
            copy_v(k, o, 6)
            copy_v(k, o, 7)
            if not last:
                q_final(k, o + 1)

        act.preload_act_table_set("natural_log_exp_and_others")
        prepare(0, 0, first=True)
        square(0, 0, 0, first=True)
        q_front(0, 0)
        q_moment(0, 0)
        square(0, 0, 1)
        q_back(0, 0)
        q_final(0, 0)
        step(0, 0)
        with act.Fori(0, STEADY) as k:
            step(k, 1)
            step(k, 2)
        step(STEADY, 1, last=True)

    @block.gpsimd
    def _(pool):
        g = nc.gpsimd

        def split(k, o, half, first=False):
            t, par = tile(k, o)
            s = slice(half * PIX // 2, (half + 1) * PIX // 2)
            if half == 0 and not first:
                pool.wait_ge(z["v_product"], NCH * (t - 1))
            pool.wait_ge(z["split_hi"], 2 * t + half + 1)
            g.tensor_tensor(x_lo[:, par, s], x[:, par, s], x_hi[:, par, s].bitcast(F32), ALU.subtract).then_inc(z["split_lo"], 1)

        def fold(k, o, half, first=False):
            t, par = tile(k, o)
            pool.wait_ge(z["va_ready"], NCH * t + 4 * half + 4)
            v = va[:, 4 * half:4 * half + 4, :].rearrange("p j (h s w) -> p (j h) s w", s=S, w=HW)
            p1 = pre1[:, :].rearrange("p (g s w) -> p g s w", s=2, w=HW)
            if not (first and half == 0):
                pool.wait_ge(z["quartered"], 2 * t + half)
            g.tensor_tensor(p1, v[:, :, 0:2, :], v[:, :, 2:4, :], ALU.add).then_inc(z["halved"], 1)
            pool.wait_ge(z["halved"], 2 * t + half + 1)
            if half == 0 and not first:
                pool.wait_ge(z["attn_out"], t)
            dst = pre2[:, :, :].rearrange("p (j e h) w -> p j e h w", e=2, h=2)[:, :, half, :, :]
            p1 = pre1[:, :].rearrange("p (j h s w) -> p j h s w", h=2, s=2, w=HW)
            g.tensor_tensor(dst, p1[:, :, :, 0, :], p1[:, :, :, 1, :], ALU.add).then_inc(z["quartered"], 1)

        def step(k, o, first=False, last=False):
            if not last:
                split(k, o + 1, 0, first=first)
            if not first:
                fold(k, o - 1, 0, first=isinstance(k, int) and 2 * k + o == 1)
            if not last:
                split(k, o + 1, 1)
            if not first:
                fold(k, o - 1, 1)

        split(0, 0, 0, first=True)
        split(0, 0, 1)
        step(0, 0, first=True)
        step(0, 1)
        with pool.Fori(1, STEADY) as k:
            step(k, 0)
            step(k, 1)
        step(STEADY, 0)
        step(STEADY, 1, last=True)
        fold(STEADY, 1, 0)
        fold(STEADY, 1, 1)

    @block.vector
    def _(v):
        d = nc.vector

        def pool_px(k, o):
            t, par = tile(k, o)
            v.wait_ge(x_in[par], 16 * (k + o // 2 + 1))
            if not (isinstance(t, int) and t == 0):
                v.wait_ge(z["pooled_biased"], t)
            for half in range(2):
                d.tensor_reduce(px_sum[:, half * TOK // 2:(half + 1) * TOK // 2].rearrange("p (h w) -> p h w", w=TH),
                                x[:, par, half * PIX // 2:(half + 1) * PIX // 2].rearrange("p (h s w u) -> p h w s u", h=TH // 2, s=S, u=S),
                                AX.XY, ALU.add).then_inc(z["pooled"], 1)

        def qk_mul(k, o, n):
            t, par = tile(k, o)
            j = ORDER[n]
            if n == 0:
                v.wait_ge(z["q_ready"], t + 1)
            v.wait_ge(z["k_product"], NCH * t + n + 1)
            if n % 4 == 0 and not (isinstance(t, int) and t == 0 and n == 0):
                v.wait_ge(z["scores"], 2 * t + n // 4)
            d.tensor_tensor(qk[:, n % 4, :].rearrange("p (h s w) -> p h s w", s=S, w=HW),
                            b_k[n % 2][:, :].rearrange("p (h s w) -> p h s w", s=S, w=HW),
                            q4[:, 2 * j:2 * j + 2, :].rearrange("p h (o w) -> p h o w", o=1).broadcast_to([P, 2, S, HW]),
                            ALU.mult).then_inc(z["qk_ready"], 1)

        def va_mul(k, o, n):
            t, par = tile(k, o)
            v.wait_ge(z["a_spread"], NCH * t + n + 1)
            if n == 0:
                v.wait_ge(z["v_copied"], NCH * (t + 1))
            if n % 4 == 0 and not (isinstance(t, int) and t == 0):
                v.wait_ge(z["halved"], 2 * t - 1 + n // 4)
            d.tensor_tensor(va[:, n, :], b_w[n % 2][:, :], v_sb[:, n, :], ALU.mult).then_inc(z["va_ready"], 1)

        def kv_var(k, o):
            t, par = tile(k, o)
            v.wait_ge(z["kv_mean_sq"], t + 1)
            v.wait_ge(z["square_sums"], 2 * t + 2)
            d.tensor_tensor(rkv[:, :], b_q[:, :], rkv[:, :], ALU.subtract).then_inc(z["kv_var"], 1)
            v.wait_ge(z["kv_var"], t + 1)
            d.tensor_scalar(rkv[:, :], rkv[:, :], 0.0, None, ALU.max).then_inc(z["kv_clamped"], 1)

        hs = lambda a, h: a[:, 256 * h:256 * h + 256].rearrange("p (s w u) -> p s w u", s=S, u=S)
        hb = lambda a, h: a[:, TH * h:TH * h + TH].rearrange("p (a w u) -> p a w u", a=1, u=1).broadcast_to([P, S, TH, S])

        def softmax_a(k, o):
            t, par = tile(k, o)
            v.wait_ge(z["scores"], 2 * t + 2)
            v.wait_ge(z["kv_rstd"], t + 1)
            d.tensor_tensor(sc[:, :], b_s[:, :], rkv[:, :], ALU.mult).then_inc(z["scores_scaled"], 1)
            v.wait_ge(z["scores_scaled"], t + 1)
            d.tensor_reduce(mx[:, :].rearrange("p (h w) -> p h w", w=TH),
                            sc[:, :].rearrange("p (h s w u) -> p h w s u", h=2, s=S, u=S), AX.XY, ALU.max).then_inc(z["scores_max"], 1)
            v.wait_ge(z["scores_max"], t + 1)
            for h in range(2):
                d.tensor_tensor(hs(sc, h), hs(sc, h), hb(mx, h), ALU.subtract).then_inc(z["scores_shifted"], 1)

        def softmax_b(k, o, first=False):
            t, par = tile(k, o)
            v.wait_ge(z["exps"], t + 1)
            d.tensor_reduce(sm[:, :].rearrange("p (h w) -> p h w", w=TH),
                            ex[:, :].rearrange("p (h s w u) -> p h w s u", h=2, s=S, u=S), AX.XY, ALU.add).then_inc(z["exp_sum"], 1)
            v.wait_ge(z["exp_sum"], t + 1)
            d.reciprocal(rc[:, :], sm[:, :]).then_inc(z["exp_recip"], 1)
            d.tensor_tensor(ex[:, :], ex[:, :], rkv[:, :], ALU.mult).then_inc(z["exps_scaled"], 1)
            v.wait_ge(z["exps_scaled"], t + 1)
            v.wait_ge(z["exp_recip"], t + 1)
            for h in range(2):
                d.tensor_tensor(hs(ex, h), hs(ex, h), hb(rc, h), ALU.mult).then_inc(z["weights"], 1)
            v.wait_ge(z["weights"], 2 * t + 2)
            if not first:
                v.wait_ge(z["a_spread"], NCH * t)
            d.tensor_copy(a_hi[:, :], ex[:, :]).then_inc(z["weights_hi"], 1)
            v.wait_ge(z["weights_hi"], t + 1)
            d.tensor_tensor(a_lo[:, :], ex[:, :], a_hi[:, :].bitcast(F32), ALU.subtract).then_inc(z["weights_lo"], 1)

        def q_var(k, o):
            t, par = tile(k, o)
            v.wait_ge(z["q_mean_sq"], t + 1)
            d.scalar_tensor_tensor(rq[:, :], rq[:, :], -1.0, b_b[:, TOK:2 * TOK], ALU.mult, ALU.add).then_inc(z["q_var"], 1)

        def q_scale(k, o):
            t, par = tile(k, o)
            v.wait_ge(z["q_rstd"], t + 1)
            v.wait_ge(z["q_product"], t + 1)
            d.tensor_tensor(qs[:, :], b_b[:, 0:TOK], rq[:, :], ALU.mult).then_inc(z["q_scaled"], 1)

        def finish(k, o):
            t, par = tile(k, o)
            v.wait_ge(z["attn_out"], t + 1)
            v.wait_ge(z["pooled_biased"], t + 1)
            dst = h1[:, bass.ts(t, TOK)]
            d.tensor_tensor(dst, b_b[:, 0:TOK], dst, ALU.add).then_inc(z["h1_ready"], 1)

        def step(k, o, first=False, last=False):
            kv_var(k, o)
            for n in range(NCH):
                qk_mul(k, o, n)
                if not first:
                    va_mul(k, o - 1, n)
            if not last:
                pool_px(k, o + 1)
            softmax_a(k, o)
            if not first:
                finish(k, o - 1)
            if not last:
                q_var(k, o + 1)
            softmax_b(k, o, first=first)
            if not last:
                q_scale(k, o + 1)

        pool_px(0, 0)
        q_var(0, 0)
        q_scale(0, 0)
        step(0, 0, first=True)
        step(0, 1)
        step(0, 2)
        with v.Fori(1, STEADY) as k:
            step(k, 1)
            step(k, 2)
        step(STEADY, 1, last=True)
        for n in range(NCH):
            va_mul(STEADY, 1, n)
        finish(STEADY, 1)

    @block.tensor
    def _(pe):
        mm = nc.tensor.matmul

        def px(buf, par, j):
            return buf[:, par, CH * j:CH * j + CH]

        def three(dst, w, par, j):
            mm(dst, w_hi[:, w, :], px(x_hi, par, j), start=True, stop=False)
            mm(dst, w_lo[:, w, :], px(x_hi, par, j), start=False, stop=False)
            return mm(dst, w_hi[:, w, :], px(x_lo, par, j), start=False, stop=True)

        def k_mm(k, o, n):
            t, par = tile(k, o)
            if n == 0:
                pe.wait_ge(z["split_lo"], 2 * t + 2)
            if not (isinstance(t, int) and t == 0 and n < 2):
                pe.wait_ge(z["qk_ready"], NCH * t + n - 1)
            three(b_k[n % 2][:, :], 0, par, ORDER[n]).then_inc(z["k_product"], 1)

        def v_mm(k, o, n, first=False):
            t, par = tile(k, o)
            if n < 2:
                if not first:
                    pe.wait_ge(z["va_ready"], NCH * (t - 1) + 7 + n)
            else:
                pe.wait_ge(z["v_copied"], NCH * t + n - 1)
            three(b_w[n % 2][:, :], 1, par, ORDER[n]).then_inc(z["v_product"], 1)

        def spread(k, o, n):
            t, par = tile(k, o)
            if n == 0:
                pe.wait_ge(z["weights_lo"], t + 1)
            if n < 2:
                pe.wait_ge(z["v_copied"], NCH * t + 7 + n)
            else:
                pe.wait_ge(z["va_ready"], NCH * t + n - 1)
            mm(b_w[n % 2][:, :], e_r[:, ORDER[n], :], a_hi[:, :], start=True, stop=False)
            mm(b_w[n % 2][:, :], e_r[:, ORDER[n], :], a_lo[:, :], start=False, stop=True).then_inc(z["a_spread"], 1)

        def scores(k, o, e):
            t, par = tile(k, o)
            pe.wait_ge(z["qk_ready"], NCH * t + 4 * e + 4)
            if e == 0 and not (isinstance(t, int) and t == 0):
                pe.wait_ge(z["scores_scaled"], t)
            for c in range(4):
                i = mm(b_s[32 * c:32 * c + 32, :], sel[:, e, :], qk[:, c, :], start=e == 0, stop=e == 1)
            i.then_inc(z["scores"], 1)

        def sums(k, o, e):
            t, par = tile(k, o)
            pe.wait_ge(z["squared"], 2 * t + e + 1)
            if e == 0 and not (isinstance(t, int) and t == 0):
                pe.wait_ge(z["kv_var"], t)
            for c in range(4):
                i = mm(b_m[32 * c:32 * c + 32, :], msel[:, e, :], px(x, par, 2 * c + e), start=e == 0, stop=e == 1)
            if e == 1:
                i.then_inc(z["moments"], 1)
            for c in range(4):
                i = mm(b_q[32 * c:32 * c + 32, :], msel[:, e, :], x_sq[:, c, :], start=e == 0, stop=e == 1)
            i.then_inc(z["square_sums"], 1)

        def q_moments(k, o):
            t, par = tile(k, o)
            pe.wait_ge(z["pooled_squared"], t + 1)
            pe.wait_ge(z["pooled_copied"], t + 1)
            if not (isinstance(t, int) and t < 2):
                pe.wait_ge(z["h1_ready"], t - 1)
            if not (isinstance(t, int) and t == 0):
                pe.wait_ge(z["q_scaled"], t)
            mm(b_b[:, :], avg[:, :], rs2[:, :], start=True, stop=True).then_inc(z["q_moments"], 1)

        def q_mm(k, o):
            t, par = tile(k, o)
            pe.wait_ge(z["q_var"], t + 1)
            mm(b_b[:, 0:TOK], gq[:, :], rs2[:, 0:TOK], start=True, stop=True).then_inc(z["q_product"], 1)

        def out_mm(k, o, last=False):
            t, par = tile(k, o)
            pe.wait_ge(z["quartered"], 2 * t + 2)
            pe.wait_ge(z["q_scaled"], t + (1 if last else 2))
            p2 = pre2[:, :, :].rearrange("p h (w u) -> p (h w) u", u=S)
            for u in range(S):
                i = mm(b_b[:, 0:TOK], w_ld[:, 3, :], p2[:, :, u], start=u == 0, stop=u == S - 1)
            i.then_inc(z["attn_out"], 1)

        def step(k, o, first=False, last=False):
            for n in range(NCH):
                k_mm(k, o, n)
                if not first:
                    spread(k, o - 1, n)
                if n == 5:
                    scores(k, o, 0)
            v_mm(k, o, 0, first=first)
            scores(k, o, 1)
            v_mm(k, o, 1, first=first)
            if not last:
                sums(k, o + 1, 0)
            v_mm(k, o, 2)
            if not first:
                out_mm(k, o - 1)
            v_mm(k, o, 3)
            if not last:
                q_moments(k, o + 1)
            v_mm(k, o, 4)
            v_mm(k, o, 5)
            if not last:
                q_mm(k, o + 1)
            v_mm(k, o, 6)
            v_mm(k, o, 7)
            if not last:
                sums(k, o + 1, 1)

        sums(0, 0, 0)
        q_moments(0, 0)
        q_mm(0, 0)
        sums(0, 0, 1)
        step(0, 0, first=True)
        with pe.Fori(0, STEADY) as k:
            step(k, 1)
            step(k, 2)
        step(STEADY, 1, last=True)
        for n in range(NCH):
            spread(STEADY, 1, n)
        out_mm(STEADY, 1, last=True)


N_ST = 128
NODES = 255
LEVELS = 8
NT = TILES * 4
ROW = 144
UNITS = 12


def scan_and_logits(nc, ctx, A, h1, pay, lg):
    def sb(name, shape, dt=F32):
        return ctx.enter_context(nc.sbuf_tensor(name, shape, dt))

    def sem(name):
        return ctx.enter_context(nc.semaphore(name))

    w_p = sb("w_p", [P, 2, 4, N_ST])
    w_y = sb("w_y", [P, C])
    b_p = sb("b_p", [P, 5])
    w1 = sb("w1", [P, 2, 256])
    b1 = sb("b1", [P, 256])
    avg = sb("avg2", [P, P])
    ident = sb("ident", [P, P])
    eps = sb("eps2", [P, 1])
    xc2, sq2, r2, xn2 = (sb(n, [P, TOK]) for n in ("xc2", "sq2", "r2", "xn2"))
    xc3, sq3, r3 = (sb(n, [P, TOK]) for n in ("xc3", "sq3", "r3"))
    xn3 = sb("xn3", [P, TOK])
    h2 = sb("h2", [P, 2, TOK])
    delta, mag, pos, decay, om, drive, states, y = (sb(n, [P, 2 * TOK]) for n in ("delta", "mag", "pos", "decay", "om", "drive", "states", "y"))
    def bank(name):
        return ctx.enter_context(nc.psum_tensor(name, [P, CH], F32))
    b_x, b_b, b_c, b_d, b_l2, b_l3, b_g, b_t = (bank("s_" + n) for n in ("x", "b", "c", "d", "l2", "l3", "g", "t"))

    with ExitStack() as wctx:
        zeroed, loaded, masks = (wctx.enter_context(nc.semaphore(n)) for n in ("w2_zeroed", "w2_loaded", "w2_masks"))
        with nc.Block() as block:
            @block.sync
            def _(sp):
                sp.wait_ge(zeroed, 2)
                n = 0
                def ld(dst, src):
                    nonlocal n
                    sp.dma_start(dst, src).then_inc(loaded, 16)
                    n += 16
                for b in range(2):
                    s = slice(C * b, C * b + C)
                    ld(w_p[s, b, 0, :], A["L0_attn_Wx"])
                    ld(w_p[s, b, 1:3, :], A["L0_attn_Wbc"].rearrange("c (k n) -> c k n", k=2))
                    ld(w_p[s, b, 3, :], A["L0_attn_Wd"])
                    ld(b_p[s, 4:5], A["L0_attn_by"].rearrange("(c o) -> c o", o=1))
                    ld(w1[s, b, 0:NODES], A["w1T"])
                ld(w_y[:, :], A["L0_attn_Wy"])
                ld(b_p[:, 0:1], A["L0_attn_bx"].rearrange("(c o) -> c o", o=1))
                for i in range(2):
                    ld(b_p[:, 1 + i:2 + i], A["L0_attn_bbc"][N_ST * i:N_ST * i + N_ST].rearrange("(c o) -> c o", o=1))
                ld(b_p[:, 3:4], A["L0_attn_bd"].rearrange("(c o) -> c o", o=1))
                ld(b1[:, 0:NODES], A["b1r"].broadcast_to([P, NODES]))
                sp.wait_ge(loaded, n)

            @block.vector
            def _(v):
                nc.vector.memset(w_p[:, :, :, :], 0.0).then_inc(zeroed, 1)
                nc.vector.memset(w1[:, :, :], 0.0).then_inc(zeroed, 1)
                nc.vector.memset(b1[:, NODES:256], 0.0)
                nc.vector.memset(eps[:, :], EPS)

            @block.gpsimd
            def _(pool):
                g = nc.gpsimd
                k = [0]
                def step(ins):
                    ins.then_inc(masks, 1)
                    k[0] += 1
                    pool.wait_ge(masks, k[0])
                step(g.memset(avg[:, :], 1.0 / C))
                for m in range(2):
                    v = avg[:, C * m:C * m + C]
                    step(g.affine_select(out=v, in_=v, compare_op=ALU.is_ge, fill=0.0, base=-C * m, pattern=[[0, C]], channel_multiplier=1))
                    step(g.affine_select(out=v, in_=v, compare_op=ALU.is_ge, fill=0.0, base=C * m + C - 1, pattern=[[0, C]], channel_multiplier=-1))
                step(g.memset(ident[:, :], 0.0))
                step(g.affine_select(out=ident[:, :], in_=ident[:, :], compare_op=ALU.not_equal, fill=1.0, base=0, pattern=[[-1, P]], channel_multiplier=1))

    N = "mean2 centred2 squared2 var2 ln2 rstd2 norm2 projected delta magnitude exp_mag log_mag softplus decay one_minus gated driven scanned gated_y y_out h2_ready " \
        "mean3 centred3 squared3 var3 ln3 rstd3 norm3 x_rows h_rows x_kept h_kept logits01 logits23 kept01 kept23"
    z = {n: sem("f_" + n) for n in N.split()}
    block = ctx.enter_context(nc.Block())
    STEADY = (TILES - 2) // 2

    def zero(t):
        return isinstance(t, int) and t == 0

    def sweep(eng, step):
        step(0, -1, ("A",))
        step(0, 0, ("A", "B"))
        step(0, 1, ("A", "B", "C"))
        step(0, 2, ("A", "B", "C"))
        with eng.Fori(1, STEADY) as k:
            step(k, 1, ("A", "B", "C"))
            step(k, 2, ("A", "B", "C"))
        step(STEADY, 1, ("B", "C"))
        step(STEADY, 2, ("C",))

    @block.tensor
    def _(pe):
        mm = nc.tensor.matmul

        def step(k, o, S):
            i = 2 * k + o
            p = o % 2
            if "A" in S:
                t = i + 1
                if not zero(t):
                    pe.wait_ge(z["rstd2"], t)
                mm(b_l2[:, 0:TOK], avg[:, :], h1[:, bass.ts(t, TOK)], start=True, stop=True).then_inc(z["mean2"], 1)
            if "C" in S:
                t = i - 1
                pe.wait_ge(z["h2_ready"], t + 1)
                if not zero(t):
                    pe.wait_ge(z["kept23"], t)
                mm(b_l3[:, 0:TOK], avg[:, :], h2[:, 1 - p, :], start=True, stop=True).then_inc(z["mean3"], 1)
                if not zero(t):
                    pe.wait_ge(z["x_kept"], t)
                for f in range(2):
                    j = nc.tensor.transpose(b_t[:, P * f:P * f + P], h2[:, 1 - p, P * f:P * f + P], ident[:, :])
                j.then_inc(z["h_rows"], 1)
            if "A" in S:
                t = i + 1
                pe.wait_ge(z["squared2"], t + 1)
                mm(b_l2[:, 0:TOK], avg[:, :], sq2[:, :], start=True, stop=True).then_inc(z["var2"], 1)
            if "C" in S:
                t = i - 1
                pe.wait_ge(z["squared3"], t + 1)
                mm(b_l3[:, 0:TOK], avg[:, :], sq3[:, :], start=True, stop=True).then_inc(z["var3"], 1)
            if "B" in S:
                t = i
                pe.wait_ge(z["gated_y"], t + 1)
                if "C" in S:
                    pe.wait_ge(z["h_kept"], t)
                for b in range(2):
                    j = mm(b_t[C * b:C * b + C, TOK:2 * TOK], w_y[:, :], y[:, TOK * b:TOK * b + TOK], start=True, stop=True)
                j.then_inc(z["y_out"], 1)
            if "A" in S:
                t = i + 1
                pe.wait_ge(z["norm2"], t + 1)
                for kind, bk in ((3, b_d), (1, b_b), (0, b_x), (2, b_c)):
                    for b in range(2):
                        j = mm(bk[:, TOK * b:TOK * b + TOK], w_p[:, b, kind, :], xn2[:, :], start=True, stop=True)
                    if kind == 3:
                        pass
                j.then_inc(z["projected"], 1)
            if "C" in S:
                t = i - 1
                pe.wait_ge(z["norm3"], t + 1)
                pe.wait_ge(z["h2_ready"], t + (2 if "B" in S else 1))
                pe.wait_ge(z["h_kept"], t + 1)
                for f in range(2):
                    j = nc.tensor.transpose(b_t[:, P * f:P * f + P], xn3[:, P * f:P * f + P], ident[:, :])
                j.then_inc(z["x_rows"], 1)
                if not zero(t):
                    pe.wait_ge(z["kept01"], t)
                for f in range(2):
                    j = mm(b_g[:, 256 * f:256 * f + 256], xn3[:, P * f:P * f + P], w1[:, 0, :], start=True, stop=True)
                j.then_inc(z["logits01"], 1)
                for f in range(2):
                    j = mm(b_l3[:, 256 * f:256 * f + 256], xn3[:, P * f:P * f + P], w1[:, 1, :], start=True, stop=True)
                j.then_inc(z["logits23"], 1)

        sweep(pe, step)

    @block.scalar
    def _(act):
        a = nc.scalar
        act.preload_act_table_set("natural_log_exp_and_others")

        def step(k, o, S):
            i = 2 * k + o
            keep = "C" in S and not zero(i - 1)
            if keep:
                act.wait_ge(z["x_rows"], i - 1)
            if "B" in S:
                t = i
                act.wait_ge(z["projected"], t + 1)
                a.activation(delta[:, :], b_d[:, :], ACT.Identity, bias=b_p[:, 3:4]).then_inc(z["delta"], 1)
                if keep:
                    keep_x(i - 2)
                act.wait_ge(z["delta"], t + 1)
                a.activation(mag[:, :], delta[:, :], ACT.Abs).then_inc(z["magnitude"], 1)
                act.wait_ge(z["magnitude"], t + 1)
                a.activation(mag[:, :], mag[:, :], ACT.Exp, scale=-1.0).then_inc(z["exp_mag"], 1)
                act.wait_ge(z["exp_mag"], t + 1)
                a.activation(mag[:, :], mag[:, :], ACT.Ln, bias=1.0).then_inc(z["log_mag"], 1)
            elif keep:
                keep_x(i - 2)
            if "A" in S:
                t = i + 1
                act.wait_ge(z["centred2"], t + 1)
                a.activation(sq2[:, :], xc2[:, :], ACT.Square).then_inc(z["squared2"], 1)
            if "C" in S:
                t = i - 1
                act.wait_ge(z["centred3"], t + 1)
                act.wait_ge(z["h_rows"], t + 1)
                a.activation(sq3[:, :], xc3[:, :], ACT.Square).then_inc(z["squared3"], 1)
                a.activation(pay[:, bass.ts(t, 4), 76:140].rearrange("p (b f) c -> p f b c", b=2),
                             b_t[:, 0:TOK].rearrange("p (f b c) -> p f b c", f=2, b=2), ACT.Copy).then_inc(z["h_kept"], 1)
            if "B" in S:
                t = i
                act.wait_ge(z["softplus"], t + 1)
                a.activation(decay[:, :], pos[:, :], ACT.Exp, scale=-1.0).then_inc(z["decay"], 1)
            if "A" in S:
                t = i + 1
                act.wait_ge(z["var2"], t + 1)
                a.activation(r2[:, :], b_l2[:, 0:TOK], ACT.Ln, bias=eps[:, :]).then_inc(z["ln2"], 1)
                act.wait_ge(z["ln2"], t + 1)
                a.activation(r2[:, :], r2[:, :], ACT.Exp, scale=-0.5).then_inc(z["rstd2"], 1)
            if "C" in S:
                t = i - 1
                act.wait_ge(z["var3"], t + 1)
                a.activation(r3[:, :], b_l3[:, 0:TOK], ACT.Ln, bias=eps[:, :]).then_inc(z["ln3"], 1)
                act.wait_ge(z["ln3"], t + 1)
                a.activation(r3[:, :], r3[:, :], ACT.Exp, scale=-0.5).then_inc(z["rstd3"], 1)

        def keep_x(t):
            a.activation(pay[:, bass.ts(t, 4), 0:C].rearrange("p (b f) c -> p f b c", b=2),
                         b_t[:, 0:TOK].rearrange("p (f b c) -> p f b c", f=2, b=2), ACT.Copy).then_inc(z["x_kept"], 1)

        step(0, -1, ("A",))
        step(0, 0, ("A", "B"))
        step(0, 1, ("A", "B", "C"))
        step(0, 2, ("A", "B", "C"))
        with act.Fori(1, STEADY) as k:
            step(k, 1, ("A", "B", "C"))
            step(k, 2, ("A", "B", "C"))
        step(STEADY, 1, ("B", "C"))
        step(STEADY, 2, ("C",))
        act.wait_ge(z["x_rows"], TILES)
        keep_x(TILES - 1)

    @block.vector
    def _(v):
        d = nc.vector

        def step(k, o, S):
            i = 2 * k + o
            p = o % 2
            if "A" in S:
                t = i + 1
                v.wait_ge(z["mean2"], t + 1)
                d.tensor_tensor(xc2[:, :], h1[:, bass.ts(t, TOK)], b_l2[:, 0:TOK], ALU.subtract).then_inc(z["centred2"], 1)
            if "B" in S:
                t = i
                v.wait_ge(z["log_mag"], t + 1)
                d.scalar_tensor_tensor(pos[:, :], delta[:, :], 0.0, mag[:, :], ALU.max, ALU.add).then_inc(z["softplus"], 1)
            if "C" in S:
                t = i - 1
                v.wait_ge(z["mean3"], t + 1)
                d.tensor_tensor(xc3[:, :], h2[:, 1 - p, :], b_l3[:, 0:TOK], ALU.subtract).then_inc(z["centred3"], 1)
            if "B" in S:
                t = i
                v.wait_ge(z["decay"], t + 1)
                d.tensor_scalar(om[:, :], decay[:, :], -1.0, 1.0, ALU.mult, ALU.add).then_inc(z["one_minus"], 1)
                v.wait_ge(z["one_minus"], t + 1)
                d.scalar_tensor_tensor(om[:, :], b_b[:, :], b_p[:, 1:2], om[:, :], ALU.add, ALU.mult).then_inc(z["gated"], 1)
                v.wait_ge(z["gated"], t + 1)
                d.scalar_tensor_tensor(drive[:, :], b_x[:, :], b_p[:, 0:1], om[:, :], ALU.add, ALU.mult).then_inc(z["driven"], 1)
                v.wait_ge(z["driven"], t + 1)
                for b in range(2):
                    s = slice(TOK * b, TOK * b + TOK)
                    d.tensor_tensor_scan(states[:, s], decay[:, s], drive[:, s], 0.0, ALU.mult, ALU.add).then_inc(z["scanned"], 1)
                v.wait_ge(z["scanned"], 2 * t + 2)
                d.scalar_tensor_tensor(y[:, :], b_c[:, :], b_p[:, 2:3], states[:, :], ALU.add, ALU.mult).then_inc(z["gated_y"], 1)
            if "A" in S:
                t = i + 1
                v.wait_ge(z["rstd2"], t + 1)
                d.tensor_tensor(xn2[:, :], xc2[:, :], r2[:, :], ALU.mult).then_inc(z["norm2"], 1)
            if "B" in S:
                t = i
                v.wait_ge(z["y_out"], t + 1)
                d.scalar_tensor_tensor(h2[:, p, :], b_t[:, TOK:2 * TOK], b_p[:, 4:5], h1[:, bass.ts(t, TOK)], ALU.add, ALU.add).then_inc(z["h2_ready"], 1)
            if "C" in S:
                t = i - 1
                v.wait_ge(z["rstd3"], t + 1)
                d.tensor_tensor(xn3[:, :], xc3[:, :], r3[:, :], ALU.mult).then_inc(z["norm3"], 1)
                for f, (bk, n) in enumerate(((b_g, "01"), (b_l3, "23"))):
                    v.wait_ge(z["logits" + n], t + 1)
                    d.tensor_tensor(lg[:, bass.ds(4 * t + 2 * f, 2), :], bk[:, :].rearrange("p (f n) -> p f n", f=2),
                                    b1[:, :].rearrange("p (o n) -> p o n", o=1).broadcast_to([P, 2, 256]), ALU.add).then_inc(z["kept" + n], 1)

        sweep(v, step)


I32 = mybir.dt.int32
U32 = mybir.dt.uint32
BF16 = mybir.dt.bfloat16
GRP = 32
BLK = 128
TOKENS = B * TOK
NBLK = (TOKENS + GRP * (BLK - 1)) // BLK
NBLK += -NBLK % 8
X0, P0, H0, ID0 = 0, 64, 76, 140
KT = 7


def paths(nc, ctx, pay, lg, grp):
    def sb(name, shape, dt=F32):
        return ctx.enter_context(nc.sbuf_tensor(name, shape, dt))
    bits = sb("bits", [P, LEVELS - 1, NT])
    pw = sb("pw", [P, NT, LEVELS])
    n5, n6, pl, pr = (sb(n, [P, NT]) for n in ("not5", "not6", "p7_left", "p7_right"))
    chosen, magn, weight, steps, outs = (ctx.enter_context(nc.semaphore("t_" + n)) for n in ("chosen", "magn", "weight", "steps", "outs"))
    with nc.Block() as block:
        @block.vector
        def _(v):
            d = nc.vector
            n = [0]
            for l in range(LEVELS - 1):
                s = 2 ** (LEVELS - 1 - l) - 1
                d.tensor_scalar(bits[:, l, :], lg[:, :, l], 0.0, None, ALU.is_gt).then_inc(chosen, 1)
                v.wait_ge(chosen, 2 * l + 1)
                d.copy_predicated(lg[:, :, l + 1:l + 1 + s], bits[:, l, :].rearrange("p (n o) -> p n o", o=1).broadcast_to([P, NT, s]).bitcast(U32),
                                  lg[:, :, l + 1 + s:l + 1 + 2 * s]).then_inc(chosen, 1)
                v.wait_ge(chosen, 2 * l + 2)

            def step(ins):
                ins.then_inc(steps, 1)
                n[0] += 1
                v.wait_ge(steps, n[0])
            step(d.scalar_tensor_tensor(grp[:, :], bits[:, 0, :], 2.0, bits[:, 1, :], ALU.mult, ALU.add))
            for l in range(2, 5):
                step(d.scalar_tensor_tensor(grp[:, :], grp[:, :], 2.0, bits[:, l, :], ALU.mult, ALU.add))
            step(d.tensor_scalar(n5[:, :], bits[:, 5, :], -1.0, 1.0, ALU.mult, ALU.add))
            step(d.tensor_scalar(n6[:, :], bits[:, 6, :], -1.0, 1.0, ALU.mult, ALU.add))
            v.wait_ge(weight, 1)
            step(d.tensor_tensor(pl[:, :], pw[:, :, 7], n5[:, :], ALU.mult))
            step(d.tensor_tensor(pr[:, :], pw[:, :, 7], bits[:, 5, :], ALU.mult))
            step(d.tensor_copy(pay[:, :, P0:P0 + 6], pw[:, :, 0:6]))
            for u, (a, b) in enumerate(((pw[:, :, 6], n5[:, :]), (pw[:, :, 6], bits[:, 5, :]), (pl[:, :], n6[:, :]), (pl[:, :], bits[:, 6, :]),
                                        (pr[:, :], n6[:, :]), (pr[:, :], bits[:, 6, :]))):
                step(d.tensor_tensor(pay[:, :, P0 + 6 + u], a, b, ALU.mult))

        @block.scalar
        def _(act):
            a = nc.scalar
            act.wait_ge(chosen, 2 * LEVELS - 2)
            a.activation(pw[:, :, :], lg[:, :, 0:LEVELS], ACT.Abs).then_inc(magn, 1)
            act.wait_ge(magn, 1)
            a.activation(pw[:, :, :], pw[:, :, :], ACT.Gelu).then_inc(weight, 1)

        @block.gpsimd
        def _(pool):
            nc.gpsimd.iota(pay[:, :, ID0:ID0 + 1].bitcast(I32), pattern=[[P, NT], [0, 1]], base=0, channel_multiplier=1)
            nc.gpsimd.memset(pay[:, :, ID0 + 1:ROW], 0.0)


def sort_and_mix(nc, ctx, A, pay, grp, rows_d, out_d):
    def sb(name, shape, dt=F32):
        return ctx.enter_context(nc.sbuf_tensor(name, shape, dt))

    def sem(name):
        return ctx.enter_context(nc.semaphore(name))

    wt = sb("wt", [P, GRP, KT, C])
    gid = sb("gid", [1, P], I32)
    ident = sb("ident3", [P, P])
    table = sem("m_table")
    gid_ready, scattered = sem("gid_ready"), sem("scattered")

    with ExitStack() as c2:
        sb2 = lambda n, s, dt=F32: c2.enter_context(nc.sbuf_tensor(n, s, dt))
        pb2 = lambda n: c2.enter_context(nc.psum_tensor(n, [P, 512], F32))
        s2 = lambda n: c2.enter_context(nc.semaphore("o_" + n))
        oh = sb2("oh", [P, NT, GRP]); ohb = sb2("ohb", [P, NT, GRP], BF16)
        iog = sb2("iog", [P, GRP]); iop = sb2("iop", [P, 1])
        tri = sb2("tri", [P, P], BF16); one = sb2("one", [P, P], BF16)
        tot = sb2("tot", [P, GRP, NT]); inc = sb2("inc", [P, GRP, NT]); keep = sb2("keep", [P, GRP, NT])
        rank = sb2("rank", [P, NT, GRP])
        cnt, nbl, bend, base = (sb2(n, [P, GRP]) for n in ("cnt", "nbl", "bend", "base"))
        nbi = sb2("nbi", [P, GRP], I32)
        dst = sb2("dst", [P, NT]); dsti = sb2("dsti", [P, NT], I32)
        cmp = sb2("cmp", [P, GRP]); gcol = sb2("gcol", [P, 1])
        fill = sb2("fill", [P, ROW])
        pre_b = [pb2(f"pre_b{i}") for i in range(4)]; tot_b = [pb2(f"tot_b{i}") for i in range(4)]
        consts, hot, counted, steps, zeroed, filled, dest_ready, gcol_ready, gid_row = (s2(n) for n in
            "consts hot counted steps zeroed filled dest_ready gcol_ready gid_row".split())
        with nc.Block() as block:
            @block.gpsimd
            def _(pool):
                g = nc.gpsimd
                k = [0]
                def step(ins):
                    ins.then_inc(consts, 1)
                    k[0] += 1
                    pool.wait_ge(consts, k[0])
                step(g.memset(fill[:, :], 0.0))
                step(g.iota(fill[:, ID0:ID0 + 1].bitcast(I32), pattern=[[0, 1]], base=TOKENS, channel_multiplier=0))
                step(g.iota(iog[:, :], pattern=[[1, GRP]], base=0, channel_multiplier=0, allow_small_or_imprecise_dtypes=True))
                step(g.memset(tri[:, :], 1.0))
                step(g.affine_select(out=tri[:, :], in_=tri[:, :], compare_op=ALU.is_ge, fill=0.0, base=-1, pattern=[[1, P]], channel_multiplier=-1))
                step(g.memset(one[:, :], 1.0))
                step(g.memset(keep[:, :, :], 1.0))
                step(g.memset(keep[:, :, 0:1], 0.0))
                step(g.iota(iop[:, :], pattern=[[0, 1]], base=0, channel_multiplier=1, allow_small_or_imprecise_dtypes=True))
                step(g.memset(ident[:, :], 0.0))
                step(g.affine_select(out=ident[:, :], in_=ident[:, :], compare_op=ALU.not_equal, fill=1.0, base=0, pattern=[[-1, P]], channel_multiplier=1))
                step(g.memset(wt[:, :, 6, :], 0.0))
                v = wt[:, :, 6, :]
                pool.wait_ge(consts, k[0])
                g.affine_select(out=v, in_=v, compare_op=ALU.not_equal, fill=1.0, base=-(H0 - 16), pattern=[[0, GRP], [-1, C]], channel_multiplier=1).then_inc(zeroed, 1)
                pool.wait_ge(filled, 16)
                pool.wait_ge(dest_ready, 1)
                for t in range(NT):
                    g.indirect_dma_start(rows_d, bass.IndirectOffsetOnAxis(ap=dsti[:, t:t + 1], axis=0), pay[:, t, :], None).then_inc(scattered, 16)

            @block.sync
            def _(sp):
                n = 0
                def ld(dst, src):
                    nonlocal n
                    sp.dma_start(dst, src).then_inc(table, 16)
                    n += 16
                sp.wait_ge(consts, 2)
                sp.dma_start(rows_d.rearrange("(n p) c -> p n c", p=P), fill[:, :].rearrange("p (o c) -> p o c", o=1).broadcast_to([P, NBLK, ROW])).then_inc(filled, 16)
                w2 = A["w2T"]
                for l in range(6):
                    k, half = l // 2, l % 2
                    n0, cn = 2 ** l - 1, 2 ** l
                    for v in range(cn):
                        r = GRP // cn
                        if l < 5:
                            ld(wt[C * half:C * half + C, v * r:(v + 1) * r, k, :], w2[:, n0 + v:n0 + v + 1, :].broadcast_to([C, r, C]))
                    if l == 5:
                        ld(wt[C * half:C * half + C, :, k, :], w2[:, n0:n0 + cn, :])
                for half in range(2):
                    ld(wt[C * half:C * half + C, :, 3, :], w2[:, 63:127, :].rearrange("d (g u) o -> d g u o", u=2)[:, :, half, :])
                    for m in range(2):
                        ld(wt[C * half:C * half + C, :, 4 + m, :], w2[:, 127:255, :].rearrange("d (g u) o -> d g u o", u=4)[:, :, 2 * m + half, :])
                sp.wait_ge(zeroed, 1)
                b2 = A["L0_ffn_b2s"]
                for l in range(6):
                    n0, cn = 2 ** l - 1, 2 ** l
                    r = GRP // cn
                    q = P0 - 16 + l
                    ld(wt[q:q + 1, :, 6, :].rearrange("q (v r) o -> q v r o", r=r),
                       b2[n0:n0 + cn, :].rearrange("(q v r) o -> q v r o", q=1, r=1).broadcast_to([1, cn, r, C]))
                for u in range(2):
                    q = P0 - 16 + 6 + u
                    ld(wt[q:q + 1, :, 6, :], b2[63:127, :].rearrange("(q g u) o -> q g u o", q=1, u=2)[:, :, u, :])
                for u in range(4):
                    q = P0 - 16 + 8 + u
                    ld(wt[q:q + 1, :, 6, :], b2[127:255, :].rearrange("(q g u) o -> q g u o", q=1, u=4)[:, :, u, :])
                sp.wait_ge(table, n)
                sp.wait_ge(scattered, 16 * NT)

            @block.tensor
            def _(pe):
                pe.wait_ge(hot, 2)
                pe.wait_ge(consts, 6)
                for i in range(4):
                    s = ohb[:, 16 * i:16 * i + 16, :].rearrange("p a b -> p (a b)")
                    nc.tensor.matmul(tot_b[i][:, :], one[:, :], s, start=True, stop=True)
                    j = nc.tensor.matmul(pre_b[i][:, :], tri[:, :], s, start=True, stop=True)
                j.then_inc(counted, 1)
                pe.wait_ge(gcol_ready, 1)
                pe.wait_ge(consts, 11)
                nc.tensor.matmul(tot_b[0][0:1, 0:P], gcol[:, :], ident[:, :], start=True, stop=True).then_inc(gid_row, 1)

            @block.vector
            def _(v):
                d = nc.vector
                n = [0]
                def step(ins):
                    ins.then_inc(steps, 1)
                    n[0] += 1
                    v.wait_ge(steps, n[0])
                def col(a):
                    return a.rearrange("p (g o) -> p g o", o=1)
                v.wait_ge(consts, 3)
                d.tensor_tensor(oh[:, :, :], grp[:, :].rearrange("p (n o) -> p n o", o=1).broadcast_to([P, NT, GRP]),
                                iog[:, :].rearrange("p (o g) -> p o g", o=1).broadcast_to([P, NT, GRP]), ALU.is_equal).then_inc(hot, 1)
                v.wait_ge(hot, 1)
                d.tensor_copy(ohb[:, :, :], oh[:, :, :]).then_inc(hot, 1)
                v.wait_ge(counted, 1)
                for i in range(4):
                    step(d.tensor_copy(tot[:, :, 16 * i:16 * i + 16].rearrange("p g n -> p n g"), tot_b[i][:, :].rearrange("p (n g) -> p n g", g=GRP)))
                v.wait_ge(consts, 9)
                f = lambda a: a[:, :, :].rearrange("p g n -> p (g n)")
                step(d.tensor_tensor_scan(f(inc), f(keep), f(tot), 0.0, ALU.mult, ALU.add))
                step(d.tensor_scalar(nbi[:, :], inc[:, :, NT - 1], float(BLK - 1), None, ALU.add))
                step(d.tensor_scalar(nbi[:, :], nbi[:, :], BLK.bit_length() - 1, None, ALU.logical_shift_right))
                step(d.tensor_copy(nbl[:, :], nbi[:, :]))
                step(d.memset(cnt[:, :], 1.0))
                step(d.tensor_tensor_scan(bend[:, :], cnt[:, :], nbl[:, :], 0.0, ALU.mult, ALU.add))
                step(d.tensor_tensor(base[:, :], bend[:, :], nbl[:, :], ALU.subtract))
                step(d.tensor_scalar(base[:, :], base[:, :], float(BLK), None, ALU.mult))
                step(d.tensor_tensor(inc[:, :, :], inc[:, :, :], tot[:, :, :], ALU.subtract))
                step(d.tensor_tensor(inc[:, :, :], inc[:, :, :], col(base[:, :]).broadcast_to([P, GRP, NT]), ALU.add))
                for i in range(4):
                    step(d.tensor_tensor(rank[:, 16 * i:16 * i + 16, :], pre_b[i][:, :].rearrange("p (n g) -> p n g", g=GRP),
                                         inc[:, :, 16 * i:16 * i + 16].rearrange("p g n -> p n g"), ALU.add))
                step(d.tensor_tensor(rank[:, :, :], rank[:, :, :], oh[:, :, :], ALU.mult))
                step(d.tensor_reduce(dst[:, :], rank[:, :, :], AX.X, ALU.add))
                d.tensor_copy(dsti[:, :], dst[:, :]).then_inc(dest_ready, 1)
                step(d.tensor_scalar(cmp[:, :], bend[:, :], iop[:, :], None, ALU.is_le))
                step(d.tensor_reduce(gcol[:, :], cmp[:, :], AX.X, ALU.add))
                d.tensor_scalar(gcol[:, :], gcol[:, :], float(GRP - 1), None, ALU.min).then_inc(gcol_ready, 1)
                v.wait_ge(gid_row, 1)
                d.tensor_copy(gid[:, :], tot_b[0][0:1, 0:P]).then_inc(gid_ready, 1)

    ROWS, RING, LOOKAHEAD = 8, 4, 6
    PAIRS, TURN = NBLK // 2, ROWS // 2
    TURNS, PEELED = NBLK // ROWS, 2
    rows = sb("rows", [P, ROWS, ROW])
    ids = sb("ids", [P, 2 * ROWS], I32)
    xs = sb("xs", [P, RING, UNITS, C])
    xsT = sb("xsT", [P, RING, KT, P])
    w_cur = sb("w_cur", [P, RING, KT, C])
    oT = sb("oT", [P, 2, P])
    orow = sb("orow", [P, ROWS, C])
    turned = [[ctx.enter_context(nc.psum_tensor(f"turned{i}{n}", [P, 512], F32)) for n in "ab"] for i in range(2)]
    ob = [ctx.enter_context(nc.psum_tensor(f"mixed_bank{i}", [P, 512], F32)) for i in range(2)]
    rb = [ctx.enter_context(nc.psum_tensor(f"back_bank{i}", [P, 512], F32)) for i in range(2)]
    scaled, turned_a, turned_b, kept_a, kept_b, w_kept, mixed, mixed_kept, back, back_kept, ids_kept = (sem("m_" + n) for n in
        "scaled turned_a turned_b kept_a kept_b w_kept mixed mixed_kept back back_kept ids_kept".split())
    rows_in = [sem(f"m_rows_in{i}") for i in range(ROWS)]
    written = [sem(f"m_written{i}") for i in range(ROWS)]
    rows_v = rows_d.rearrange("(n p) c -> n p c", p=P)
    block = ctx.enter_context(nc.Block())

    def due(n):
        return not isinstance(n, int) or n > 0

    def there(m):
        return not isinstance(m, int) or 0 <= m < PAIRS

    def steps_of(eng, step, skew):
        for m in range(PEELED * TURN):
            step(m // TURN, m % TURN)
        with eng.Fori(PEELED, TURNS) as k:
            for j in range(TURN):
                step(k, j)
        for m in range(PAIRS, PAIRS + skew):
            step(m // TURN, m % TURN)

    @block.sync
    def _(sp):
        def load(k, i):
            b = ROWS * k + i
            if due(b - ROWS + 1):
                sp.wait_ge(scaled, b - ROWS + 1)
                sp.wait_ge(turned_b, b - ROWS + 1)
                sp.wait_ge(ids_kept, b - ROWS + 1)
            src = rows_v[b, :, :] if isinstance(b, int) else rows_v[bass.ds(b, 1), :, :].rearrange("o p c -> (o p) c")
            sp.dma_start(rows[:, i, :], src).then_inc(rows_in[i], 16)
        for i in range(ROWS):
            load(0, i)
        with sp.Fori(1, TURNS) as k:
            for i in range(ROWS):
                load(k, i)

    @block.vector
    def _(v):
        d = nc.vector

        def step(k, j):
            m = TURN * k + j
            for h in range(2):
                if there(m):
                    b, i = 2 * m + h, 2 * j + h
                    v.wait_ge(rows_in[i], 16 * (k + 1))
                    if due(b - RING + 1):
                        v.wait_ge(turned_a, b - RING + 1)
                        v.wait_ge(turned_b, b - RING + 1)
                    d.tensor_tensor(xs[:, i % RING, :, :], rows[:, i, X0:X0 + C].rearrange("p (o c) -> p o c", o=1).broadcast_to([P, UNITS, C]),
                                    rows[:, i, P0:P0 + UNITS].rearrange("p (u o) -> p u o", o=1).broadcast_to([P, UNITS, C]), ALU.mult).then_inc(scaled, 1)
                if there(m - 1):
                    b, i = 2 * m - 2 + h, (2 * j - 2 + h) % ROWS
                    v.wait_ge(turned_b, b + 1)
                    if due(m - 2):
                        v.wait_ge(mixed, m - 2)
                    d.tensor_copy(xsT[:, i % RING, 4:KT, :], turned[h][1][:, 0:3 * P].rearrange("p (u n) -> p u n", u=3)).then_inc(kept_b, 1)
            if there(m - 2):
                v.wait_ge(mixed, m - 1)
                if due(m - 3):
                    v.wait_ge(back, m - 3)
                d.tensor_copy(oT[:, j % 2, :], ob[j % 2][:, 0:P]).then_inc(mixed_kept, 1)
        steps_of(v, step, 2)

    @block.scalar
    def _(act):
        a = nc.scalar

        def step(k, j):
            m = TURN * k + j
            for h in range(2):
                if there(m):
                    b, i = 2 * m + h, 2 * j + h
                    g = act.value_load(gid[0:1, b:b + 1] if isinstance(b, int) else gid[0:1, bass.ds(b, 1)], min_val=0, max_val=GRP - 1)
                    if due(m - 1):
                        act.wait_ge(mixed, m - 1)
                    a.activation(w_cur[:, i % RING, :, :], wt[:, bass.ds(g, 1), :, :].rearrange("p o k c -> p (o k) c"), ACT.Copy).then_inc(w_kept, 1)
                    act.wait_ge(turned_a, b + 1)
                    a.activation(xsT[:, i % RING, 0:4, :], turned[h][0][:, :].rearrange("p (u n) -> p u n", u=4), ACT.Copy).then_inc(kept_a, 1)
            if there(m - 2):
                i = (2 * j - 4) % ROWS
                act.wait_ge(back, m - 1)
                q = k if j >= 2 else k - 1
                if due(q):
                    act.wait_ge(written[i], 16 * q)
                    act.wait_ge(written[i + 1], 16 * q)
                a.activation(orow[:, i:i + 2, :], rb[j % 2][:, 0:P].rearrange("p (b c) -> p b c", b=2), ACT.Copy).then_inc(back_kept, 1)
        steps_of(act, step, 2)

    @block.tensor
    def _(pe):
        mm = nc.tensor.matmul

        def step(k, j):
            m = TURN * k + j
            for h in range(2):
                if there(m):
                    b, i = 2 * m + h, 2 * j + h
                    pe.wait_ge(scaled, b + 1)
                    if due(b - 1):
                        pe.wait_ge(kept_a, b - 1)
                    for u in range(4):
                        t = nc.tensor.transpose(turned[h][0][:, P * u:P * u + P], xs[:, i % RING, 2 * u:2 * u + 2, :].rearrange("p a c -> p (a c)"), ident[:, :])
                    t.then_inc(turned_a, 1)
                    if due(b - 1):
                        pe.wait_ge(kept_b, b - 1)
                    for u in range(2):
                        nc.tensor.transpose(turned[h][1][:, P * u:P * u + P], xs[:, i % RING, 8 + 2 * u:10 + 2 * u, :].rearrange("p a c -> p (a c)"), ident[:, :])
                    pe.wait_ge(rows_in[i], 16 * (k + 1))
                    nc.tensor.transpose(turned[h][1][:, 2 * P:3 * P], rows[:, i, 16:ROW], ident[:, :]).then_inc(turned_b, 1)
            if there(m - 1):
                i = (2 * j - 2) % RING
                pe.wait_ge(kept_a, 2 * m)
                pe.wait_ge(kept_b, 2 * m)
                pe.wait_ge(w_kept, 2 * m)
                if due(m - 2):
                    pe.wait_ge(mixed_kept, m - 2)
                for u in range(KT):
                    for h in range(2):
                        t = mm(ob[(j + 1) % 2][C * h:C * h + C, 0:P], w_cur[:, i + h, u, :], xsT[:, i + h, u, :], start=u == 0, stop=u == KT - 1)
                t.then_inc(mixed, 1)
            if there(m - 2):
                pe.wait_ge(mixed_kept, m - 1)
                if due(m - 3):
                    pe.wait_ge(back_kept, m - 3)
                nc.tensor.transpose(rb[j % 2][:, 0:P], oT[:, j % 2, :], ident[:, :]).then_inc(back, 1)
        steps_of(pe, step, 2)

    @block.gpsimd
    def _(pool):
        def take_ids(b):
            pool.wait_ge(rows_in[b % ROWS], 16 * (b // ROWS + 1))
            if b >= 2 * ROWS:
                pool.wait_ge(written[b % ROWS], 16 * (b // ROWS - 1))
            nc.gpsimd.tensor_copy(ids[:, b % (2 * ROWS):b % (2 * ROWS) + 1], rows[:, b % ROWS, ID0:ID0 + 1].bitcast(I32)).then_inc(ids_kept, 1)
        for b in range(LOOKAHEAD):
            take_ids(b)
        for b in range(NBLK):
            if b + LOOKAHEAD < NBLK:
                take_ids(b + LOOKAHEAD)
            pool.wait_ge(ids_kept, b + 1)
            pool.wait_ge(back_kept, b // 2 + 1)
            nc.gpsimd.indirect_dma_start(out_d, bass.IndirectOffsetOnAxis(ap=ids[:, b % (2 * ROWS):b % (2 * ROWS) + 1], axis=0), orow[:, b % ROWS, :], None,
                                         bounds_check=TOKENS - 1, oob_is_err=False).then_inc(written[b % ROWS], 16)
        for i in range(ROWS):
            pool.wait_ge(written[i], 16 * TURNS)


def program(nc, A, out):
    rows_d = nc.dram_tensor("rows_sorted", (NBLK * BLK, ROW), F32, kind="Internal").ap()
    with ExitStack() as top:
        h1 = top.enter_context(nc.sbuf_tensor("h1", [P, TILES * TOK], F32))
        with ExitStack() as ctx:
            tokenizer(nc, ctx, A, h1)
        pay = top.enter_context(nc.sbuf_tensor("pay", [P, NT, ROW], F32))
        grp = top.enter_context(nc.sbuf_tensor("grp", [P, NT], F32))
        with ExitStack() as logits:
            lg = logits.enter_context(nc.sbuf_tensor("lg", [P, NT, 256], F32))
            with ExitStack() as ctx:
                scan_and_logits(nc, ctx, A, h1, pay, lg)
            with ExitStack() as ctx:
                paths(nc, ctx, pay, lg, grp)
        with ExitStack() as ctx:
            sort_and_mix(nc, ctx, A, pay, grp, rows_d, out)


def preorder(node=0, level=0):
    if level == LEVELS - 1:
        return [node]
    return [node] + preorder(2 * node + 1, level + 1) + preorder(2 * node + 2, level + 1)


_INS = ["x"] + ["L0_tok_" + n for n in ("ln_q_w", "ln_q_b", "ln_kv_w", "ln_kv_b", "proj_b")] + \
       ["L0_attn_" + n for n in ("Wx", "bx", "Wbc", "bbc", "Wd", "bd", "Wy", "by")] + ["L0_ffn_b2s"]


def kernel(**inputs):
    import concourse.bacc as bacc
    from concourse.bass_utils import run_bass_kernel_spmd

    arrays = {n: np.ascontiguousarray(inputs[n]) for n in _INS}
    order = preorder()
    arrays["WqT"] = np.ascontiguousarray(np.asarray(inputs["L0_tok_Wq"]).T)
    arrays["WkvT"] = np.ascontiguousarray(np.asarray(inputs["L0_tok_Wkv"]).T)
    arrays["projT"] = np.ascontiguousarray(np.asarray(inputs["L0_tok_proj_w"]).T)
    arrays["w1T"] = np.ascontiguousarray(np.asarray(inputs["L0_ffn_w1s"])[order].T)
    arrays["b1r"] = np.ascontiguousarray(np.asarray(inputs["L0_ffn_b1s"])[order].reshape(1, NODES))
    arrays["w2T"] = np.ascontiguousarray(np.asarray(inputs["L0_ffn_w2s"]).transpose(1, 0, 2))

    nc = bacc.Bacc("TRN2", target_bir_lowering=False, num_devices=1)
    A = {n: nc.dram_tensor("in_" + n, a.shape, mybir.dt.from_np(a.dtype), kind="ExternalInput").ap() for n, a in arrays.items()}
    out = nc.dram_tensor("out", (TOKENS, C), F32, kind="ExternalOutput").ap()
    program(nc, A, out)
    r = run_bass_kernel_spmd(nc, [{"in_" + n: a for n, a in arrays.items()}], core_ids=[0])
    return r.results[0]["out"].reshape(B, TOK, C)
```

```python
import numpy as np
import concourse.bass as bass
from concourse import mybir
from contextlib import ExitStack

F32 = mybir.dt.float32
F32R = mybir.dt.float32r
ALU = mybir.AluOpType
ACT = mybir.ActivationFunctionType
AX = mybir.AxisListType

P = 128
B, C, HW = 32, 64, 64
S = 4
TH = HW // S
TOK = TH * TH
NP = S * S
HEADS = 8
HD = C // HEADS
PIX = HW * HW
TILES = B // 2
CH = 512
NCH = PIX // CH
ORDER = [0, 2, 4, 6, 1, 3, 5, 7]
EPS = 1e-5


def tokenizer(nc, ctx, A, h1):
    def sb(name, shape, dt=F32):
        return ctx.enter_context(nc.sbuf_tensor(name, shape, dt))

    def bank(name):
        return ctx.enter_context(nc.psum_tensor(name, [P, CH], F32))

    def sem(name):
        return ctx.enter_context(nc.semaphore(name))

    x_v = A["x"].rearrange("(t b) c h w -> t (b c) (h w)", b=2)

    x = sb("x_px", [P, 2, PIX])
    x_hi = sb("x_hi", [P, 2, PIX], F32R)
    x_lo = sb("x_lo", [P, 2, PIX], F32R)
    x_sq = sb("x_sq", [P, NCH // 2, CH])
    v_sb = sb("v_sb", [P, NCH, CH])
    qk = sb("qk", [P, NCH, CH])
    va = sb("va", [P, NCH, CH])
    pre1 = sb("pre1", [P, 1024])
    pre2 = sb("pre2", [P, TH, HW])
    rkv = sb("rkv", [P, CH])
    sc = sb("sc", [P, CH])
    ex = sb("ex", [P, CH])
    a_hi = sb("a_hi", [P, CH], F32R)
    a_lo = sb("a_lo", [P, CH], F32R)
    mx = sb("mx", [P, 2 * TH])
    sm = sb("sm", [P, 2 * TH])
    rc = sb("rc", [P, 2 * TH])
    px_sum = sb("px_sum", [P, TOK])
    q4 = sb("q4", [P, TH, HW])
    rs2 = sb("rs2", [P, 2 * TOK])
    rq = sb("rq", [P, TOK])
    qs = sb("qs", [P, TOK])
    w_ld = sb("w_ld", [P, 4, P])
    w_sc = sb("w_sc", [P, 3, P])
    w_hi = sb("w_hi", [P, 2, P], F32R)
    w_lo = sb("w_lo", [P, 2, P], F32R)
    gq = sb("gq", [P, P])
    vec = sb("vec", [P, 8])
    avg = sb("avg", [P, P])
    cen = sb("cen", [P, P])
    sel = sb("sel", [P, 2, 32])
    msel = sb("msel", [P, 2, 32])
    e_f = va[:, 0:2, :].rearrange("p a (b m) -> p (a b) m", m=P)
    e_r = sb("e_r", [P, NCH, P], F32R)
    eps = sb("eps", [P, 1])

    b_k = [bank(f"b_k{i}") for i in range(2)]
    b_w = [bank(f"b_w{i}") for i in range(2)]
    b_s, b_m, b_q, b_b = bank("b_s"), bank("b_m"), bank("b_q"), bank("b_b")

    with ExitStack() as wctx:
        wsem = lambda n: wctx.enter_context(nc.semaphore(n))
        zeroed, loaded, masks, scaled, prod, folded = (wsem(n) for n in
            ("w_zeroed", "w_loaded", "w_masks", "w_scaled", "w_prod", "w_folded"))
        with nc.Block() as block:
            @block.sync
            def _(sp):
                for i, n in enumerate(("ln_q_w", "ln_q_b", "ln_kv_w", "ln_kv_b", "proj_b")):
                    for b in range(2):
                        sp.dma_start(vec[C * b:C * b + C, i:i + 1], A["L0_tok_" + n].rearrange("(c o) -> c o", o=1)).then_inc(loaded, 16)
                sp.wait_ge(zeroed, 1)
                for b in range(2):
                    s = slice(C * b, C * b + C)
                    sp.dma_start(w_ld[s, 0, s], A["WqT"]).then_inc(loaded, 16)
                    sp.dma_start(w_ld[s, 1, s], A["WkvT"][:, 0:C]).then_inc(loaded, 16)
                    sp.dma_start(w_ld[s, 2, s], A["WkvT"][:, C:2 * C]).then_inc(loaded, 16)
                    sp.dma_start(w_ld[s, 3, s], A["projT"]).then_inc(loaded, 16)
                sp.wait_ge(loaded, 16 * 18)

            @block.gpsimd
            def _(pool):
                g = nc.gpsimd
                n = [0]

                def step(ins):
                    ins.then_inc(masks, 1)
                    n[0] += 1
                    pool.wait_ge(masks, n[0])

                def band(view, fill_outside, lo_base, lo_pat, lo_mul, hi_base, hi_pat, hi_mul):
                    step(g.affine_select(out=view, in_=view, compare_op=ALU.is_ge, fill=fill_outside, base=lo_base,
                                         pattern=lo_pat, channel_multiplier=lo_mul))
                    step(g.affine_select(out=view, in_=view, compare_op=ALU.is_ge, fill=fill_outside, base=hi_base,
                                         pattern=hi_pat, channel_multiplier=hi_mul))

                step(g.memset(avg[:, :], 1.0 / C))
                for m in range(2):
                    v = avg[:, C * m:C * m + C]
                    band(v, 0.0, -C * m, [[0, C]], 1, C * m + C - 1, [[0, C]], -1)
                step(g.memset(cen[:, :], 0.0))
                step(g.affine_select(out=cen[:, :], in_=cen[:, :], compare_op=ALU.not_equal, fill=1.0, base=0,
                                     pattern=[[-1, P]], channel_multiplier=1))
                step(g.tensor_tensor(cen[:, :], cen[:, :], avg[:, :], ALU.subtract))
                step(g.memset(sel[:, :, :], 0.0))
                for e in range(2):
                    v = sel[:, e, 16 * e:16 * e + 16]
                    step(g.memset(v, 1.0))
                    band(v, 0.0, 0, [[-HD, 16]], 1, HD - 1, [[HD, 16]], -1)
                step(g.memset(msel[:, :, :], 0.0))
                for e in range(2):
                    for b in range(2):
                        v = msel[:, e, 16 * e + 8 * b:16 * e + 8 * b + 8]
                        step(g.memset(v, 1.0 / C))
                        band(v, 0.0, -C * b, [[0, 8]], 1, C * b + C - 1, [[0, 8]], -1)
                step(g.memset(e_f[:, :, :], 1.0))
                band(e_f[:, :, :], 0.0, 0, [[16 * HD, NCH], [1, P]], -HD, HD - 1, [[-16 * HD, NCH], [-1, P]], HD)
                step(g.memset(eps[:, :], EPS))

            @block.vector
            def _(v):
                nc.vector.memset(w_ld[:, :, :], 0.0).then_inc(zeroed, 1)
                v.wait_ge(loaded, 16 * 18)
                v.wait_ge(masks, 32)
                for i, w in ((0, 0), (1, 2), (2, 2)):
                    nc.vector.tensor_scalar(w_sc[:, i, :], w_ld[:, i, :], vec[:, w:w + 1], None, ALU.mult).then_inc(scaled, 1)
                nc.vector.tensor_copy(e_r[:, :, :], e_f[:, :, :]).then_inc(scaled, 1)
                v.wait_ge(prod, 1)
                for i in range(2):
                    nc.vector.tensor_copy(w_hi[:, i, :], b_k[0][:, P * (i + 1):P * (i + 2)]).then_inc(folded, 1)
                nc.vector.tensor_scalar(gq[:, :], b_k[0][:, 0:P], C ** -0.5, None, ALU.mult).then_inc(folded, 1)
                nc.vector.tensor_scalar(vec[:, 5:6], b_k[1][:, 0:1], C ** -0.5, None, ALU.mult).then_inc(folded, 1)
                nc.vector.tensor_copy(vec[:, 6:7], b_k[1][:, 1:2]).then_inc(folded, 1)
                v.wait_ge(folded, 5)
                for i in range(2):
                    nc.vector.tensor_tensor(w_lo[:, i, :], b_k[0][:, P * (i + 1):P * (i + 2)], w_hi[:, i, :].bitcast(F32),
                                            ALU.subtract).then_inc(folded, 1)
                v.wait_ge(prod, 2)
                nc.vector.tensor_tensor(vec[:, 7:8], b_w[0][:, 0:1], vec[:, 4:5], ALU.add).then_inc(folded, 1)

            @block.tensor
            def _(pe):
                pe.wait_ge(scaled, 4)
                for i in range(3):
                    nc.tensor.matmul(b_k[0][:, P * i:P * (i + 1)], cen[:, :], w_sc[:, i, :], start=True, stop=True)
                nc.tensor.matmul(b_k[1][:, 0:1], w_ld[:, 0, :], vec[:, 1:2], start=True, stop=True)
                nc.tensor.matmul(b_k[1][:, 1:2], w_ld[:, 2, :], vec[:, 3:4], start=True, stop=True).then_inc(prod, 1)
                pe.wait_ge(folded, 7)
                nc.tensor.matmul(b_w[0][:, 0:1], w_ld[:, 3, :], vec[:, 6:7], start=True, stop=True).then_inc(prod, 1)

    N = "x_in0 x_in1 split_hi split_lo squared pooled pooled_copied pooled_squared pooled_biased q_moments q_mean_sq q_var q_ln q_rstd q_product q_scaled q_ready " \
        "moments square_sums kv_mean_sq kv_var kv_clamped kv_ln kv_rstd k_product qk_ready scores scores_scaled scores_max scores_shifted exps " \
        "exp_sum exp_recip exps_scaled weights weights_hi weights_lo a_spread va_ready v_product v_copied " \
        "halved quartered attn_out h1_ready"
    class Z:
        pass
    z = {n: sem(n) for n in N.split()}
    x_in = [z["x_in0"], z["x_in1"]]

    def tile(k, o):
        return 2 * k + o, o % 2

    block = ctx.enter_context(nc.Block())

    STEADY = (TILES - 2) // 2

    @block.sync
    def _(sp):
        def load(k, o):
            t, par = tile(k, o)
            sp.dma_start(x[:, par, :], x_v[t, :, :] if isinstance(t, int) else x_v[bass.ds(t, 1), :, :].rearrange("o p n -> (o p) n")).then_inc(x_in[par], 16)

        load(0, 0)
        load(0, 1)

        def reload(k, o):
            t, par = tile(k, o)
            sp.wait_ge(z["split_lo"], 2 * t - 2)
            sp.wait_ge(z["pooled"], 2 * t - 2)
            sp.wait_ge(z["square_sums"], 2 * t - 2)
            load(k, o)

        with sp.Fori(1, STEADY + 1) as k:
            reload(k, 0)
            reload(k, 1)

    @block.scalar
    def _(act):
        a = nc.scalar

        def split(k, o, half, first=False):
            t, par = tile(k, o)
            s = slice(half * PIX // 2, (half + 1) * PIX // 2)
            a.activation(x_hi[:, par, s], x[:, par, s], ACT.Copy).then_inc(z["split_hi"], 1)

        def square(k, o, half, part, first=False):
            t, par = tile(k, o)
            if part == 0 and not (first and half == 0):
                act.wait_ge(z["square_sums"], 2 * t + half)
            src = x[:, par, :].rearrange("p (j e n) -> p j e n", e=2, n=CH)[:, 2 * part:2 * part + 2, half, :]
            a.activation(x_sq[:, 2 * part:2 * part + 2, :], src, ACT.Square).then_inc(z["squared"], 1)

        def q_front(k, o):
            t, par = tile(k, o)
            act.wait_ge(z["pooled"], 2 * t + 2)
            src = px_sum[:, :]
            a.activation(rs2[:, 0:TOK], src, ACT.Copy, scale=1.0 / NP).then_inc(z["pooled_copied"], 1)
            a.activation(rs2[:, TOK:2 * TOK], src, ACT.Square, scale=1.0 / NP).then_inc(z["pooled_squared"], 1)
            a.activation(h1[:, bass.ts(t, TOK)], src, ACT.Identity, scale=1.0 / NP, bias=vec[:, 7:8]).then_inc(z["pooled_biased"], 1)

        def q_moment(k, o):
            t, par = tile(k, o)
            act.wait_ge(z["q_moments"], t + 1)
            a.activation(rq[:, :], b_b[:, 0:TOK], ACT.Square).then_inc(z["q_mean_sq"], 1)

        def q_back(k, o):
            t, par = tile(k, o)
            act.wait_ge(z["q_var"], t + 1)
            a.activation(rq[:, :], rq[:, :], ACT.Ln, bias=eps[:, :]).then_inc(z["q_ln"], 1)
            act.wait_ge(z["q_ln"], t + 1)
            a.activation(rq[:, :], rq[:, :], ACT.Exp, scale=-0.5).then_inc(z["q_rstd"], 1)

        def q_final(k, o):
            t, par = tile(k, o)
            act.wait_ge(z["q_scaled"], t + 1)
            a.activation(q4[:, :, :].rearrange("p h (w s) -> p (h w) s", s=S),
                         qs[:, :].rearrange("p (n s) -> p n s", s=1).broadcast_to([P, TOK, S]),
                         ACT.Identity, bias=vec[:, 5:6]).then_inc(z["q_ready"], 1)

        def kv_mean(k, o):
            t, par = tile(k, o)
            act.wait_ge(z["moments"], t + 1)
            a.activation(rkv[:, :], b_m[:, :], ACT.Square).then_inc(z["kv_mean_sq"], 1)

        def kv_rstd(k, o):
            t, par = tile(k, o)
            act.wait_ge(z["kv_clamped"], t + 1)
            a.activation(rkv[:, :], rkv[:, :], ACT.Ln, bias=eps[:, :]).then_inc(z["kv_ln"], 1)
            act.wait_ge(z["kv_ln"], t + 1)
            a.activation(rkv[:, :], rkv[:, :], ACT.Exp, scale=-0.5).then_inc(z["kv_rstd"], 1)

        def copy_v(k, o, n):
            t, par = tile(k, o)
            act.wait_ge(z["v_product"], NCH * t + n + 1)
            a.activation(v_sb[:, n, :], b_w[n % 2][:, :], ACT.Copy).then_inc(z["v_copied"], 1)

        def softmax_exp(k, o):
            t, par = tile(k, o)
            act.wait_ge(z["scores_shifted"], 2 * t + 2)
            a.activation(ex[:, :], sc[:, :], ACT.Exp).then_inc(z["exps"], 1)

        def prepare(k, o, first=False):
            t, par = tile(k, o)
            act.wait_ge(x_in[par], 16 * (k + o // 2 + 1))
            if not (first or isinstance(t, int) and t < 2):
                act.wait_ge(z["v_product"], NCH * (t - 1))
            split(k, o, 0)
            split(k, o, 1)

        def step(k, o, last=False):
            if not last:
                prepare(k, o + 1)
            kv_mean(k, o)
            if not last:
                square(k, o + 1, 0, 0)
                square(k, o + 1, 0, 1)
            kv_rstd(k, o)
            copy_v(k, o, 0)
            copy_v(k, o, 1)
            if not last:
                square(k, o + 1, 1, 0)
            copy_v(k, o, 2)
            if not last:
                q_front(k, o + 1)
            copy_v(k, o, 3)
            copy_v(k, o, 4)
            if not last:
                q_moment(k, o + 1)
            softmax_exp(k, o)
            if not last:
                q_back(k, o + 1)
            copy_v(k, o, 5)
            if not last:
                square(k, o + 1, 1, 1)
            copy_v(k, o, 6)
            if not last:
                q_final(k, o + 1)
            copy_v(k, o, 7)

        act.preload_act_table_set("natural_log_exp_and_others")
        prepare(0, 0, first=True)
        for part in range(2):
            square(0, 0, 0, part, first=True)
        q_front(0, 0)
        q_moment(0, 0)
        for part in range(2):
            square(0, 0, 1, part)
        q_back(0, 0)
        q_final(0, 0)
        step(0, 0)
        with act.Fori(0, STEADY) as k:
            step(k, 1)
            step(k, 2)
        step(STEADY, 1, last=True)

    @block.gpsimd
    def _(pool):
        g = nc.gpsimd

        def split(k, o, half, first=False):
            t, par = tile(k, o)
            s = slice(half * PIX // 2, (half + 1) * PIX // 2)
            if half == 0 and not first:
                pool.wait_ge(z["v_product"], NCH * (t - 1))
            pool.wait_ge(z["split_hi"], 2 * t + half + 1)
            g.tensor_tensor(x_lo[:, par, s], x[:, par, s], x_hi[:, par, s].bitcast(F32), ALU.subtract).then_inc(z["split_lo"], 1)

        def fold(k, o, half, first=False):
            t, par = tile(k, o)
            pool.wait_ge(z["va_ready"], NCH * t + 4 * half + 4)
            v = va[:, 4 * half:4 * half + 4, :].rearrange("p j (h s w) -> p (j h) s w", s=S, w=HW)
            p1 = pre1[:, :].rearrange("p (g s w) -> p g s w", s=2, w=HW)
            if not (first and half == 0):
                pool.wait_ge(z["quartered"], 2 * t + half)
            g.tensor_tensor(p1, v[:, :, 0:2, :], v[:, :, 2:4, :], ALU.add).then_inc(z["halved"], 1)
            pool.wait_ge(z["halved"], 2 * t + half + 1)
            if half == 0 and not first:
                pool.wait_ge(z["attn_out"], t)
            dst = pre2[:, :, :].rearrange("p (j e h) w -> p j e h w", e=2, h=2)[:, :, half, :, :]
            p1 = pre1[:, :].rearrange("p (j h s w) -> p j h s w", h=2, s=2, w=HW)
            g.tensor_tensor(dst, p1[:, :, :, 0, :], p1[:, :, :, 1, :], ALU.add).then_inc(z["quartered"], 1)

        def step(k, o, first=False, last=False):
            if not last:
                split(k, o + 1, 0, first=first)
            if not first:
                fold(k, o - 1, 0, first=isinstance(k, int) and 2 * k + o == 1)
                fold(k, o - 1, 1)
            if not last:
                split(k, o + 1, 1)

        split(0, 0, 0, first=True)
        split(0, 0, 1)
        step(0, 0, first=True)
        step(0, 1)
        with pool.Fori(1, STEADY) as k:
            step(k, 0)
            step(k, 1)
        step(STEADY, 0)
        step(STEADY, 1, last=True)
        fold(STEADY, 1, 0)
        fold(STEADY, 1, 1)

    @block.vector
    def _(v):
        d = nc.vector

        def pool_px(k, o):
            t, par = tile(k, o)
            v.wait_ge(x_in[par], 16 * (k + o // 2 + 1))
            if not (isinstance(t, int) and t == 0):
                v.wait_ge(z["pooled_biased"], t)
            for half in range(2):
                d.tensor_reduce(px_sum[:, half * TOK // 2:(half + 1) * TOK // 2].rearrange("p (h w) -> p h w", w=TH),
                                x[:, par, half * PIX // 2:(half + 1) * PIX // 2].rearrange("p (h s w u) -> p h w s u", h=TH // 2, s=S, u=S),
                                AX.XY, ALU.add).then_inc(z["pooled"], 1)

        def qk_mul(k, o, n):
            t, par = tile(k, o)
            j = ORDER[n]
            if n == 0:
                v.wait_ge(z["q_ready"], t + 1)
            v.wait_ge(z["k_product"], NCH * t + n + 1)
            if n % 4 == 0 and not (isinstance(t, int) and t == 0):
                v.wait_ge(z["scores"], 2 * t + n // 4 - 1)
            d.tensor_tensor(qk[:, n, :].rearrange("p (h s w) -> p h s w", s=S, w=HW),
                            b_k[n % 2][:, :].rearrange("p (h s w) -> p h s w", s=S, w=HW),
                            q4[:, 2 * j:2 * j + 2, :].rearrange("p h (o w) -> p h o w", o=1).broadcast_to([P, 2, S, HW]),
                            ALU.mult).then_inc(z["qk_ready"], 1)

        def va_mul(k, o, n):
            t, par = tile(k, o)
            v.wait_ge(z["a_spread"], NCH * t + n + 1)
            if n == 0:
                v.wait_ge(z["v_copied"], NCH * (t + 1))
            if n % 4 == 0 and not (isinstance(t, int) and t == 0):
                v.wait_ge(z["halved"], 2 * t - 1 + n // 4)
            d.tensor_tensor(va[:, n, :], b_w[n % 2][:, :], v_sb[:, n, :], ALU.mult).then_inc(z["va_ready"], 1)

        def kv_var(k, o):
            t, par = tile(k, o)
            v.wait_ge(z["kv_mean_sq"], t + 1)
            v.wait_ge(z["square_sums"], 2 * t + 2)
            d.tensor_tensor(rkv[:, :], b_q[:, :], rkv[:, :], ALU.subtract).then_inc(z["kv_var"], 1)
            v.wait_ge(z["kv_var"], t + 1)
            d.tensor_scalar(rkv[:, :], rkv[:, :], 0.0, None, ALU.max).then_inc(z["kv_clamped"], 1)

        hs = lambda a, h: a[:, 256 * h:256 * h + 256].rearrange("p (s w u) -> p s w u", s=S, u=S)
        hb = lambda a, h: a[:, TH * h:TH * h + TH].rearrange("p (a w u) -> p a w u", a=1, u=1).broadcast_to([P, S, TH, S])

        def softmax_a(k, o):
            t, par = tile(k, o)
            v.wait_ge(z["scores"], 2 * t + 2)
            v.wait_ge(z["kv_rstd"], t + 1)
            d.tensor_tensor(sc[:, :], b_s[:, :], rkv[:, :], ALU.mult).then_inc(z["scores_scaled"], 1)
            v.wait_ge(z["scores_scaled"], t + 1)
            d.tensor_reduce(mx[:, :].rearrange("p (h w) -> p h w", w=TH),
                            sc[:, :].rearrange("p (h s w u) -> p h w s u", h=2, s=S, u=S), AX.XY, ALU.max).then_inc(z["scores_max"], 1)
            v.wait_ge(z["scores_max"], t + 1)
            for h in range(2):
                d.tensor_tensor(hs(sc, h), hs(sc, h), hb(mx, h), ALU.subtract).then_inc(z["scores_shifted"], 1)

        def softmax_b(k, o, first=False, last=False):
            t, par = tile(k, o)
            v.wait_ge(z["exps"], t + 1)
            d.tensor_reduce(sm[:, :].rearrange("p (h w) -> p h w", w=TH),
                            ex[:, :].rearrange("p (h s w u) -> p h w s u", h=2, s=S, u=S), AX.XY, ALU.add).then_inc(z["exp_sum"], 1)
            v.wait_ge(z["exp_sum"], t + 1)
            d.reciprocal(rc[:, :], sm[:, :]).then_inc(z["exp_recip"], 1)
            d.tensor_tensor(ex[:, :], ex[:, :], rkv[:, :], ALU.mult).then_inc(z["exps_scaled"], 1)
            if not last:
                q_scale(k, o + 1)
            v.wait_ge(z["exps_scaled"], t + 1)
            v.wait_ge(z["exp_recip"], t + 1)
            for h in range(2):
                d.tensor_tensor(hs(ex, h), hs(ex, h), hb(rc, h), ALU.mult).then_inc(z["weights"], 1)
            v.wait_ge(z["weights"], 2 * t + 2)
            if not first:
                v.wait_ge(z["a_spread"], NCH * t)
            d.tensor_copy(a_hi[:, :], ex[:, :]).then_inc(z["weights_hi"], 1)
            v.wait_ge(z["weights_hi"], t + 1)
            d.tensor_tensor(a_lo[:, :], ex[:, :], a_hi[:, :].bitcast(F32), ALU.subtract).then_inc(z["weights_lo"], 1)

        def q_var(k, o):
            t, par = tile(k, o)
            v.wait_ge(z["q_mean_sq"], t + 1)
            d.scalar_tensor_tensor(rq[:, :], rq[:, :], -1.0, b_b[:, TOK:2 * TOK], ALU.mult, ALU.add).then_inc(z["q_var"], 1)

        def q_scale(k, o):
            t, par = tile(k, o)
            v.wait_ge(z["q_rstd"], t + 1)
            v.wait_ge(z["q_product"], t + 1)
            d.tensor_tensor(qs[:, :], b_b[:, 0:TOK], rq[:, :], ALU.mult).then_inc(z["q_scaled"], 1)

        def finish(k, o):
            t, par = tile(k, o)
            v.wait_ge(z["attn_out"], t + 1)
            v.wait_ge(z["pooled_biased"], t + 1)
            dst = h1[:, bass.ts(t, TOK)]
            d.tensor_tensor(dst, b_b[:, 0:TOK], dst, ALU.add).then_inc(z["h1_ready"], 1)

        def step(k, o, first=False, last=False):
            for n in range(NCH):
                qk_mul(k, o, n)
                if not first:
                    va_mul(k, o - 1, n)
                if n == 4:
                    kv_var(k, o)
                if n == 5 and not (isinstance(k, int) and 2 * k + o < 2):
                    finish(k, o - 2)
            if not last:
                pool_px(k, o + 1)
            softmax_a(k, o)
            if not last:
                q_var(k, o + 1)
            softmax_b(k, o, first=first, last=last)

        pool_px(0, 0)
        q_var(0, 0)
        q_scale(0, 0)
        step(0, 0, first=True)
        step(0, 1)
        step(0, 2)
        with v.Fori(1, STEADY) as k:
            step(k, 1)
            step(k, 2)
        step(STEADY, 1, last=True)
        for n in range(NCH):
            va_mul(STEADY, 1, n)
            if n == 4:
                finish(STEADY, 0)
        finish(STEADY, 1)

    @block.tensor
    def _(pe):
        mm = nc.tensor.matmul

        def px(buf, par, j):
            return buf[:, par, CH * j:CH * j + CH]

        def three(dst, w, par, j):
            mm(dst, w_hi[:, w, :], px(x_hi, par, j), start=True, stop=False)
            mm(dst, w_lo[:, w, :], px(x_hi, par, j), start=False, stop=False)
            return mm(dst, w_hi[:, w, :], px(x_lo, par, j), start=False, stop=True)

        def k_mm(k, o, n):
            t, par = tile(k, o)
            if n == 0:
                pe.wait_ge(z["split_lo"], 2 * t + 2)
            if not (isinstance(t, int) and t == 0 and n < 2):
                pe.wait_ge(z["qk_ready"], NCH * t + n - 1)
            three(b_k[n % 2][:, :], 0, par, ORDER[n]).then_inc(z["k_product"], 1)

        def v_mm(k, o, n, first=False):
            t, par = tile(k, o)
            if n < 2:
                if not first:
                    pe.wait_ge(z["va_ready"], NCH * (t - 1) + 7 + n)
            else:
                pe.wait_ge(z["v_copied"], NCH * t + n - 1)
            three(b_w[n % 2][:, :], 1, par, ORDER[n]).then_inc(z["v_product"], 1)

        def spread(k, o, n):
            t, par = tile(k, o)
            if n == 0:
                pe.wait_ge(z["weights_lo"], t + 1)
            if n < 2:
                pe.wait_ge(z["v_copied"], NCH * t + 7 + n)
            else:
                pe.wait_ge(z["va_ready"], NCH * t + n - 1)
            mm(b_w[n % 2][:, :], e_r[:, ORDER[n], :], a_hi[:, :], start=True, stop=False)
            mm(b_w[n % 2][:, :], e_r[:, ORDER[n], :], a_lo[:, :], start=False, stop=True).then_inc(z["a_spread"], 1)

        def scores(k, o, e):
            t, par = tile(k, o)
            pe.wait_ge(z["qk_ready"], NCH * t + 4 * e + 4)
            if e == 0 and not (isinstance(t, int) and t == 0):
                pe.wait_ge(z["scores_scaled"], t)
            for c in range(4):
                i = mm(b_s[32 * c:32 * c + 32, :], sel[:, e, :], qk[:, 4 * e + c, :], start=e == 0, stop=e == 1)
            i.then_inc(z["scores"], 1)

        def sums(k, o, e):
            t, par = tile(k, o)
            pe.wait_ge(z["squared"], 4 * t + 2 * e + 2)
            if e == 0 and not (isinstance(t, int) and t == 0):
                pe.wait_ge(z["kv_var"], t)
            for c in range(4):
                i = mm(b_m[32 * c:32 * c + 32, :], msel[:, e, :], px(x, par, 2 * c + e), start=e == 0, stop=e == 1)
            if e == 1:
                i.then_inc(z["moments"], 1)
            for c in range(4):
                i = mm(b_q[32 * c:32 * c + 32, :], msel[:, e, :], x_sq[:, c, :], start=e == 0, stop=e == 1)
            i.then_inc(z["square_sums"], 1)

        def q_moments(k, o):
            t, par = tile(k, o)
            pe.wait_ge(z["pooled_squared"], t + 1)
            pe.wait_ge(z["pooled_copied"], t + 1)
            if not (isinstance(t, int) and t < 3):
                pe.wait_ge(z["h1_ready"], t - 2)
            if not (isinstance(t, int) and t == 0):
                pe.wait_ge(z["q_scaled"], t)
            mm(b_b[:, :], avg[:, :], rs2[:, :], start=True, stop=True).then_inc(z["q_moments"], 1)

        def q_mm(k, o):
            t, par = tile(k, o)
            pe.wait_ge(z["q_var"], t + 1)
            mm(b_b[:, 0:TOK], gq[:, :], rs2[:, 0:TOK], start=True, stop=True).then_inc(z["q_product"], 1)

        def out_mm(k, o, scaled):
            t, par = tile(k, o)
            pe.wait_ge(z["quartered"], 2 * t + 2)
            pe.wait_ge(z["q_scaled"], scaled)
            if not (isinstance(t, int) and t == 0):
                pe.wait_ge(z["h1_ready"], t)
            p2 = pre2[:, :, :].rearrange("p h (w u) -> p (h w) u", u=S)
            for u in range(S):
                i = mm(b_b[:, 0:TOK], w_ld[:, 3, :], p2[:, :, u], start=u == 0, stop=u == S - 1)
            i.then_inc(z["attn_out"], 1)

        def step(k, o, first=False, last=False):
            for n in range(NCH):
                if n == 5:
                    scores(k, o, 0)
                k_mm(k, o, n)
                if n == 1:
                    sums(k, o, 1)
                if not first:
                    spread(k, o - 1, n)
            if not last:
                sums(k, o + 1, 0)
            v_mm(k, o, 0, first=first)
            scores(k, o, 1)
            for n in range(1, 5):
                v_mm(k, o, n, first=first)
            if not last:
                q_moments(k, o + 1)
            v_mm(k, o, 5)
            if not last:
                q_mm(k, o + 1)
            v_mm(k, o, 6)
            v_mm(k, o, 7)
            if not first:
                out_mm(k, o - 1, 2 * k + o + (1 if last else 2))
        sums(0, 0, 0)
        q_moments(0, 0)
        q_mm(0, 0)
        step(0, 0, first=True)
        step(0, 1)
        step(0, 2)
        with pe.Fori(1, STEADY) as k:
            step(k, 1)
            step(k, 2)
        step(STEADY, 1, last=True)
        for n in range(NCH):
            spread(STEADY, 1, n)
        out_mm(STEADY, 1, TILES)


N_ST = 128
NODES = 255
LEVELS = 8
NT = TILES * 4
ROW = 144
UNITS = 12


def scan_and_logits(nc, ctx, A, h1, pay, lg):
    def sb(name, shape, dt=F32):
        return ctx.enter_context(nc.sbuf_tensor(name, shape, dt))

    def sem(name):
        return ctx.enter_context(nc.semaphore(name))

    w_p = sb("w_p", [P, 2, 4, N_ST])
    w_y = sb("w_y", [P, C])
    b_p = sb("b_p", [P, 5])
    w1 = sb("w1", [P, 2, 256])
    b1 = sb("b1", [P, 256])
    avg = sb("avg2", [P, P])
    ident = sb("ident", [P, P])
    eps = sb("eps2", [P, 1])
    xc2, sq2, r2, xc3, sq3, r3 = (sb(n, [P, TOK]) for n in ("xc2", "sq2", "r2", "xc3", "sq3", "r3"))
    xn2, xn3, h2 = (sb(n, [P, 2, TOK]) for n in ("xn2", "xn3", "h2"))
    delta, mag, pos, drive, states, y = (sb(n, [P, 2 * TOK]) for n in ("delta", "mag", "pos", "drive", "states", "y"))
    decay, om = (sb(n, [P, 2, 2 * TOK]) for n in ("decay", "om"))
    def bank(name):
        return ctx.enter_context(nc.psum_tensor(name, [P, CH], F32))
    b_x, b_bc, b_d, b_l2, b_l3, b_g0, b_g1, b_y = (bank("s_" + n) for n in ("x", "bc", "d", "l2", "l3", "g0", "g1", "y"))

    with ExitStack() as wctx:
        zeroed, loaded, masks = (wctx.enter_context(nc.semaphore(n)) for n in ("w2_zeroed", "w2_loaded", "w2_masks"))
        with nc.Block() as block:
            @block.sync
            def _(sp):
                sp.wait_ge(zeroed, 2)
                n = 0
                def ld(dst, src):
                    nonlocal n
                    sp.dma_start(dst, src).then_inc(loaded, 16)
                    n += 16
                for b in range(2):
                    s = slice(C * b, C * b + C)
                    ld(w_p[s, b, 0, :], A["L0_attn_Wx"])
                    ld(w_p[s, b, 1:3, :], A["L0_attn_Wbc"].rearrange("c (k n) -> c k n", k=2))
                    ld(w_p[s, b, 3, :], A["L0_attn_Wd"])
                    ld(b_p[s, 4:5], A["L0_attn_by"].rearrange("(c o) -> c o", o=1))
                    ld(w1[s, b, 0:NODES], A["w1T"])
                ld(w_y[:, :], A["L0_attn_Wy"])
                ld(b_p[:, 0:1], A["L0_attn_bx"].rearrange("(c o) -> c o", o=1))
                for i in range(2):
                    ld(b_p[:, 1 + i:2 + i], A["L0_attn_bbc"][N_ST * i:N_ST * i + N_ST].rearrange("(c o) -> c o", o=1))
                ld(b_p[:, 3:4], A["L0_attn_bd"].rearrange("(c o) -> c o", o=1))
                ld(b1[:, 0:NODES], A["b1r"].broadcast_to([P, NODES]))
                sp.wait_ge(loaded, n)

            @block.vector
            def _(v):
                nc.vector.memset(w_p[:, :, :, :], 0.0).then_inc(zeroed, 1)
                nc.vector.memset(w1[:, :, :], 0.0).then_inc(zeroed, 1)
                nc.vector.memset(b1[:, NODES:256], 0.0)
                nc.vector.memset(eps[:, :], EPS)

            @block.gpsimd
            def _(pool):
                g = nc.gpsimd
                k = [0]
                def step(ins):
                    ins.then_inc(masks, 1)
                    k[0] += 1
                    pool.wait_ge(masks, k[0])
                step(g.memset(avg[:, :], 1.0 / C))
                for m in range(2):
                    v = avg[:, C * m:C * m + C]
                    step(g.affine_select(out=v, in_=v, compare_op=ALU.is_ge, fill=0.0, base=-C * m, pattern=[[0, C]], channel_multiplier=1))
                    step(g.affine_select(out=v, in_=v, compare_op=ALU.is_ge, fill=0.0, base=C * m + C - 1, pattern=[[0, C]], channel_multiplier=-1))
                step(g.memset(ident[:, :], 0.0))
                step(g.affine_select(out=ident[:, :], in_=ident[:, :], compare_op=ALU.not_equal, fill=1.0, base=0, pattern=[[-1, P]], channel_multiplier=1))

    mean2, centred2, squared2, var2, ln2, rstd2, norm2 = (sem("s2_" + n) for n in "mean centred squared var ln rstd norm".split())
    proj_b, proj_x, proj_c, proj_d = (sem("s2_proj_" + n) for n in "bxcd")
    biased, magnitude, exp_mag, log_mag, softplus, decayed, one_minus, gated, driven, scanned, gated_y, y_out, h2_ready = (sem("s2_" + n) for n in
        "biased magnitude exp_mag log_mag softplus decayed one_minus gated driven scanned gated_y y_out h2_ready".split())
    mean3, centred3, squared3, var3, ln3, rstd3, norm3 = (sem("s3_" + n) for n in "mean centred squared var ln rstd norm".split())
    h_kept, x_rows, x_kept, logits01, logits23, kept01, kept23 = (sem("s3_" + n) for n in "h_kept x_rows x_kept logits01 logits23 kept01 kept23".split())
    block = ctx.enter_context(nc.Block())

    def due(n):
        return not isinstance(n, int) or n > 0

    def there(t):
        return not isinstance(t, int) or 0 <= t < TILES

    def sweep(eng, step):
        for i in range(-2, 4):
            step(0, i)
        with eng.Fori(2, TILES // 2 - 1) as k:
            step(k, 0)
            step(k, 1)
        for i in range(TILES - 2, TILES + 2):
            step(0, i)

    @block.tensor
    def _(pe):
        mm = nc.tensor.matmul

        def project(bk, kind, t, q, done):
            for b in range(2):
                j = mm(bk[:, TOK * b:TOK * b + TOK], w_p[:, b, kind, :], xn2[:, q, :], start=True, stop=True)
            j.then_inc(done, 1)

        def step(k, o):
            i = 2 * k + o
            q = o % 2
            if there(i):
                pe.wait_ge(norm2, i + 1)
                if due(i):
                    pe.wait_ge(gated_y, i)
                project(b_bc, 1, i, q, proj_b)
                project(b_x, 0, i, q, proj_x)
            if there(i + 1):
                pe.wait_ge(norm2, i + 2)
                if due(i + 1):
                    pe.wait_ge(biased, i + 1)
                project(b_d, 3, i + 1, 1 - q, proj_d)
            if there(i):
                pe.wait_ge(gated, i + 1)
                project(b_bc, 2, i, q, proj_c)
            if there(i - 1):
                pe.wait_ge(h2_ready, i)
                if due(i - 1):
                    pe.wait_ge(ln3, i - 1)
                for f in range(2):
                    nc.tensor.transpose(b_l3[:, TOK + P * f:TOK + P * f + P], h2[:, 1 - q, P * f:P * f + P], ident[:, :])
                mm(b_l3[:, 0:TOK], avg[:, :], h2[:, 1 - q, :], start=True, stop=True).then_inc(mean3, 1)
            if there(i + 2):
                if due(i + 2):
                    pe.wait_ge(ln2, i + 2)
                mm(b_l2[:, 0:TOK], avg[:, :], h1[:, bass.ts(i + 2, TOK)], start=True, stop=True).then_inc(mean2, 1)
            if there(i - 2):
                pe.wait_ge(norm3, i - 1)
                if there(i - 1):
                    pe.wait_ge(h2_ready, i)
                for f in range(2):
                    j = nc.tensor.transpose(b_y[:, P * f:P * f + P], xn3[:, q, P * f:P * f + P], ident[:, :])
                j.then_inc(x_rows, 1)
                if due(i - 2):
                    pe.wait_ge(kept01, i - 2)
                for f in range(2):
                    j = mm(b_g0[:, 256 * f:256 * f + 256], xn3[:, q, P * f:P * f + P], w1[:, 0, :], start=True, stop=True)
                j.then_inc(logits01, 1)
            if there(i - 1):
                pe.wait_ge(squared3, i)
                pe.wait_ge(h_kept, i)
                mm(b_l3[:, 0:TOK], avg[:, :], sq3[:, :], start=True, stop=True).then_inc(var3, 1)
            if there(i):
                pe.wait_ge(gated_y, i + 1)
                if there(i - 2):
                    pe.wait_ge(x_kept, i - 1)
                for b in range(2):
                    j = mm(b_y[C * b:C * b + C, TOK:2 * TOK], w_y[:, :], y[:, TOK * b:TOK * b + TOK], start=True, stop=True)
                j.then_inc(y_out, 1)
            if there(i + 2):
                pe.wait_ge(squared2, i + 3)
                mm(b_l2[:, 0:TOK], avg[:, :], sq2[:, :], start=True, stop=True).then_inc(var2, 1)
            if there(i - 2):
                if due(i - 2):
                    pe.wait_ge(kept23, i - 2)
                for f in range(2):
                    j = mm(b_g1[:, 256 * f:256 * f + 256], xn3[:, q, P * f:P * f + P], w1[:, 1, :], start=True, stop=True)
                j.then_inc(logits23, 1)

        sweep(pe, step)

    @block.scalar
    def _(act):
        a = nc.scalar
        act.preload_act_table_set("natural_log_exp_and_others")

        def step(k, o):
            i = 2 * k + o
            q = o % 2
            if there(i + 1):
                act.wait_ge(proj_d, i + 2)
                a.activation(delta[:, :], b_d[:, :], ACT.Identity, bias=b_p[:, 3:4]).then_inc(biased, 1)
                act.wait_ge(biased, i + 2)
                a.activation(mag[:, :], delta[:, :], ACT.Abs).then_inc(magnitude, 1)
                act.wait_ge(magnitude, i + 2)
                a.activation(mag[:, :], mag[:, :], ACT.Exp, scale=-1.0).then_inc(exp_mag, 1)
            if there(i - 1):
                act.wait_ge(centred3, i)
                a.activation(sq3[:, :], xc3[:, :], ACT.Square).then_inc(squared3, 1)
                a.activation(pay[:, bass.ts(i - 1, 4), 76:140].rearrange("p (b f) c -> p f b c", b=2),
                             b_l3[:, TOK:2 * TOK].rearrange("p (f b c) -> p f b c", f=2, b=2), ACT.Copy).then_inc(h_kept, 1)
            if there(i + 2):
                act.wait_ge(centred2, i + 3)
                a.activation(sq2[:, :], xc2[:, :], ACT.Square).then_inc(squared2, 1)
            if there(i + 1):
                act.wait_ge(exp_mag, i + 2)
                a.activation(mag[:, :], mag[:, :], ACT.Ln, bias=1.0).then_inc(log_mag, 1)
            if there(i - 2):
                act.wait_ge(x_rows, i - 1)
                a.activation(pay[:, bass.ts(i - 2, 4), 0:C].rearrange("p (b f) c -> p f b c", b=2),
                             b_y[:, 0:TOK].rearrange("p (f b c) -> p f b c", f=2, b=2), ACT.Copy).then_inc(x_kept, 1)
            if there(i - 1):
                act.wait_ge(var3, i)
                a.activation(r3[:, :], b_l3[:, 0:TOK], ACT.Ln, bias=eps[:, :]).then_inc(ln3, 1)
                act.wait_ge(ln3, i)
                a.activation(r3[:, :], r3[:, :], ACT.Exp, scale=-0.5).then_inc(rstd3, 1)
            if there(i + 1):
                act.wait_ge(softplus, i + 2)
                if due(i):
                    act.wait_ge(scanned, 2 * i)
                a.activation(decay[:, 1 - q, :], pos[:, :], ACT.Exp, scale=-1.0).then_inc(decayed, 1)
            if there(i + 2):
                act.wait_ge(var2, i + 3)
                a.activation(r2[:, :], b_l2[:, 0:TOK], ACT.Ln, bias=eps[:, :]).then_inc(ln2, 1)
                act.wait_ge(ln2, i + 3)
                a.activation(r2[:, :], r2[:, :], ACT.Exp, scale=-0.5).then_inc(rstd2, 1)

        sweep(act, step)

    @block.vector
    def _(v):
        d = nc.vector

        def keep_logits(t, f, bk, ready, kept):
            v.wait_ge(ready, t + 1)
            d.tensor_tensor(lg[:, bass.ds(4 * t + 2 * f, 2), :], bk[:, :].rearrange("p (f n) -> p f n", f=2),
                            b1[:, :].rearrange("p (o n) -> p o n", o=1).broadcast_to([P, 2, 256]), ALU.add).then_inc(kept, 1)

        def step(k, o):
            i = 2 * k + o
            q = o % 2
            if there(i):
                v.wait_ge(proj_b, i + 1)
                v.wait_ge(one_minus, i + 1)
                d.scalar_tensor_tensor(om[:, q, :], b_bc[:, :], b_p[:, 1:2], om[:, q, :], ALU.add, ALU.mult).then_inc(gated, 1)
                v.wait_ge(gated, i + 1)
                v.wait_ge(proj_x, i + 1)
                d.scalar_tensor_tensor(drive[:, :], b_x[:, :], b_p[:, 0:1], om[:, q, :], ALU.add, ALU.mult).then_inc(driven, 1)
                v.wait_ge(driven, i + 1)
                v.wait_ge(decayed, i + 1)
                for b in range(2):
                    s = slice(TOK * b, TOK * b + TOK)
                    d.tensor_tensor_scan(states[:, s], decay[:, q, s], drive[:, s], 0.0, ALU.mult, ALU.add).then_inc(scanned, 1)
                v.wait_ge(scanned, 2 * i + 2)
                v.wait_ge(proj_c, i + 1)
                d.scalar_tensor_tensor(y[:, :], b_bc[:, :], b_p[:, 2:3], states[:, :], ALU.add, ALU.mult).then_inc(gated_y, 1)
            if there(i - 1):
                v.wait_ge(mean3, i)
                if due(i - 1):
                    v.wait_ge(norm3, i - 1)
                d.tensor_tensor(xc3[:, :], h2[:, 1 - q, :], b_l3[:, 0:TOK], ALU.subtract).then_inc(centred3, 1)
            if there(i + 2):
                v.wait_ge(mean2, i + 3)
                if due(i + 2):
                    v.wait_ge(norm2, i + 2)
                d.tensor_tensor(xc2[:, :], h1[:, bass.ts(i + 2, TOK)], b_l2[:, 0:TOK], ALU.subtract).then_inc(centred2, 1)
            if there(i - 2):
                keep_logits(i - 2, 0, b_g0, logits01, kept01)
            if there(i + 1):
                v.wait_ge(log_mag, i + 2)
                d.scalar_tensor_tensor(pos[:, :], delta[:, :], 0.0, mag[:, :], ALU.max, ALU.add).then_inc(softplus, 1)
            if there(i):
                v.wait_ge(y_out, i + 1)
                d.scalar_tensor_tensor(h2[:, q, :], b_y[:, TOK:2 * TOK], b_p[:, 4:5], h1[:, bass.ts(i, TOK)], ALU.add, ALU.add).then_inc(h2_ready, 1)
            if there(i - 1):
                v.wait_ge(rstd3, i)
                d.tensor_tensor(xn3[:, 1 - q, :], xc3[:, :], r3[:, :], ALU.mult).then_inc(norm3, 1)
            if there(i + 1):
                v.wait_ge(decayed, i + 2)
                d.tensor_scalar(om[:, 1 - q, :], decay[:, 1 - q, :], -1.0, 1.0, ALU.mult, ALU.add).then_inc(one_minus, 1)
            if there(i + 2):
                v.wait_ge(rstd2, i + 3)
                d.tensor_tensor(xn2[:, q, :], xc2[:, :], r2[:, :], ALU.mult).then_inc(norm2, 1)
            if there(i - 2):
                keep_logits(i - 2, 1, b_g1, logits23, kept23)

        sweep(v, step)


I32 = mybir.dt.int32
U32 = mybir.dt.uint32
BF16 = mybir.dt.bfloat16
GRP = 32
BLK = 128
TOKENS = B * TOK
NBLK = (TOKENS + GRP * (BLK - 1)) // BLK
NBLK += -NBLK % 8
X0, P0, H0, ID0 = 0, 64, 76, 140
KT = 7


def paths(nc, ctx, pay, lg, grp):
    def sb(name, shape, dt=F32):
        return ctx.enter_context(nc.sbuf_tensor(name, shape, dt))
    bits = sb("bits", [P, LEVELS - 1, NT])
    pw = sb("pw", [P, NT, LEVELS])
    n5, n6, pl, pr = (sb(n, [P, NT]) for n in ("not5", "not6", "p7_left", "p7_right"))
    chosen, magn, weight, steps, outs = (ctx.enter_context(nc.semaphore("t_" + n)) for n in ("chosen", "magn", "weight", "steps", "outs"))
    with nc.Block() as block:
        @block.vector
        def _(v):
            d = nc.vector
            n = [0]
            for l in range(LEVELS - 1):
                s = 2 ** (LEVELS - 1 - l) - 1
                d.tensor_scalar(bits[:, l, :], lg[:, :, l], 0.0, None, ALU.is_gt).then_inc(chosen, 1)
                v.wait_ge(chosen, 2 * l + 1)
                d.copy_predicated(lg[:, :, l + 1:l + 1 + s], bits[:, l, :].rearrange("p (n o) -> p n o", o=1).broadcast_to([P, NT, s]).bitcast(U32),
                                  lg[:, :, l + 1 + s:l + 1 + 2 * s]).then_inc(chosen, 1)
                v.wait_ge(chosen, 2 * l + 2)

            def step(ins):
                ins.then_inc(steps, 1)
                n[0] += 1
                v.wait_ge(steps, n[0])
            step(d.scalar_tensor_tensor(grp[:, :], bits[:, 0, :], 2.0, bits[:, 1, :], ALU.mult, ALU.add))
            for l in range(2, 5):
                step(d.scalar_tensor_tensor(grp[:, :], grp[:, :], 2.0, bits[:, l, :], ALU.mult, ALU.add))
            step(d.tensor_scalar(n5[:, :], bits[:, 5, :], -1.0, 1.0, ALU.mult, ALU.add))
            step(d.tensor_scalar(n6[:, :], bits[:, 6, :], -1.0, 1.0, ALU.mult, ALU.add))
            v.wait_ge(weight, 1)
            step(d.tensor_tensor(pl[:, :], pw[:, :, 7], n5[:, :], ALU.mult))
            step(d.tensor_tensor(pr[:, :], pw[:, :, 7], bits[:, 5, :], ALU.mult))
            step(d.tensor_copy(pay[:, :, P0:P0 + 6], pw[:, :, 0:6]))
            for u, (a, b) in enumerate(((pw[:, :, 6], n5[:, :]), (pw[:, :, 6], bits[:, 5, :]), (pl[:, :], n6[:, :]), (pl[:, :], bits[:, 6, :]),
                                        (pr[:, :], n6[:, :]), (pr[:, :], bits[:, 6, :]))):
                step(d.tensor_tensor(pay[:, :, P0 + 6 + u], a, b, ALU.mult))

        @block.scalar
        def _(act):
            a = nc.scalar
            act.wait_ge(chosen, 2 * LEVELS - 2)
            a.activation(pw[:, :, :], lg[:, :, 0:LEVELS], ACT.Abs).then_inc(magn, 1)
            act.wait_ge(magn, 1)
            a.activation(pw[:, :, :], pw[:, :, :], ACT.Gelu).then_inc(weight, 1)

        @block.gpsimd
        def _(pool):
            nc.gpsimd.iota(pay[:, :, ID0:ID0 + 1].bitcast(I32), pattern=[[P, NT], [0, 1]], base=0, channel_multiplier=1)
            nc.gpsimd.memset(pay[:, :, ID0 + 1:ROW], 0.0)


def sort_and_mix(nc, ctx, A, pay, grp, rows_d, out_d):
    def sb(name, shape, dt=F32):
        return ctx.enter_context(nc.sbuf_tensor(name, shape, dt))

    def sem(name):
        return ctx.enter_context(nc.semaphore(name))

    wt = sb("wt", [P, GRP, KT, C])
    gid = sb("gid", [1, P], I32)
    ident = sb("ident3", [P, P])
    table = sem("m_table")
    gid_ready, scattered = sem("gid_ready"), sem("scattered")

    with ExitStack() as c2:
        sb2 = lambda n, s, dt=F32: c2.enter_context(nc.sbuf_tensor(n, s, dt))
        pb2 = lambda n: c2.enter_context(nc.psum_tensor(n, [P, 512], F32))
        s2 = lambda n: c2.enter_context(nc.semaphore("o_" + n))
        oh = sb2("oh", [P, NT, GRP]); ohb = sb2("ohb", [P, NT, GRP], BF16)
        iog = sb2("iog", [P, GRP]); iop = sb2("iop", [P, 1])
        tri = sb2("tri", [P, P], BF16); one = sb2("one", [P, P], BF16)
        tot = sb2("tot", [P, GRP, NT]); inc = sb2("inc", [P, GRP, NT]); keep = sb2("keep", [P, GRP, NT])
        rank = sb2("rank", [P, NT, GRP])
        cnt, nbl, bend, base = (sb2(n, [P, GRP]) for n in ("cnt", "nbl", "bend", "base"))
        nbi = sb2("nbi", [P, GRP], I32)
        dst = sb2("dst", [P, NT]); dsti = sb2("dsti", [P, NT], I32)
        cmp = sb2("cmp", [P, GRP]); gcol = sb2("gcol", [P, 1])
        fill = sb2("fill", [P, ROW])
        pre_b = [pb2(f"pre_b{i}") for i in range(4)]; tot_b = [pb2(f"tot_b{i}") for i in range(4)]
        consts, hot, counted, steps, zeroed, filled, dest_ready, gcol_ready, gid_row = (s2(n) for n in
            "consts hot counted steps zeroed filled dest_ready gcol_ready gid_row".split())
        with nc.Block() as block:
            @block.gpsimd
            def _(pool):
                g = nc.gpsimd
                k = [0]
                def step(ins):
                    ins.then_inc(consts, 1)
                    k[0] += 1
                    pool.wait_ge(consts, k[0])
                step(g.memset(fill[:, :], 0.0))
                step(g.iota(fill[:, ID0:ID0 + 1].bitcast(I32), pattern=[[0, 1]], base=TOKENS, channel_multiplier=0))
                step(g.iota(iog[:, :], pattern=[[1, GRP]], base=0, channel_multiplier=0, allow_small_or_imprecise_dtypes=True))
                step(g.memset(tri[:, :], 1.0))
                step(g.affine_select(out=tri[:, :], in_=tri[:, :], compare_op=ALU.is_ge, fill=0.0, base=-1, pattern=[[1, P]], channel_multiplier=-1))
                step(g.memset(one[:, :], 1.0))
                step(g.memset(keep[:, :, :], 1.0))
                step(g.memset(keep[:, :, 0:1], 0.0))
                step(g.iota(iop[:, :], pattern=[[0, 1]], base=0, channel_multiplier=1, allow_small_or_imprecise_dtypes=True))
                step(g.memset(ident[:, :], 0.0))
                step(g.affine_select(out=ident[:, :], in_=ident[:, :], compare_op=ALU.not_equal, fill=1.0, base=0, pattern=[[-1, P]], channel_multiplier=1))
                step(g.memset(wt[:, :, 6, :], 0.0))
                v = wt[:, :, 6, :]
                pool.wait_ge(consts, k[0])
                g.affine_select(out=v, in_=v, compare_op=ALU.not_equal, fill=1.0, base=-(H0 - 16), pattern=[[0, GRP], [-1, C]], channel_multiplier=1).then_inc(zeroed, 1)
                pool.wait_ge(filled, 16)
                pool.wait_ge(dest_ready, 1)
                for t in range(NT):
                    g.indirect_dma_start(rows_d, bass.IndirectOffsetOnAxis(ap=dsti[:, t:t + 1], axis=0), pay[:, t, :], None).then_inc(scattered, 16)

            @block.sync
            def _(sp):
                n = 0
                def ld(dst, src):
                    nonlocal n
                    sp.dma_start(dst, src).then_inc(table, 16)
                    n += 16
                sp.wait_ge(consts, 2)
                sp.dma_start(rows_d.rearrange("(n p) c -> p n c", p=P), fill[:, :].rearrange("p (o c) -> p o c", o=1).broadcast_to([P, NBLK, ROW])).then_inc(filled, 16)
                w2 = A["w2T"]
                for l in range(6):
                    k, half = l // 2, l % 2
                    n0, cn = 2 ** l - 1, 2 ** l
                    for v in range(cn):
                        r = GRP // cn
                        if l < 5:
                            ld(wt[C * half:C * half + C, v * r:(v + 1) * r, k, :], w2[:, n0 + v:n0 + v + 1, :].broadcast_to([C, r, C]))
                    if l == 5:
                        ld(wt[C * half:C * half + C, :, k, :], w2[:, n0:n0 + cn, :])
                for half in range(2):
                    ld(wt[C * half:C * half + C, :, 3, :], w2[:, 63:127, :].rearrange("d (g u) o -> d g u o", u=2)[:, :, half, :])
                    for m in range(2):
                        ld(wt[C * half:C * half + C, :, 4 + m, :], w2[:, 127:255, :].rearrange("d (g u) o -> d g u o", u=4)[:, :, 2 * m + half, :])
                sp.wait_ge(zeroed, 1)
                b2 = A["L0_ffn_b2s"]
                for l in range(6):
                    n0, cn = 2 ** l - 1, 2 ** l
                    r = GRP // cn
                    q = P0 - 16 + l
                    ld(wt[q:q + 1, :, 6, :].rearrange("q (v r) o -> q v r o", r=r),
                       b2[n0:n0 + cn, :].rearrange("(q v r) o -> q v r o", q=1, r=1).broadcast_to([1, cn, r, C]))
                for u in range(2):
                    q = P0 - 16 + 6 + u
                    ld(wt[q:q + 1, :, 6, :], b2[63:127, :].rearrange("(q g u) o -> q g u o", q=1, u=2)[:, :, u, :])
                for u in range(4):
                    q = P0 - 16 + 8 + u
                    ld(wt[q:q + 1, :, 6, :], b2[127:255, :].rearrange("(q g u) o -> q g u o", q=1, u=4)[:, :, u, :])
                sp.wait_ge(table, n)
                sp.wait_ge(scattered, 16 * NT)

            @block.tensor
            def _(pe):
                pe.wait_ge(hot, 2)
                pe.wait_ge(consts, 6)
                for i in range(4):
                    s = ohb[:, 16 * i:16 * i + 16, :].rearrange("p a b -> p (a b)")
                    nc.tensor.matmul(tot_b[i][:, :], one[:, :], s, start=True, stop=True)
                    j = nc.tensor.matmul(pre_b[i][:, :], tri[:, :], s, start=True, stop=True)
                j.then_inc(counted, 1)
                pe.wait_ge(gcol_ready, 1)
                pe.wait_ge(consts, 11)
                nc.tensor.matmul(tot_b[0][0:1, 0:P], gcol[:, :], ident[:, :], start=True, stop=True).then_inc(gid_row, 1)

            @block.vector
            def _(v):
                d = nc.vector
                n = [0]
                def step(ins):
                    ins.then_inc(steps, 1)
                    n[0] += 1
                    v.wait_ge(steps, n[0])
                def col(a):
                    return a.rearrange("p (g o) -> p g o", o=1)
                v.wait_ge(consts, 3)
                d.tensor_tensor(oh[:, :, :], grp[:, :].rearrange("p (n o) -> p n o", o=1).broadcast_to([P, NT, GRP]),
                                iog[:, :].rearrange("p (o g) -> p o g", o=1).broadcast_to([P, NT, GRP]), ALU.is_equal).then_inc(hot, 1)
                v.wait_ge(hot, 1)
                d.tensor_copy(ohb[:, :, :], oh[:, :, :]).then_inc(hot, 1)
                v.wait_ge(counted, 1)
                for i in range(4):
                    step(d.tensor_copy(tot[:, :, 16 * i:16 * i + 16].rearrange("p g n -> p n g"), tot_b[i][:, :].rearrange("p (n g) -> p n g", g=GRP)))
                v.wait_ge(consts, 9)
                f = lambda a: a[:, :, :].rearrange("p g n -> p (g n)")
                step(d.tensor_tensor_scan(f(inc), f(keep), f(tot), 0.0, ALU.mult, ALU.add))
                step(d.tensor_scalar(nbi[:, :], inc[:, :, NT - 1], float(BLK - 1), None, ALU.add))
                step(d.tensor_scalar(nbi[:, :], nbi[:, :], BLK.bit_length() - 1, None, ALU.logical_shift_right))
                step(d.tensor_copy(nbl[:, :], nbi[:, :]))
                step(d.memset(cnt[:, :], 1.0))
                step(d.tensor_tensor_scan(bend[:, :], cnt[:, :], nbl[:, :], 0.0, ALU.mult, ALU.add))
                step(d.tensor_tensor(base[:, :], bend[:, :], nbl[:, :], ALU.subtract))
                step(d.tensor_scalar(base[:, :], base[:, :], float(BLK), None, ALU.mult))
                step(d.tensor_tensor(inc[:, :, :], inc[:, :, :], tot[:, :, :], ALU.subtract))
                step(d.tensor_tensor(inc[:, :, :], inc[:, :, :], col(base[:, :]).broadcast_to([P, GRP, NT]), ALU.add))
                for i in range(4):
                    step(d.tensor_tensor(rank[:, 16 * i:16 * i + 16, :], pre_b[i][:, :].rearrange("p (n g) -> p n g", g=GRP),
                                         inc[:, :, 16 * i:16 * i + 16].rearrange("p g n -> p n g"), ALU.add))
                step(d.tensor_tensor(rank[:, :, :], rank[:, :, :], oh[:, :, :], ALU.mult))
                step(d.tensor_reduce(dst[:, :], rank[:, :, :], AX.X, ALU.add))
                d.tensor_copy(dsti[:, :], dst[:, :]).then_inc(dest_ready, 1)
                step(d.tensor_scalar(cmp[:, :], bend[:, :], iop[:, :], None, ALU.is_le))
                step(d.tensor_reduce(gcol[:, :], cmp[:, :], AX.X, ALU.add))
                d.tensor_scalar(gcol[:, :], gcol[:, :], float(GRP - 1), None, ALU.min).then_inc(gcol_ready, 1)
                v.wait_ge(gid_row, 1)
                d.tensor_copy(gid[:, :], tot_b[0][0:1, 0:P]).then_inc(gid_ready, 1)

    ROWS, RING, LOOKAHEAD = 8, 4, 6
    PAIRS, TURN = NBLK // 2, ROWS // 2
    TURNS, PEELED = NBLK // ROWS, 2
    rows = sb("rows", [P, ROWS, ROW])
    ids = sb("ids", [P, 2 * ROWS], I32)
    xs = sb("xs", [P, RING, UNITS, C])
    xsT = sb("xsT", [P, RING, KT, P])
    w_cur = sb("w_cur", [P, RING, KT, C])
    oT = sb("oT", [P, 2, P])
    orow = sb("orow", [P, ROWS, C])
    turned = [[ctx.enter_context(nc.psum_tensor(f"turned{i}{n}", [P, 512], F32)) for n in "ab"] for i in range(2)]
    ob = [ctx.enter_context(nc.psum_tensor(f"mixed_bank{i}", [P, 512], F32)) for i in range(2)]
    rb = [ctx.enter_context(nc.psum_tensor(f"back_bank{i}", [P, 512], F32)) for i in range(2)]
    scaled, turned_a, turned_b, kept_a, kept_b, w_kept, mixed, mixed_kept, back, back_kept, ids_kept = (sem("m_" + n) for n in
        "scaled turned_a turned_b kept_a kept_b w_kept mixed mixed_kept back back_kept ids_kept".split())
    rows_in = [sem(f"m_rows_in{i}") for i in range(ROWS)]
    written = [sem(f"m_written{i}") for i in range(ROWS)]
    rows_v = rows_d.rearrange("(n p) c -> n p c", p=P)
    block = ctx.enter_context(nc.Block())

    def due(n):
        return not isinstance(n, int) or n > 0

    def there(m):
        return not isinstance(m, int) or 0 <= m < PAIRS

    def steps_of(eng, step, skew):
        for m in range(PEELED * TURN):
            step(m // TURN, m % TURN)
        with eng.Fori(PEELED, TURNS) as k:
            for j in range(TURN):
                step(k, j)
        for m in range(PAIRS, PAIRS + skew):
            step(m // TURN, m % TURN)

    @block.sync
    def _(sp):
        def load(k, i):
            b = ROWS * k + i
            if due(b - ROWS + 1):
                sp.wait_ge(scaled, b - ROWS + 1)
                sp.wait_ge(turned_b, b - ROWS + 1)
                sp.wait_ge(ids_kept, b - ROWS + 1)
            src = rows_v[b, :, :] if isinstance(b, int) else rows_v[bass.ds(b, 1), :, :].rearrange("o p c -> (o p) c")
            sp.dma_start(rows[:, i, :], src).then_inc(rows_in[i], 16)
        for i in range(ROWS):
            load(0, i)
        with sp.Fori(1, TURNS) as k:
            for i in range(ROWS):
                load(k, i)

    @block.vector
    def _(v):
        d = nc.vector

        def step(k, j):
            m = TURN * k + j
            for h in range(2):
                if there(m):
                    b, i = 2 * m + h, 2 * j + h
                    v.wait_ge(rows_in[i], 16 * (k + 1))
                    if due(b - RING + 1):
                        v.wait_ge(turned_a, b - RING + 1)
                        v.wait_ge(turned_b, b - RING + 1)
                    d.tensor_tensor(xs[:, i % RING, :, :], rows[:, i, X0:X0 + C].rearrange("p (o c) -> p o c", o=1).broadcast_to([P, UNITS, C]),
                                    rows[:, i, P0:P0 + UNITS].rearrange("p (u o) -> p u o", o=1).broadcast_to([P, UNITS, C]), ALU.mult).then_inc(scaled, 1)
                if there(m - 1):
                    b, i = 2 * m - 2 + h, (2 * j - 2 + h) % ROWS
                    v.wait_ge(turned_b, b + 1)
                    if due(m - 2):
                        v.wait_ge(mixed, m - 2)
                    d.tensor_copy(xsT[:, i % RING, 4:KT, :], turned[h][1][:, 0:3 * P].rearrange("p (u n) -> p u n", u=3)).then_inc(kept_b, 1)
            if there(m - 2):
                v.wait_ge(mixed, m - 1)
                if due(m - 3):
                    v.wait_ge(back, m - 3)
                d.tensor_copy(oT[:, j % 2, :], ob[j % 2][:, 0:P]).then_inc(mixed_kept, 1)
        steps_of(v, step, 2)

    @block.scalar
    def _(act):
        a = nc.scalar

        def step(k, j):
            m = TURN * k + j
            for h in range(2):
                if there(m):
                    b, i = 2 * m + h, 2 * j + h
                    g = act.value_load(gid[0:1, b:b + 1] if isinstance(b, int) else gid[0:1, bass.ds(b, 1)], min_val=0, max_val=GRP - 1)
                    if due(m - 1):
                        act.wait_ge(mixed, m - 1)
                    a.activation(w_cur[:, i % RING, :, :], wt[:, bass.ds(g, 1), :, :].rearrange("p o k c -> p (o k) c"), ACT.Copy).then_inc(w_kept, 1)
                    act.wait_ge(turned_a, b + 1)
                    a.activation(xsT[:, i % RING, 0:4, :], turned[h][0][:, :].rearrange("p (u n) -> p u n", u=4), ACT.Copy).then_inc(kept_a, 1)
            if there(m - 2):
                i = (2 * j - 4) % ROWS
                act.wait_ge(back, m - 1)
                q = k if j >= 2 else k - 1
                if due(q):
                    act.wait_ge(written[i], 16 * q)
                    act.wait_ge(written[i + 1], 16 * q)
                a.activation(orow[:, i:i + 2, :], rb[j % 2][:, 0:P].rearrange("p (b c) -> p b c", b=2), ACT.Copy).then_inc(back_kept, 1)
        steps_of(act, step, 2)

    @block.tensor
    def _(pe):
        mm = nc.tensor.matmul

        def step(k, j):
            m = TURN * k + j
            for h in range(2):
                if there(m):
                    b, i = 2 * m + h, 2 * j + h
                    pe.wait_ge(scaled, b + 1)
                    if due(b - 1):
                        pe.wait_ge(kept_a, b - 1)
                    for u in range(4):
                        t = nc.tensor.transpose(turned[h][0][:, P * u:P * u + P], xs[:, i % RING, 2 * u:2 * u + 2, :].rearrange("p a c -> p (a c)"), ident[:, :])
                    t.then_inc(turned_a, 1)
                    if due(b - 1):
                        pe.wait_ge(kept_b, b - 1)
                    for u in range(2):
                        nc.tensor.transpose(turned[h][1][:, P * u:P * u + P], xs[:, i % RING, 8 + 2 * u:10 + 2 * u, :].rearrange("p a c -> p (a c)"), ident[:, :])
                    pe.wait_ge(rows_in[i], 16 * (k + 1))
                    nc.tensor.transpose(turned[h][1][:, 2 * P:3 * P], rows[:, i, 16:ROW], ident[:, :]).then_inc(turned_b, 1)
            if there(m - 1):
                i = (2 * j - 2) % RING
                pe.wait_ge(kept_a, 2 * m)
                pe.wait_ge(kept_b, 2 * m)
                pe.wait_ge(w_kept, 2 * m)
                if due(m - 2):
                    pe.wait_ge(mixed_kept, m - 2)
                for u in range(KT):
                    for h in range(2):
                        t = mm(ob[(j + 1) % 2][C * h:C * h + C, 0:P], w_cur[:, i + h, u, :], xsT[:, i + h, u, :], start=u == 0, stop=u == KT - 1)
                t.then_inc(mixed, 1)
            if there(m - 2):
                pe.wait_ge(mixed_kept, m - 1)
                if due(m - 3):
                    pe.wait_ge(back_kept, m - 3)
                nc.tensor.transpose(rb[j % 2][:, 0:P], oT[:, j % 2, :], ident[:, :]).then_inc(back, 1)
        steps_of(pe, step, 2)

    @block.gpsimd
    def _(pool):
        def take_ids(b):
            pool.wait_ge(rows_in[b % ROWS], 16 * (b // ROWS + 1))
            if b >= 2 * ROWS:
                pool.wait_ge(written[b % ROWS], 16 * (b // ROWS - 1))
            nc.gpsimd.tensor_copy(ids[:, b % (2 * ROWS):b % (2 * ROWS) + 1], rows[:, b % ROWS, ID0:ID0 + 1].bitcast(I32)).then_inc(ids_kept, 1)
        for b in range(LOOKAHEAD):
            take_ids(b)
        for b in range(NBLK):
            if b + LOOKAHEAD < NBLK:
                take_ids(b + LOOKAHEAD)
            pool.wait_ge(ids_kept, b + 1)
            pool.wait_ge(back_kept, b // 2 + 1)
            nc.gpsimd.indirect_dma_start(out_d, bass.IndirectOffsetOnAxis(ap=ids[:, b % (2 * ROWS):b % (2 * ROWS) + 1], axis=0), orow[:, b % ROWS, :], None,
                                         bounds_check=TOKENS - 1, oob_is_err=False).then_inc(written[b % ROWS], 16)
        for i in range(ROWS):
            pool.wait_ge(written[i], 16 * TURNS)


def program(nc, A, out):
    rows_d = nc.dram_tensor("rows_sorted", (NBLK * BLK, ROW), F32, kind="Internal").ap()
    with ExitStack() as top:
        h1 = top.enter_context(nc.sbuf_tensor("h1", [P, TILES * TOK], F32))
        with ExitStack() as ctx:
            tokenizer(nc, ctx, A, h1)
        pay = top.enter_context(nc.sbuf_tensor("pay", [P, NT, ROW], F32))
        grp = top.enter_context(nc.sbuf_tensor("grp", [P, NT], F32))
        with ExitStack() as logits:
            lg = logits.enter_context(nc.sbuf_tensor("lg", [P, NT, 256], F32))
            with ExitStack() as ctx:
                scan_and_logits(nc, ctx, A, h1, pay, lg)
            with ExitStack() as ctx:
                paths(nc, ctx, pay, lg, grp)
        with ExitStack() as ctx:
            sort_and_mix(nc, ctx, A, pay, grp, rows_d, out)


def preorder(node=0, level=0):
    if level == LEVELS - 1:
        return [node]
    return [node] + preorder(2 * node + 1, level + 1) + preorder(2 * node + 2, level + 1)


_INS = ["x"] + ["L0_tok_" + n for n in ("ln_q_w", "ln_q_b", "ln_kv_w", "ln_kv_b", "proj_b")] + \
       ["L0_attn_" + n for n in ("Wx", "bx", "Wbc", "bbc", "Wd", "bd", "Wy", "by")] + ["L0_ffn_b2s"]


def kernel(**inputs):
    import concourse.bacc as bacc
    from concourse.bass_utils import run_bass_kernel_spmd

    arrays = {n: np.ascontiguousarray(inputs[n]) for n in _INS}
    order = preorder()
    arrays["WqT"] = np.ascontiguousarray(np.asarray(inputs["L0_tok_Wq"]).T)
    arrays["WkvT"] = np.ascontiguousarray(np.asarray(inputs["L0_tok_Wkv"]).T)
    arrays["projT"] = np.ascontiguousarray(np.asarray(inputs["L0_tok_proj_w"]).T)
    arrays["w1T"] = np.ascontiguousarray(np.asarray(inputs["L0_ffn_w1s"])[order].T)
    arrays["b1r"] = np.ascontiguousarray(np.asarray(inputs["L0_ffn_b1s"])[order].reshape(1, NODES))
    arrays["w2T"] = np.ascontiguousarray(np.asarray(inputs["L0_ffn_w2s"]).transpose(1, 0, 2))

    nc = bacc.Bacc("TRN2", target_bir_lowering=False, num_devices=1)
    A = {n: nc.dram_tensor("in_" + n, a.shape, mybir.dt.from_np(a.dtype), kind="ExternalInput").ap() for n, a in arrays.items()}
    out = nc.dram_tensor("out", (TOKENS, C), F32, kind="ExternalOutput").ap()
    program(nc, A, out)
    r = run_bass_kernel_spmd(nc, [{"in_" + n: a for n, a in arrays.items()}], core_ids=[0])
    return r.results[0]["out"].reshape(B, TOK, C)
```

```python
import numpy as np
import concourse.bass as bass
from concourse import mybir
from contextlib import ExitStack

F32 = mybir.dt.float32
F32R = mybir.dt.float32r
ALU = mybir.AluOpType
ACT = mybir.ActivationFunctionType
AX = mybir.AxisListType

P = 128
B, C, HW = 32, 64, 64
S = 4
TH = HW // S
TOK = TH * TH
NP = S * S
HEADS = 8
HD = C // HEADS
PIX = HW * HW
TILES = B // 2
CH = 512
NCH = PIX // CH
ORDER = [0, 2, 4, 6, 1, 3, 5, 7]
EPS = 1e-5


def tokenizer(nc, ctx, A, h1):
    def sb(name, shape, dt=F32):
        return ctx.enter_context(nc.sbuf_tensor(name, shape, dt))

    def bank(name):
        return ctx.enter_context(nc.psum_tensor(name, [P, CH], F32))

    def sem(name):
        return ctx.enter_context(nc.semaphore(name))

    x_v = A["x"].rearrange("(t b) c h w -> t (b c) (h w)", b=2)

    x = sb("x_px", [P, 2, PIX])
    x_hi = sb("x_hi", [P, 2, PIX], F32R)
    x_lo = sb("x_lo", [P, 2, PIX], F32R)
    x_sq = sb("x_sq", [P, NCH // 2, CH])
    v_sb = sb("v_sb", [P, NCH, CH])
    qk = sb("qk", [P, NCH, CH])
    va = sb("va", [P, NCH, CH])
    pre1 = sb("pre1", [P, 1024])
    pre2 = sb("pre2", [P, TH, HW])
    rkv = sb("rkv", [P, CH])
    sc = sb("sc", [P, CH])
    ex = sb("ex", [P, CH])
    a_hi = sb("a_hi", [P, CH], F32R)
    a_lo = sb("a_lo", [P, CH], F32R)
    mx = sb("mx", [P, 2 * TH])
    sm = sb("sm", [P, 2 * TH])
    rc = sb("rc", [P, 2 * TH])
    px_sum = sb("px_sum", [P, TOK])
    q4 = sb("q4", [P, TH, HW])
    rs2 = sb("rs2", [P, 2 * TOK])
    rq = sb("rq", [P, TOK])
    qs = sb("qs", [P, TOK])
    w_ld = sb("w_ld", [P, 4, P])
    w_sc = sb("w_sc", [P, 3, P])
    w_hi = sb("w_hi", [P, 2, P], F32R)
    w_lo = sb("w_lo", [P, 2, P], F32R)
    gq = sb("gq", [P, P])
    vec = sb("vec", [P, 8])
    avg = sb("avg", [P, P])
    cen = sb("cen", [P, P])
    sel = sb("sel", [P, 2, 32])
    msel = sb("msel", [P, 2, 32])
    e_f = va[:, 0:2, :].rearrange("p a (b m) -> p (a b) m", m=P)
    e_r = sb("e_r", [P, NCH, P], F32R)
    eps = sb("eps", [P, 1])

    b_k = [bank(f"b_k{i}") for i in range(2)]
    b_w = [bank(f"b_w{i}") for i in range(2)]
    b_s, b_m, b_q, b_b = bank("b_s"), bank("b_m"), bank("b_q"), bank("b_b")

    x_in = [sem("x_in0"), sem("x_in1")]

    LOADS, CENTRED, MASKS = 16 * 4, 8, 32
    with ExitStack() as wctx:
        wsem = lambda n: wctx.enter_context(nc.semaphore(n))
        zeroed, loaded, masks, scaled, prod, folded = (wsem(n) for n in
            ("w_zeroed", "w_loaded", "w_masks", "w_scaled", "w_prod", "w_folded"))
        with nc.Block() as block:
            @block.sync
            def _(sp):
                for b in range(2):
                    sp.dma_start(vec[C * b:C * b + C, 0:5], A["tok_vectors"]).then_inc(loaded, 16)
                sp.wait_ge(zeroed, 1)
                for b in range(2):
                    s = slice(C * b, C * b + C)
                    sp.dma_start(w_ld[s, :, s], A["tok_weights"].rearrange("c (k d) -> c k d", k=4)).then_inc(loaded, 16)
                for t in range(2):
                    sp.dma_start(x[:, t, :], x_v[t, :, :]).then_inc(x_in[t], 16)
                sp.wait_ge(loaded, LOADS)

            @block.gpsimd
            def _(pool):
                g = nc.gpsimd
                n = [0]

                def step(ins):
                    ins.then_inc(masks, 1)
                    n[0] += 1
                    pool.wait_ge(masks, n[0])

                def band(view, fill_outside, lo_base, lo_pat, lo_mul, hi_base, hi_pat, hi_mul):
                    step(g.affine_select(out=view, in_=view, compare_op=ALU.is_ge, fill=fill_outside, base=lo_base,
                                         pattern=lo_pat, channel_multiplier=lo_mul))
                    step(g.affine_select(out=view, in_=view, compare_op=ALU.is_ge, fill=fill_outside, base=hi_base,
                                         pattern=hi_pat, channel_multiplier=hi_mul))

                step(g.memset(avg[:, :], 1.0 / C))
                for m in range(2):
                    v = avg[:, C * m:C * m + C]
                    band(v, 0.0, -C * m, [[0, C]], 1, C * m + C - 1, [[0, C]], -1)
                step(g.memset(cen[:, :], 0.0))
                step(g.affine_select(out=cen[:, :], in_=cen[:, :], compare_op=ALU.not_equal, fill=1.0, base=0,
                                     pattern=[[-1, P]], channel_multiplier=1))
                step(g.tensor_tensor(cen[:, :], cen[:, :], avg[:, :], ALU.subtract))
                step(g.memset(sel[:, :, :], 0.0))
                for e in range(2):
                    v = sel[:, e, 16 * e:16 * e + 16]
                    step(g.memset(v, 1.0))
                    band(v, 0.0, 0, [[-HD, 16]], 1, HD - 1, [[HD, 16]], -1)
                step(g.memset(msel[:, :, :], 0.0))
                for e in range(2):
                    for b in range(2):
                        v = msel[:, e, 16 * e + 8 * b:16 * e + 8 * b + 8]
                        step(g.memset(v, 1.0 / C))
                        band(v, 0.0, -C * b, [[0, 8]], 1, C * b + C - 1, [[0, 8]], -1)
                step(g.memset(e_f[:, :, :], 1.0))
                band(e_f[:, :, :], 0.0, 0, [[16 * HD, NCH], [1, P]], -HD, HD - 1, [[-16 * HD, NCH], [-1, P]], HD)
                step(g.memset(eps[:, :], EPS))

            @block.vector
            def _(v):
                nc.vector.memset(w_ld[:, :, :], 0.0).then_inc(zeroed, 1)
                v.wait_ge(loaded, LOADS)
                v.wait_ge(masks, CENTRED)
                for i, w in ((0, 0), (1, 2), (2, 2)):
                    nc.vector.tensor_scalar(w_sc[:, i, :], w_ld[:, i, :], vec[:, w:w + 1], None, ALU.mult).then_inc(scaled, 1)
                v.wait_ge(prod, 1)
                for i in range(2):
                    nc.vector.tensor_copy(w_hi[:, i, :], b_k[0][:, P * (i + 1):P * (i + 2)]).then_inc(folded, 1)
                nc.vector.tensor_scalar(gq[:, :], b_k[0][:, 0:P], C ** -0.5, None, ALU.mult).then_inc(folded, 1)
                nc.vector.tensor_scalar(vec[:, 5:6], b_k[1][:, 0:1], C ** -0.5, None, ALU.mult).then_inc(folded, 1)
                nc.vector.tensor_copy(vec[:, 6:7], b_k[1][:, 1:2]).then_inc(folded, 1)
                v.wait_ge(folded, 5)
                for i in range(2):
                    nc.vector.tensor_tensor(w_lo[:, i, :], b_k[0][:, P * (i + 1):P * (i + 2)], w_hi[:, i, :].bitcast(F32),
                                            ALU.subtract).then_inc(folded, 1)
                v.wait_ge(prod, 2)
                nc.vector.tensor_tensor(vec[:, 7:8], b_w[0][:, 0:1], vec[:, 4:5], ALU.add).then_inc(folded, 1)
                v.wait_ge(masks, MASKS)
                nc.vector.tensor_copy(e_r[:, :, :], e_f[:, :, :]).then_inc(folded, 1)

            @block.tensor
            def _(pe):
                pe.wait_ge(scaled, 3)
                pe.wait_ge(masks, CENTRED)
                for i in range(3):
                    nc.tensor.matmul(b_k[0][:, P * i:P * (i + 1)], cen[:, :], w_sc[:, i, :], start=True, stop=True)
                nc.tensor.matmul(b_k[1][:, 0:1], w_ld[:, 0, :], vec[:, 1:2], start=True, stop=True)
                nc.tensor.matmul(b_k[1][:, 1:2], w_ld[:, 2, :], vec[:, 3:4], start=True, stop=True).then_inc(prod, 1)
                pe.wait_ge(folded, 7)
                nc.tensor.matmul(b_w[0][:, 0:1], w_ld[:, 3, :], vec[:, 6:7], start=True, stop=True).then_inc(prod, 1)

    names = (
        "split_hi split_lo squared pooled pooled_copied pooled_squared pooled_biased q_moments q_mean_sq q_var q_ln "
        "q_rstd q_product q_scaled q_ready moments square_sums kv_mean_sq kv_var kv_clamped kv_ln kv_rstd k_product "
        "qk_ready scores scores_scaled scores_max scores_shifted exps exp_sum exp_recip exps_scaled weights weights_hi "
        "weights_lo a_spread va_ready v_product v_copied halved quartered attn_out h1_ready")
    done = {n: sem(n) for n in names.split()}

    def tile(k, o):
        return 2 * k + o, o % 2

    block = ctx.enter_context(nc.Block())

    STEADY = (TILES - 2) // 2


    @block.sync
    def _(sp):
        def load(k, o):
            t, par = tile(k, o)
            sp.dma_start(x[:, par, :], x_v[t, :, :] if isinstance(t, int) else x_v[bass.ds(t, 1), :, :].rearrange("o p n -> (o p) n")).then_inc(x_in[par], 16)

        def reload(k, o):
            t, par = tile(k, o)
            sp.wait_ge(done["split_lo"], 2 * t - 2)
            sp.wait_ge(done["pooled"], 2 * t - 2)
            sp.wait_ge(done["square_sums"], 2 * t - 2)
            load(k, o)

        with sp.Fori(1, STEADY + 1) as k:
            reload(k, 0)
            reload(k, 1)

    @block.scalar
    def _(act):
        a = nc.scalar

        def split(k, o, half):
            t, par = tile(k, o)
            s = slice(half * PIX // 2, (half + 1) * PIX // 2)
            a.activation(x_hi[:, par, s], x[:, par, s], ACT.Copy).then_inc(done["split_hi"], 1)

        def square(k, o, half, part, first=False):
            t, par = tile(k, o)
            if part == 0 and not (first and half == 0):
                act.wait_ge(done["square_sums"], 2 * t + half)
            src = x[:, par, :].rearrange("p (j e n) -> p j e n", e=2, n=CH)[:, 2 * part:2 * part + 2, half, :]
            a.activation(x_sq[:, 2 * part:2 * part + 2, :], src, ACT.Square).then_inc(done["squared"], 1)

        def q_front(k, o):
            t, par = tile(k, o)
            act.wait_ge(done["pooled"], 2 * t + 2)
            src = px_sum[:, :]
            a.activation(rs2[:, 0:TOK], src, ACT.Copy, scale=1.0 / NP).then_inc(done["pooled_copied"], 1)
            a.activation(rs2[:, TOK:2 * TOK], src, ACT.Square, scale=1.0 / NP).then_inc(done["pooled_squared"], 1)
            a.activation(h1[:, bass.ts(t, TOK)], src, ACT.Identity, scale=1.0 / NP, bias=vec[:, 7:8]).then_inc(done["pooled_biased"], 1)

        def q_moment(k, o):
            t, par = tile(k, o)
            act.wait_ge(done["q_moments"], t + 1)
            a.activation(rq[:, :], b_b[:, 0:TOK], ACT.Square).then_inc(done["q_mean_sq"], 1)

        def q_back(k, o):
            t, par = tile(k, o)
            act.wait_ge(done["q_var"], t + 1)
            a.activation(rq[:, :], rq[:, :], ACT.Ln, bias=eps[:, :]).then_inc(done["q_ln"], 1)
            act.wait_ge(done["q_ln"], t + 1)
            a.activation(rq[:, :], rq[:, :], ACT.Exp, scale=-0.5).then_inc(done["q_rstd"], 1)

        def q_final(k, o):
            t, par = tile(k, o)
            act.wait_ge(done["q_scaled"], t + 1)
            a.activation(q4[:, :, :].rearrange("p h (w s) -> p (h w) s", s=S),
                         qs[:, :].rearrange("p (n s) -> p n s", s=1).broadcast_to([P, TOK, S]),
                         ACT.Identity, bias=vec[:, 5:6]).then_inc(done["q_ready"], 1)

        def kv_mean(k, o):
            t, par = tile(k, o)
            act.wait_ge(done["moments"], t + 1)
            a.activation(rkv[:, :], b_m[:, :], ACT.Square).then_inc(done["kv_mean_sq"], 1)

        def kv_rstd(k, o):
            t, par = tile(k, o)
            act.wait_ge(done["kv_var"], t + 1)
            a.activation(rkv[:, :], rkv[:, :], ACT.Relu).then_inc(done["kv_clamped"], 1)
            act.wait_ge(done["kv_clamped"], t + 1)
            a.activation(rkv[:, :], rkv[:, :], ACT.Ln, bias=eps[:, :]).then_inc(done["kv_ln"], 1)
            act.wait_ge(done["kv_ln"], t + 1)
            a.activation(rkv[:, :], rkv[:, :], ACT.Exp, scale=-0.5).then_inc(done["kv_rstd"], 1)

        def copy_v(k, o, n):
            t, par = tile(k, o)
            act.wait_ge(done["v_product"], NCH * t + n + 1)
            a.activation(v_sb[:, n, :], b_w[n % 2][:, :], ACT.Copy).then_inc(done["v_copied"], 1)

        def softmax_exp(k, o):
            t, par = tile(k, o)
            act.wait_ge(done["scores_shifted"], 2 * t + 2)
            a.activation(ex[:, :], sc[:, :], ACT.Exp).then_inc(done["exps"], 1)

        def prepare(k, o, first=False):
            t, par = tile(k, o)
            act.wait_ge(x_in[par], 16 * (k + o // 2 + 1))
            if not (first or isinstance(t, int) and t < 2):
                act.wait_ge(done["v_product"], NCH * (t - 1))
            split(k, o, 0)
            split(k, o, 1)

        def step(k, o, last=False):
            if not last:
                prepare(k, o + 1)
            kv_mean(k, o)
            if not last:
                square(k, o + 1, 0, 0)
                square(k, o + 1, 0, 1)
            kv_rstd(k, o)
            copy_v(k, o, 0)
            copy_v(k, o, 1)
            if not last:
                q_front(k, o + 1)
            copy_v(k, o, 2)
            copy_v(k, o, 3)
            if not last:
                q_moment(k, o + 1)
            softmax_exp(k, o)
            copy_v(k, o, 4)
            copy_v(k, o, 5)
            if not last:
                q_back(k, o + 1)
            if not last:
                square(k, o + 1, 1, 0)
            copy_v(k, o, 6)
            if not last:
                q_final(k, o + 1)
            copy_v(k, o, 7)
            if not last:
                square(k, o + 1, 1, 1)

        act.preload_act_table_set("natural_log_exp_and_others")
        prepare(0, 0, first=True)
        q_front(0, 0)
        for part in range(2):
            square(0, 0, 0, part, first=True)
        q_moment(0, 0)
        q_back(0, 0)
        q_final(0, 0)
        for part in range(2):
            square(0, 0, 1, part)
        step(0, 0)
        with act.Fori(0, STEADY) as k:
            step(k, 1)
            step(k, 2)
        step(STEADY, 1, last=True)

    @block.gpsimd
    def _(pool):
        g = nc.gpsimd

        def split(k, o, half, first=False):
            t, par = tile(k, o)
            s = slice(half * PIX // 2, (half + 1) * PIX // 2)
            if half == 0 and not first:
                pool.wait_ge(done["v_product"], NCH * (t - 1))
            pool.wait_ge(done["split_hi"], 2 * t + half + 1)
            g.tensor_tensor(x_lo[:, par, s], x[:, par, s], x_hi[:, par, s].bitcast(F32), ALU.subtract).then_inc(done["split_lo"], 1)

        def fold(k, o, half, first=False):
            t, par = tile(k, o)
            pool.wait_ge(done["va_ready"], NCH * t + 4 * half + 4)
            v = va[:, 4 * half:4 * half + 4, :].rearrange("p j (h s w) -> p (j h) s w", s=S, w=HW)
            p1 = pre1[:, :].rearrange("p (g s w) -> p g s w", s=2, w=HW)
            if not (first and half == 0):
                pool.wait_ge(done["quartered"], 2 * t + half)
            g.tensor_tensor(p1, v[:, :, 0:2, :], v[:, :, 2:4, :], ALU.add).then_inc(done["halved"], 1)
            pool.wait_ge(done["halved"], 2 * t + half + 1)
            if half == 0 and not first:
                pool.wait_ge(done["attn_out"], t)
            dst = pre2[:, :, :].rearrange("p (j e h) w -> p j e h w", e=2, h=2)[:, :, half, :, :]
            p1 = pre1[:, :].rearrange("p (j h s w) -> p j h s w", h=2, s=2, w=HW)
            g.tensor_tensor(dst, p1[:, :, :, 0, :], p1[:, :, :, 1, :], ALU.add).then_inc(done["quartered"], 1)

        def step(k, o, first=False, last=False):
            if not last:
                split(k, o + 1, 0, first=first)
            if not first:
                fold(k, o - 1, 0, first=isinstance(k, int) and 2 * k + o == 1)
                fold(k, o - 1, 1)
            if not last:
                split(k, o + 1, 1)

        split(0, 0, 0, first=True)
        split(0, 0, 1)
        step(0, 0, first=True)
        step(0, 1)
        with pool.Fori(1, STEADY) as k:
            step(k, 0)
            step(k, 1)
        step(STEADY, 0)
        step(STEADY, 1, last=True)
        fold(STEADY, 1, 0)
        fold(STEADY, 1, 1)

    @block.vector
    def _(v):
        d = nc.vector

        def pool_px(k, o, half):
            t, par = tile(k, o)
            if half == 0:
                v.wait_ge(x_in[par], 16 * (k + o // 2 + 1))
                if not (isinstance(t, int) and t == 0):
                    v.wait_ge(done["pooled_biased"], t)
            d.tensor_reduce(px_sum[:, half * TOK // 2:(half + 1) * TOK // 2].rearrange("p (h w) -> p h w", w=TH),
                            x[:, par, half * PIX // 2:(half + 1) * PIX // 2].rearrange("p (h s w u) -> p h w s u", h=TH // 2, s=S, u=S),
                            AX.XY, ALU.add).then_inc(done["pooled"], 1)

        def qk_mul(k, o, n):
            t, par = tile(k, o)
            j = ORDER[n]
            if n == 0:
                v.wait_ge(done["q_ready"], t + 1)
            v.wait_ge(done["k_product"], NCH * t + n + 1)
            if n % 4 == 0 and not (isinstance(t, int) and t == 0):
                v.wait_ge(done["scores"], 2 * t + n // 4 - 1)
            d.tensor_tensor(qk[:, n, :].rearrange("p (h s w) -> p h s w", s=S, w=HW),
                            b_k[n % 2][:, :].rearrange("p (h s w) -> p h s w", s=S, w=HW),
                            q4[:, 2 * j:2 * j + 2, :].rearrange("p h (o w) -> p h o w", o=1).broadcast_to([P, 2, S, HW]),
                            ALU.mult).then_inc(done["qk_ready"], 1)

        def va_mul(k, o, n):
            t, par = tile(k, o)
            v.wait_ge(done["a_spread"], NCH * t + n + 1)
            if n == 0:
                v.wait_ge(done["v_copied"], NCH * (t + 1))
            if n % 4 == 0 and not (isinstance(t, int) and t == 0):
                v.wait_ge(done["halved"], 2 * t - 1 + n // 4)
            d.tensor_tensor(va[:, n, :], b_w[n % 2][:, :], v_sb[:, n, :], ALU.mult).then_inc(done["va_ready"], 1)

        def kv_var(k, o):
            t, par = tile(k, o)
            v.wait_ge(done["kv_mean_sq"], t + 1)
            v.wait_ge(done["square_sums"], 2 * t + 2)
            d.tensor_tensor(rkv[:, :], b_q[:, :], rkv[:, :], ALU.subtract).then_inc(done["kv_var"], 1)

        hs = lambda a, h: a[:, 256 * h:256 * h + 256].rearrange("p (s w u) -> p s w u", s=S, u=S)
        hb = lambda a, h: a[:, TH * h:TH * h + TH].rearrange("p (a w u) -> p a w u", a=1, u=1).broadcast_to([P, S, TH, S])

        def softmax_a(k, o):
            t, par = tile(k, o)
            v.wait_ge(done["scores"], 2 * t + 2)
            v.wait_ge(done["kv_rstd"], t + 1)
            d.tensor_tensor(sc[:, :], b_s[:, :], rkv[:, :], ALU.mult).then_inc(done["scores_scaled"], 1)
            v.wait_ge(done["scores_scaled"], t + 1)
            d.tensor_reduce(mx[:, :].rearrange("p (h w) -> p h w", w=TH),
                            sc[:, :].rearrange("p (h s w u) -> p h w s u", h=2, s=S, u=S), AX.XY, ALU.max).then_inc(done["scores_max"], 1)
            v.wait_ge(done["scores_max"], t + 1)
            for h in range(2):
                d.tensor_tensor(hs(sc, h), hs(sc, h), hb(mx, h), ALU.subtract).then_inc(done["scores_shifted"], 1)

        def softmax_b(k, o, first=False, last=False):
            t, par = tile(k, o)
            v.wait_ge(done["exps"], t + 1)
            d.tensor_reduce(sm[:, :].rearrange("p (h w) -> p h w", w=TH),
                            ex[:, :].rearrange("p (h s w u) -> p h w s u", h=2, s=S, u=S), AX.XY, ALU.add).then_inc(done["exp_sum"], 1)
            v.wait_ge(done["exp_sum"], t + 1)
            d.reciprocal(rc[:, :], sm[:, :]).then_inc(done["exp_recip"], 1)
            d.tensor_tensor(ex[:, :], ex[:, :], rkv[:, :], ALU.mult).then_inc(done["exps_scaled"], 1)
            if not last:
                q_scale(k, o + 1)
            v.wait_ge(done["exps_scaled"], t + 1)
            v.wait_ge(done["exp_recip"], t + 1)
            for h in range(2):
                d.tensor_tensor(hs(ex, h), hs(ex, h), hb(rc, h), ALU.mult).then_inc(done["weights"], 1)
            v.wait_ge(done["weights"], 2 * t + 2)
            if not first:
                v.wait_ge(done["a_spread"], NCH * t)
            d.tensor_copy(a_hi[:, :], ex[:, :]).then_inc(done["weights_hi"], 1)
            v.wait_ge(done["weights_hi"], t + 1)
            d.tensor_tensor(a_lo[:, :], ex[:, :], a_hi[:, :].bitcast(F32), ALU.subtract).then_inc(done["weights_lo"], 1)

        def q_var(k, o):
            t, par = tile(k, o)
            v.wait_ge(done["q_mean_sq"], t + 1)
            d.scalar_tensor_tensor(rq[:, :], rq[:, :], -1.0, b_b[:, TOK:2 * TOK], ALU.mult, ALU.add).then_inc(done["q_var"], 1)

        def q_scale(k, o):
            t, par = tile(k, o)
            v.wait_ge(done["q_rstd"], t + 1)
            v.wait_ge(done["q_product"], t + 1)
            d.tensor_tensor(qs[:, :], b_b[:, 0:TOK], rq[:, :], ALU.mult).then_inc(done["q_scaled"], 1)

        def finish(k, o):
            t, par = tile(k, o)
            v.wait_ge(done["attn_out"], t + 1)
            v.wait_ge(done["pooled_biased"], t + 1)
            dst = h1[:, bass.ts(t, TOK)]
            d.tensor_tensor(dst, b_b[:, 0:TOK], dst, ALU.add).then_inc(done["h1_ready"], 1)

        def step(k, o, first=False, last=False):
            for n in range(NCH):
                qk_mul(k, o, n)
                if n == 1 and not last:
                    pool_px(k, o + 1, 0)
                if not first:
                    va_mul(k, o - 1, n)
                if n == 4:
                    kv_var(k, o)
                if n == 6 and not (isinstance(k, int) and 2 * k + o < 2):
                    finish(k, o - 2)
            if not last:
                pool_px(k, o + 1, 1)
            softmax_a(k, o)
            if not last:
                q_var(k, o + 1)
            softmax_b(k, o, first=first, last=last)

        pool_px(0, 0, 0)
        pool_px(0, 0, 1)
        q_var(0, 0)
        q_scale(0, 0)
        step(0, 0, first=True)
        step(0, 1)
        step(0, 2)
        with v.Fori(1, STEADY) as k:
            step(k, 1)
            step(k, 2)
        step(STEADY, 1, last=True)
        for n in range(NCH):
            va_mul(STEADY, 1, n)
            if n == 4:
                finish(STEADY, 0)
        finish(STEADY, 1)

    @block.tensor
    def _(pe):
        mm = nc.tensor.matmul

        def px(buf, par, j):
            return buf[:, par, CH * j:CH * j + CH]

        def three(dst, w, par, j):
            mm(dst, w_hi[:, w, :], px(x_hi, par, j), start=True, stop=False)
            mm(dst, w_lo[:, w, :], px(x_hi, par, j), start=False, stop=False)
            return mm(dst, w_hi[:, w, :], px(x_lo, par, j), start=False, stop=True)

        def k_mm(k, o, n):
            t, par = tile(k, o)
            if n == 0:
                pe.wait_ge(done["split_lo"], 2 * t + 2)
            if not (isinstance(t, int) and t == 0 and n < 2):
                pe.wait_ge(done["qk_ready"], NCH * t + n - 1)
            three(b_k[n % 2][:, :], 0, par, ORDER[n]).then_inc(done["k_product"], 1)

        def v_mm(k, o, n, first=False):
            t, par = tile(k, o)
            if n < 2:
                if not first:
                    pe.wait_ge(done["va_ready"], NCH * (t - 1) + 7 + n)
            else:
                pe.wait_ge(done["v_copied"], NCH * t + n - 1)
            three(b_w[n % 2][:, :], 1, par, ORDER[n]).then_inc(done["v_product"], 1)

        def spread(k, o, n):
            t, par = tile(k, o)
            if n == 0:
                pe.wait_ge(done["weights_lo"], t + 1)
            if n < 2:
                pe.wait_ge(done["v_copied"], NCH * t + 7 + n)
            else:
                pe.wait_ge(done["va_ready"], NCH * t + n - 1)
            mm(b_w[n % 2][:, :], e_r[:, ORDER[n], :], a_hi[:, :], start=True, stop=False)
            mm(b_w[n % 2][:, :], e_r[:, ORDER[n], :], a_lo[:, :], start=False, stop=True).then_inc(done["a_spread"], 1)

        def scores(k, o, e):
            t, par = tile(k, o)
            pe.wait_ge(done["qk_ready"], NCH * t + 4 * e + 4)
            if e == 0 and not (isinstance(t, int) and t == 0):
                pe.wait_ge(done["scores_scaled"], t)
            for c in range(4):
                i = mm(b_s[32 * c:32 * c + 32, :], sel[:, e, :], qk[:, 4 * e + c, :], start=e == 0, stop=e == 1)
            i.then_inc(done["scores"], 1)

        def sums(k, o, e):
            t, par = tile(k, o)
            pe.wait_ge(done["squared"], 4 * t + 2 * e + 2)
            if e == 0 and not (isinstance(t, int) and t == 0):
                pe.wait_ge(done["kv_var"], t)
            for c in range(4):
                i = mm(b_m[32 * c:32 * c + 32, :], msel[:, e, :], px(x, par, 2 * c + e), start=e == 0, stop=e == 1)
            if e == 1:
                i.then_inc(done["moments"], 1)
            for c in range(4):
                i = mm(b_q[32 * c:32 * c + 32, :], msel[:, e, :], x_sq[:, c, :], start=e == 0, stop=e == 1)
            i.then_inc(done["square_sums"], 1)

        def q_moments(k, o):
            t, par = tile(k, o)
            pe.wait_ge(done["pooled_squared"], t + 1)
            pe.wait_ge(done["pooled_copied"], t + 1)
            if not (isinstance(t, int) and t < 3):
                pe.wait_ge(done["h1_ready"], t - 2)
            if not (isinstance(t, int) and t == 0):
                pe.wait_ge(done["q_scaled"], t)
            mm(b_b[:, :], avg[:, :], rs2[:, :], start=True, stop=True).then_inc(done["q_moments"], 1)

        def q_mm(k, o):
            t, par = tile(k, o)
            pe.wait_ge(done["q_var"], t + 1)
            mm(b_b[:, 0:TOK], gq[:, :], rs2[:, 0:TOK], start=True, stop=True).then_inc(done["q_product"], 1)

        def out_mm(k, o, scaled):
            t, par = tile(k, o)
            pe.wait_ge(done["quartered"], 2 * t + 2)
            pe.wait_ge(done["q_scaled"], scaled)
            if not (isinstance(t, int) and t == 0):
                pe.wait_ge(done["h1_ready"], t)
            p2 = pre2[:, :, :].rearrange("p h (w u) -> p (h w) u", u=S)
            for u in range(S):
                i = mm(b_b[:, 0:TOK], w_ld[:, 3, :], p2[:, :, u], start=u == 0, stop=u == S - 1)
            i.then_inc(done["attn_out"], 1)

        def step(k, o, first=False, last=False):
            for n in range(NCH):
                if n == 5:
                    scores(k, o, 0)
                k_mm(k, o, n)
                if n == 1:
                    sums(k, o, 1)
                if not first:
                    spread(k, o - 1, n)
            if not last:
                sums(k, o + 1, 0)
            v_mm(k, o, 0, first=first)
            v_mm(k, o, 1, first=first)
            scores(k, o, 1)
            v_mm(k, o, 2)
            v_mm(k, o, 3)
            if not last:
                q_moments(k, o + 1)
            v_mm(k, o, 4)
            v_mm(k, o, 5)
            if not last:
                q_mm(k, o + 1)
            v_mm(k, o, 6)
            v_mm(k, o, 7)
            if not first:
                out_mm(k, o - 1, 2 * k + o + (1 if last else 2))

        q_moments(0, 0)
        sums(0, 0, 0)
        q_mm(0, 0)
        step(0, 0, first=True)
        step(0, 1)
        step(0, 2)
        with pe.Fori(1, STEADY) as k:
            step(k, 1)
            step(k, 2)
        step(STEADY, 1, last=True)
        for n in range(NCH):
            spread(STEADY, 1, n)
        out_mm(STEADY, 1, TILES)


U32 = mybir.dt.uint32
N_ST = 128
NODES = 255
LEVELS = 8
NT = TILES * 4
ROW = 144
UNITS = 12


def scan_and_logits(nc, ctx, A, h1, pay, lg):
    def sb(name, shape, dt=F32):
        return ctx.enter_context(nc.sbuf_tensor(name, shape, dt))

    def sem(name):
        return ctx.enter_context(nc.semaphore(name))

    w_p = sb("w_p", [P, 2, 4, N_ST])
    w_y = sb("w_y", [P, C])
    b_p = sb("b_p", [P, 5])
    w1 = sb("w1", [P, 2, 256])
    b1 = sb("b1", [P, 256])
    avg = sb("avg2", [P, P])
    ident = sb("ident", [P, P])
    eps = sb("eps2", [P, 1])
    xc2, sq2, r2, xc3, sq3, r3 = (sb(n, [P, TOK]) for n in ("xc2", "sq2", "r2", "xc3", "sq3", "r3"))
    xn2, xn3, h2 = (sb(n, [P, 2, TOK]) for n in ("xn2", "xn3", "h2"))
    delta, mag, pos, drive, states, y = (sb(n, [P, 2 * TOK]) for n in ("delta", "mag", "pos", "drive", "states", "y"))
    decay, om = (sb(n, [P, 2, 2 * TOK]) for n in ("decay", "om"))
    def bank(name):
        return ctx.enter_context(nc.psum_tensor(name, [P, CH], F32))
    b_x, b_bc, b_d, b_l2, b_l3, b_g0, b_g1, b_y = (bank("s_" + n) for n in ("x", "bc", "d", "l2", "l3", "g0", "g1", "y"))

    zeroed, loaded, masks = (sem("w2_" + n) for n in ("zeroed", "loaded", "masks"))
    block = ctx.enter_context(nc.Block())
    LOADS, ZEROED, MASKS = 16 * 9, 4, 7

    mean2, centred2, squared2, var2, ln2, rstd2, norm2 = (sem("s2_" + n) for n in "mean centred squared var ln rstd norm".split())
    proj_b, proj_x, proj_c, proj_d = (sem("s2_proj_" + n) for n in "bxcd")
    biased, magnitude, exp_mag, log_mag, softplus, decayed, one_minus, gated, driven, scanned, gated_y, y_out, h2_ready = (sem("s2_" + n) for n in
        "biased magnitude exp_mag log_mag softplus decayed one_minus gated driven scanned gated_y y_out h2_ready".split())
    mean3, centred3, squared3, var3, ln3, rstd3, norm3 = (sem("s3_" + n) for n in "mean centred squared var ln rstd norm".split())
    h_kept, x_rows, x_kept, logits01, logits23, kept01, kept23 = (sem("s3_" + n) for n in "h_kept x_rows x_kept logits01 logits23 kept01 kept23".split())

    def due(n):
        return not isinstance(n, int) or n > 0

    def there(t):
        return not isinstance(t, int) or 0 <= t < TILES

    def sweep(eng, step):
        for i in range(-2, 4):
            step(0, i)
        with eng.Fori(2, TILES // 2 - 1) as k:
            step(k, 0)
            step(k, 1)
        for i in range(TILES - 2, TILES + 2):
            step(0, i)

    @block.sync
    def _(sp):
        sp.wait_ge(zeroed, 1)
        for b in range(2):
            s = slice(C * b, C * b + C)
            sp.dma_start(w_p[s, b, :, :], A["scan_weights"].rearrange("c (k n) -> c k n", k=4)).then_inc(loaded, 16)
        sp.dma_start(w_y[:, :], A["L0_attn_Wy"]).then_inc(loaded, 16)
        sp.dma_start(b1[:, 0:NODES], A["b1r"].broadcast_to([P, NODES])).then_inc(loaded, 16)

    @block.gpsimd
    def _(pool):
        g = nc.gpsimd
        done = [0]

        def step(ins):
            ins.then_inc(masks, 1)
            done[0] += 1
            pool.wait_ge(masks, done[0])
        step(g.memset(avg[:, :], 1.0 / C))
        for m in range(2):
            v = avg[:, C * m:C * m + C]
            step(g.affine_select(out=v, in_=v, compare_op=ALU.is_ge, fill=0.0, base=-C * m, pattern=[[0, C]], channel_multiplier=1))
            step(g.affine_select(out=v, in_=v, compare_op=ALU.is_ge, fill=0.0, base=C * m + C - 1, pattern=[[0, C]], channel_multiplier=-1))
        step(g.memset(ident[:, :], 0.0))
        step(g.affine_select(out=ident[:, :], in_=ident[:, :], compare_op=ALU.not_equal, fill=1.0, base=0, pattern=[[-1, P]], channel_multiplier=1))

    @block.tensor
    def _(pe):
        mm = nc.tensor.matmul

        def project(bk, kind, t, q, done):
            for b in range(2):
                j = mm(bk[:, TOK * b:TOK * b + TOK], w_p[:, b, kind, :], xn2[:, q, :], start=True, stop=True)
            j.then_inc(done, 1)

        def step(k, o):
            i = 2 * k + o
            q = o % 2
            if there(i):
                pe.wait_ge(norm2, i + 1)
                if due(i):
                    pe.wait_ge(gated_y, i)
                project(b_bc, 1, i, q, proj_b)
                project(b_x, 0, i, q, proj_x)
            if isinstance(i, int) and i == -1:
                pe.wait_ge(loaded, LOADS)
            if there(i + 1):
                pe.wait_ge(norm2, i + 2)
                if due(i + 1):
                    pe.wait_ge(biased, i + 1)
                project(b_d, 3, i + 1, 1 - q, proj_d)
            if there(i):
                pe.wait_ge(gated, i + 1)
                project(b_bc, 2, i, q, proj_c)
            if there(i - 1):
                pe.wait_ge(h2_ready, i)
                if due(i - 1):
                    pe.wait_ge(ln3, i - 1)
                for f in range(2):
                    nc.tensor.transpose(b_l3[:, TOK + P * f:TOK + P * f + P], h2[:, 1 - q, P * f:P * f + P], ident[:, :])
                mm(b_l3[:, 0:TOK], avg[:, :], h2[:, 1 - q, :], start=True, stop=True).then_inc(mean3, 1)
            if there(i + 2):
                if due(i + 2):
                    pe.wait_ge(ln2, i + 2)
                mm(b_l2[:, 0:TOK], avg[:, :], h1[:, bass.ts(i + 2, TOK)], start=True, stop=True).then_inc(mean2, 1)
            if there(i - 2):
                pe.wait_ge(norm3, i - 1)
                if there(i - 1):
                    pe.wait_ge(h2_ready, i)
                for f in range(2):
                    j = nc.tensor.transpose(b_y[:, P * f:P * f + P], xn3[:, q, P * f:P * f + P], ident[:, :])
                j.then_inc(x_rows, 1)
                if due(i - 2):
                    pe.wait_ge(kept01, i - 2)
                for f in range(2):
                    j = mm(b_g0[:, 256 * f:256 * f + 256], xn3[:, q, P * f:P * f + P], w1[:, 0, :], start=True, stop=True)
                j.then_inc(logits01, 1)
            if there(i - 1):
                pe.wait_ge(squared3, i)
                pe.wait_ge(h_kept, i)
                mm(b_l3[:, 0:TOK], avg[:, :], sq3[:, :], start=True, stop=True).then_inc(var3, 1)
            if there(i):
                pe.wait_ge(gated_y, i + 1)
                if there(i - 2):
                    pe.wait_ge(x_kept, i - 1)
                for b in range(2):
                    j = mm(b_y[C * b:C * b + C, TOK:2 * TOK], w_y[:, :], y[:, TOK * b:TOK * b + TOK], start=True, stop=True)
                j.then_inc(y_out, 1)
            if there(i + 2):
                pe.wait_ge(squared2, i + 3)
                mm(b_l2[:, 0:TOK], avg[:, :], sq2[:, :], start=True, stop=True).then_inc(var2, 1)
            if there(i - 2):
                if due(i - 2):
                    pe.wait_ge(kept23, i - 2)
                for f in range(2):
                    j = mm(b_g1[:, 256 * f:256 * f + 256], xn3[:, q, P * f:P * f + P], w1[:, 1, :], start=True, stop=True)
                j.then_inc(logits23, 1)

        pe.wait_ge(masks, MASKS)
        sweep(pe, step)

    @block.scalar
    def _(act):
        a = nc.scalar
        act.preload_act_table_set("natural_log_exp_and_others")
        act.dma_start(b_p[:, 0:4], A["scan_biases"]).then_inc(loaded, 16)
        for b in range(2):
            act.dma_start(b_p[C * b:C * b + C, 4:5], A["L0_attn_by"].rearrange("(c o) -> c o", o=1)).then_inc(loaded, 16)
        act.wait_ge(zeroed, 4)
        for b in range(2):
            act.dma_start(w1[C * b:C * b + C, b, 0:NODES], A["w1T"]).then_inc(loaded, 16)

        def step(k, o):
            i = 2 * k + o
            q = o % 2
            if there(i + 1):
                act.wait_ge(proj_d, i + 2)
                a.activation(delta[:, :], b_d[:, :], ACT.Identity, bias=b_p[:, 3:4]).then_inc(biased, 1)
                act.wait_ge(biased, i + 2)
                a.activation(mag[:, :], delta[:, :], ACT.Abs).then_inc(magnitude, 1)
                act.wait_ge(magnitude, i + 2)
                a.activation(mag[:, :], mag[:, :], ACT.Exp, scale=-1.0).then_inc(exp_mag, 1)
            if there(i - 1):
                act.wait_ge(centred3, i)
                a.activation(sq3[:, :], xc3[:, :], ACT.Square).then_inc(squared3, 1)
                a.activation(pay[:, bass.ts(i - 1, 4), 76:140].rearrange("p (b f) c -> p f b c", b=2),
                             b_l3[:, TOK:2 * TOK].rearrange("p (f b c) -> p f b c", f=2, b=2), ACT.Copy).then_inc(h_kept, 1)
            if there(i - 2):
                act.wait_ge(x_rows, i - 1)
                a.activation(pay[:, bass.ts(i - 2, 4), 0:C].rearrange("p (b f) c -> p f b c", b=2),
                             b_y[:, 0:TOK].rearrange("p (f b c) -> p f b c", f=2, b=2), ACT.Copy).then_inc(x_kept, 1)
            if there(i + 2):
                act.wait_ge(centred2, i + 3)
                a.activation(sq2[:, :], xc2[:, :], ACT.Square).then_inc(squared2, 1)
            if there(i + 1):
                act.wait_ge(exp_mag, i + 2)
                a.activation(mag[:, :], mag[:, :], ACT.Ln, bias=1.0).then_inc(log_mag, 1)
            if there(i - 1):
                act.wait_ge(var3, i)
                a.activation(r3[:, :], b_l3[:, 0:TOK], ACT.Ln, bias=eps[:, :]).then_inc(ln3, 1)
                act.wait_ge(ln3, i)
                a.activation(r3[:, :], r3[:, :], ACT.Exp, scale=-0.5).then_inc(rstd3, 1)
            if there(i + 1):
                act.wait_ge(softplus, i + 2)
                if due(i):
                    act.wait_ge(scanned, 2 * i)
                a.activation(decay[:, 1 - q, :], pos[:, :], ACT.Exp, scale=-1.0).then_inc(decayed, 1)
            if there(i + 2):
                act.wait_ge(var2, i + 3)
                a.activation(r2[:, :], b_l2[:, 0:TOK], ACT.Ln, bias=eps[:, :]).then_inc(ln2, 1)
                act.wait_ge(ln2, i + 3)
                a.activation(r2[:, :], r2[:, :], ACT.Exp, scale=-0.5).then_inc(rstd2, 1)

        sweep(act, step)

    @block.vector
    def _(v):
        d = nc.vector

        nc.vector.memset(w_p[:, :, :, :], 0.0).then_inc(zeroed, 1)
        nc.vector.memset(eps[:, :], EPS).then_inc(zeroed, 1)
        nc.vector.memset(b1[:, NODES:256], 0.0).then_inc(zeroed, 1)
        nc.vector.memset(w1[:, :, :], 0.0).then_inc(zeroed, 1)
        v.wait_ge(zeroed, ZEROED)

        def keep_logits(t, f, bk, ready, kept):
            v.wait_ge(ready, t + 1)
            d.tensor_tensor(lg[:, bass.ds(4 * t + 2 * f, 2), :], bk[:, :].rearrange("p (f n) -> p f n", f=2),
                            b1[:, :].rearrange("p (o n) -> p o n", o=1).broadcast_to([P, 2, 256]), ALU.add).then_inc(kept, 1)

        def step(k, o):
            i = 2 * k + o
            q = o % 2
            if there(i):
                v.wait_ge(proj_b, i + 1)
                v.wait_ge(one_minus, i + 1)
                d.scalar_tensor_tensor(om[:, q, :], b_bc[:, :], b_p[:, 1:2], om[:, q, :], ALU.add, ALU.mult).then_inc(gated, 1)
                v.wait_ge(gated, i + 1)
                v.wait_ge(proj_x, i + 1)
                d.scalar_tensor_tensor(drive[:, :], b_x[:, :], b_p[:, 0:1], om[:, q, :], ALU.add, ALU.mult).then_inc(driven, 1)
                v.wait_ge(driven, i + 1)
                v.wait_ge(decayed, i + 1)
                for b in range(2):
                    s = slice(TOK * b, TOK * b + TOK)
                    d.tensor_tensor_scan(states[:, s], decay[:, q, s], drive[:, s], 0.0, ALU.mult, ALU.add).then_inc(scanned, 1)
                v.wait_ge(scanned, 2 * i + 2)
                v.wait_ge(proj_c, i + 1)
                d.scalar_tensor_tensor(y[:, :], b_bc[:, :], b_p[:, 2:3], states[:, :], ALU.add, ALU.mult).then_inc(gated_y, 1)
            if there(i - 1):
                v.wait_ge(mean3, i)
                if due(i - 1):
                    v.wait_ge(norm3, i - 1)
                d.tensor_tensor(xc3[:, :], h2[:, 1 - q, :], b_l3[:, 0:TOK], ALU.subtract).then_inc(centred3, 1)
            if there(i + 2):
                v.wait_ge(mean2, i + 3)
                if due(i + 2):
                    v.wait_ge(norm2, i + 2)
                d.tensor_tensor(xc2[:, :], h1[:, bass.ts(i + 2, TOK)], b_l2[:, 0:TOK], ALU.subtract).then_inc(centred2, 1)
            if there(i - 2):
                keep_logits(i - 2, 0, b_g0, logits01, kept01)
            if there(i + 1):
                v.wait_ge(log_mag, i + 2)
                d.scalar_tensor_tensor(pos[:, :], delta[:, :], 0.0, mag[:, :], ALU.max, ALU.add).then_inc(softplus, 1)
            if there(i):
                v.wait_ge(y_out, i + 1)
                d.scalar_tensor_tensor(h2[:, q, :], b_y[:, TOK:2 * TOK], b_p[:, 4:5], h1[:, bass.ts(i, TOK)], ALU.add, ALU.add).then_inc(h2_ready, 1)
            if there(i - 1):
                v.wait_ge(rstd3, i)
                d.tensor_tensor(xn3[:, 1 - q, :], xc3[:, :], r3[:, :], ALU.mult).then_inc(norm3, 1)
            if there(i + 1):
                v.wait_ge(decayed, i + 2)
                d.tensor_scalar(om[:, 1 - q, :], decay[:, 1 - q, :], -1.0, 1.0, ALU.mult, ALU.add).then_inc(one_minus, 1)
            if there(i + 2):
                v.wait_ge(rstd2, i + 3)
                d.tensor_tensor(xn2[:, q, :], xc2[:, :], r2[:, :], ALU.mult).then_inc(norm2, 1)
            if there(i - 2):
                keep_logits(i - 2, 1, b_g1, logits23, kept23)

        sweep(v, step)


I32 = mybir.dt.int32
U32 = mybir.dt.uint32
BF16 = mybir.dt.bfloat16
GRP = 32
BLK = 128
TOKENS = B * TOK
NBLK = (TOKENS + GRP * (BLK - 1)) // BLK
NBLK += -NBLK % 8
X0, P0, H0, ID0 = 0, 64, 76, 140
KT = 7


def paths_and_slots(nc, ctx, A, h1, pay, lg, bits, wt, gid, ident, rows_d):
    def sb(name, shape, dt=F32):
        return ctx.enter_context(nc.sbuf_tensor(name, shape, dt))

    def sem(name):
        return ctx.enter_context(nc.semaphore("t_" + name))

    pw = sb("pw", [P, NT, LEVELS])
    n5, n6, pl, pr, grp = (sb(n, [P, NT]) for n in ("not5", "not6", "p7_left", "p7_right", "grp"))
    hot = sb("hot", [P, NT, GRP], BF16)
    group_no, iop = sb("group_no", [P, GRP]), sb("iop", [P, 1])
    tri, one = sb("tri", [P, P], BF16), sb("one", [P, P], BF16)
    before = sb("before", [P, GRP, NT])
    first = sb("first", [P, GRP, NT])
    h1_v = h1[:, :].rearrange("p (i m) -> p i m", i=2)
    keep = h1_v[:, 0, :].rearrange("p (g n) -> p g n", g=GRP)
    rank = h1_v[:, 1, :].rearrange("p (n g) -> p n g", g=GRP)
    count, blocks, block_end, base, ended = (sb(n, [P, GRP]) for n in ("count", "blocks", "block_end", "base", "ended"))
    ones = sb("ones", [P, GRP])
    blocks_i = sb("blocks_i", [P, GRP], I32)
    slot, slot_i = sb("slot", [P, NT]), sb("slot_i", [P, NT], I32)
    block_group = sb("block_group", [P, 1])
    fill = sb("fill", [P, ROW])
    in_tile = [ctx.enter_context(nc.psum_tensor(f"in_tile{i}", [P, 512], F32)) for i in range(4)]
    tot_b = [ctx.enter_context(nc.psum_tensor(f"tot_b{i}", [P, 512], F32)) for i in range(4)]
    sum_b = in_tile[3]
    chosen, magnitudes, weight, steps, weights_done, consts, filled, zeroed, table = (sem(n) for n in
        "chosen magnitudes weight steps weights_done consts filled zeroed table".split())
    hot_ready, summed, sum_used, totals, prefixes, totals_kept, slots_ready, group_ready, group_row, gid_ready, scattered = (sem(n) for n in
        "hot_ready summed sum_used totals prefixes totals_kept slots_ready group_ready group_row gid_ready scattered".split())
    CONSTS = 12
    Q = NT // 4
    block = ctx.enter_context(nc.Block())

    @block.vector
    def _(v):
        d = nc.vector
        n = [0]

        def step(ins):
            ins.then_inc(steps, 1)
            n[0] += 1
            v.wait_ge(steps, n[0])

        for l in range(LEVELS - 1):
            s = 2 ** (LEVELS - 1 - l) - 1
            d.tensor_scalar(bits[:, l, :], lg[:, :, l], 0.0, None, ALU.is_gt).then_inc(chosen, 1)
            v.wait_ge(chosen, 2 * l + 1)
            d.copy_predicated(lg[:, :, l + 1:l + 1 + s], bits[:, l, :].rearrange("p (n o) -> p n o", o=1).broadcast_to([P, NT, s]).bitcast(U32),
                              lg[:, :, l + 1 + s:l + 1 + 2 * s]).then_inc(chosen, 1)
            v.wait_ge(chosen, 2 * l + 2)
        step(d.scalar_tensor_tensor(grp[:, :], bits[:, 0, :], 2.0, bits[:, 1, :], ALU.mult, ALU.add))
        for l in range(2, 5):
            step(d.scalar_tensor_tensor(grp[:, :], grp[:, :], 2.0, bits[:, l, :], ALU.mult, ALU.add))
        v.wait_ge(consts, CONSTS)
        d.tensor_tensor(hot[:, :, :], grp[:, :].rearrange("p (n o) -> p n o", o=1).broadcast_to([P, NT, GRP]),
                        group_no[:, :].rearrange("p (o g) -> p o g", o=1).broadcast_to([P, NT, GRP]), ALU.is_equal).then_inc(hot_ready, 1)
        d.tensor_scalar(n5[:, :], bits[:, 5, :], -1.0, 1.0, ALU.mult, ALU.add).then_inc(steps, 1)
        d.tensor_scalar(n6[:, :], bits[:, 6, :], -1.0, 1.0, ALU.mult, ALU.add).then_inc(steps, 1)
        n[0] += 2
        v.wait_ge(steps, n[0])
        v.wait_ge(summed, 1)
        step(d.tensor_reduce(count[:, :], sum_b[:, :].rearrange("p (n g) -> p g n", g=GRP), AX.X, ALU.add))
        step(d.tensor_scalar(blocks_i[:, :], count[:, :], float(BLK - 1), None, ALU.add))
        step(d.tensor_scalar(blocks_i[:, :], blocks_i[:, :], BLK.bit_length() - 1, None, ALU.logical_shift_right))
        step(d.tensor_copy(blocks[:, :], blocks_i[:, :]))
        step(d.tensor_tensor_scan(block_end[:, :], ones[:, :], blocks[:, :], 0.0, ALU.mult, ALU.add))
        step(d.tensor_tensor(base[:, :], block_end[:, :], blocks[:, :], ALU.subtract))
        step(d.tensor_scalar(before[:, :, 0], base[:, :], float(BLK), None, ALU.mult))
        d.tensor_scalar(ended[:, :], block_end[:, :], iop[:, :], None, ALU.is_le).then_inc(steps, 1)
        v.wait_ge(weight, 1)
        d.tensor_tensor(pl[:, :], pw[:, :, 7], n5[:, :], ALU.mult).then_inc(steps, 1)
        d.tensor_tensor(pr[:, :], pw[:, :, 7], bits[:, 5, :], ALU.mult).then_inc(steps, 1)
        n[0] += 3
        v.wait_ge(totals_kept, 4)
        f = lambda a: a[:, :, :].rearrange("p g n -> p (g n)")
        d.tensor_tensor_scan(f(first), f(keep), f(before), 0.0, ALU.mult, ALU.add).then_inc(steps, 1)
        n[0] += 1
        v.wait_ge(steps, n[0])
        d.tensor_copy(pay[:, :, P0:P0 + 6], pw[:, :, 0:6]).then_inc(weights_done, 1)
        for u, (a, b) in enumerate(((pw[:, :, 6], n5[:, :]), (pw[:, :, 6], bits[:, 5, :]), (pl[:, :], n6[:, :]), (pl[:, :], bits[:, 6, :]),
                                    (pr[:, :], n6[:, :]), (pr[:, :], bits[:, 6, :]))):
            d.tensor_tensor(pay[:, :, P0 + 6 + u], a, b, ALU.mult).then_inc(weights_done, 1)
        for i in range(4):
            t = slice(Q * i, Q * i + Q)
            v.wait_ge(prefixes, i + 1)
            step(d.tensor_tensor(rank[:, t, :], in_tile[i][:, :].rearrange("p (n g) -> p n g", g=GRP), first[:, :, t].rearrange("p g n -> p n g"), ALU.add))
            step(d.tensor_tensor(rank[:, t, :], rank[:, t, :], hot[:, t, :], ALU.mult))
            step(d.tensor_reduce(slot[:, t], rank[:, t, :], AX.X, ALU.add))
            d.tensor_copy(slot_i[:, t], slot[:, t]).then_inc(slots_ready, 1)
        step(d.tensor_reduce(block_group[:, :], ended[:, :], AX.X, ALU.add))
        d.tensor_scalar(block_group[:, :], block_group[:, :], float(GRP - 1), None, ALU.min).then_inc(group_ready, 1)
        v.wait_ge(group_row, 1)
        d.tensor_copy(gid[:, :], tot_b[0][0:1, 0:P]).then_inc(gid_ready, 1)

    @block.scalar
    def _(act):
        a = nc.scalar
        act.wait_ge(chosen, 2 * (LEVELS - 1))
        a.activation(pw[:, :, :], lg[:, :, 0:LEVELS], ACT.Abs).then_inc(magnitudes, 1)
        act.wait_ge(magnitudes, 1)
        a.activation(pw[:, :, :], pw[:, :, :], ACT.Gelu).then_inc(weight, 1)
        for i in range(4):
            act.wait_ge(totals, i + 1)
            m = Q if i < 3 else Q - 1
            a.activation(before[:, :, Q * i + 1:Q * i + 1 + m].rearrange("p g n -> p n g"),
                         tot_b[i][:, 0:m * GRP].rearrange("p (n g) -> p n g", g=GRP), ACT.Copy).then_inc(totals_kept, 1)

    @block.tensor
    def _(pe):
        mm = nc.tensor.matmul
        pe.wait_ge(hot_ready, 1)
        q = [hot[:, Q * i:Q * i + Q, :].rearrange("p n g -> p (n g)") for i in range(4)]
        for i in range(4):
            j = mm(sum_b[:, :], one[:, :], q[i], start=i == 0, stop=i == 3)
        j.then_inc(summed, 1)
        for i in range(4):
            mm(tot_b[i][:, :], one[:, :], q[i], start=True, stop=True).then_inc(totals, 1)
        for i in range(4):
            if i == 3:
                pe.wait_ge(steps, 7)
            mm(in_tile[i][:, :], tri[:, :], q[i], start=True, stop=True).then_inc(prefixes, 1)
        pe.wait_ge(group_ready, 1)
        pe.wait_ge(totals_kept, 1)
        mm(tot_b[0][0:1, 0:P], block_group[:, :], ident[:, :], start=True, stop=True).then_inc(group_row, 1)

    @block.gpsimd
    def _(pool):
        g = nc.gpsimd
        n = [0]

        def step(ins):
            ins.then_inc(consts, 1)
            n[0] += 1
            pool.wait_ge(consts, n[0])
        step(g.memset(fill[:, :], 0.0))
        step(g.iota(fill[:, ID0:ID0 + 1].bitcast(I32), pattern=[[0, 1]], base=TOKENS, channel_multiplier=0))
        step(g.iota(group_no[:, :], pattern=[[1, GRP]], base=0, channel_multiplier=0, allow_small_or_imprecise_dtypes=True))
        step(g.iota(iop[:, :], pattern=[[0, 1]], base=0, channel_multiplier=1, allow_small_or_imprecise_dtypes=True))
        step(g.memset(tri[:, :], 1.0))
        step(g.affine_select(out=tri[:, :], in_=tri[:, :], compare_op=ALU.is_ge, fill=0.0, base=-1, pattern=[[1, P]], channel_multiplier=-1))
        step(g.memset(one[:, :], 1.0))
        step(g.memset(ones[:, :], 1.0))
        step(g.memset(keep[:, :, :], 1.0))
        step(g.memset(keep[:, :, 0:1], 0.0))
        step(g.memset(ident[:, :], 0.0))
        step(g.affine_select(out=ident[:, :], in_=ident[:, :], compare_op=ALU.not_equal, fill=1.0, base=0, pattern=[[-1, P]], channel_multiplier=1))
        step(g.memset(wt[:, :, 6, :], 0.0))
        v = wt[:, :, 6, :]
        g.affine_select(out=v, in_=v, compare_op=ALU.not_equal, fill=1.0, base=-(H0 - 16), pattern=[[0, GRP], [-1, C]], channel_multiplier=1).then_inc(zeroed, 1)
        step(g.iota(pay[:, :, ID0:ID0 + 1].bitcast(I32), pattern=[[P, NT], [0, 1]], base=0, channel_multiplier=1))
        step(g.memset(pay[:, :, ID0 + 1:ROW], 0.0))
        pool.wait_ge(filled, 16)
        pool.wait_ge(weights_done, 7)
        for t in range(NT):
            if t % Q == 0:
                pool.wait_ge(slots_ready, t // Q + 1)
            g.indirect_dma_start(rows_d, bass.IndirectOffsetOnAxis(ap=slot_i[:, t:t + 1], axis=0), pay[:, t, :], None).then_inc(scattered, 16)

    @block.sync
    def _(sp):
        n = 0

        def ld(dst, src):
            nonlocal n
            sp.dma_start(dst, src).then_inc(table, 16)
            n += 16
        sp.wait_ge(consts, 2)
        sp.dma_start(rows_d.rearrange("(n p) c -> p n c", p=P), fill[:, :].rearrange("p (o c) -> p o c", o=1).broadcast_to([P, NBLK, ROW])).then_inc(filled, 16)
        w2 = A["w2T"]
        for l in range(6):
            k, half = l // 2, l % 2
            n0, cn = 2 ** l - 1, 2 ** l
            if l == 5:
                ld(wt[C * half:C * half + C, :, k, :], w2[:, n0:n0 + cn, :])
                continue
            r = GRP // cn
            for v in range(cn):
                ld(wt[C * half:C * half + C, v * r:(v + 1) * r, k, :], w2[:, n0 + v:n0 + v + 1, :].broadcast_to([C, r, C]))
        for half in range(2):
            ld(wt[C * half:C * half + C, :, 3, :], w2[:, 63:127, :].rearrange("d (g u) o -> d g u o", u=2)[:, :, half, :])
            for m in range(2):
                ld(wt[C * half:C * half + C, :, 4 + m, :], w2[:, 127:255, :].rearrange("d (g u) o -> d g u o", u=4)[:, :, 2 * m + half, :])
        sp.wait_ge(zeroed, 1)
        b2 = A["L0_ffn_b2s"]
        for l in range(6):
            n0, cn = 2 ** l - 1, 2 ** l
            r = GRP // cn
            q = P0 - 16 + l
            ld(wt[q:q + 1, :, 6, :].rearrange("q (v r) o -> q v r o", r=r),
               b2[n0:n0 + cn, :].rearrange("(q v r) o -> q v r o", q=1, r=1).broadcast_to([1, cn, r, C]))
        for l, per in ((6, 2), (7, 4)):
            n0, cn = 2 ** l - 1, 2 ** l
            for u in range(per):
                q = P0 - 16 + (6 if l == 6 else 8) + u
                ld(wt[q:q + 1, :, 6, :], b2[n0:n0 + cn, :].rearrange("(q g u) o -> q g u o", q=1, u=per)[:, :, u, :])
        sp.wait_ge(table, n)
        sp.wait_ge(scattered, 16 * NT)


def mix_blocks(nc, ctx, lg, wt, gid, ident, rows_d, out_d):
    def sb(name, shape, dt=F32):
        return ctx.enter_context(nc.sbuf_tensor(name, shape, dt))

    def sem(name):
        return ctx.enter_context(nc.semaphore(name))

    ROWS, RING, LOOKAHEAD = 8, 4, 6
    PAIRS, TURN = NBLK // 2, ROWS // 2
    TURNS, PEELED = NBLK // ROWS, 2
    free = [lg[:, :, :].rearrange("p n m -> p (n m)"), 0]

    def take(*shape):
        size = int(np.prod(shape))
        a = free[0][:, free[1]:free[1] + size]
        free[1] += size
        if len(shape) == 2:
            return a.rearrange("p (a b) -> p a b", a=shape[0])
        return a.rearrange("p (a b c) -> p a b c", a=shape[0], b=shape[1])
    rows = take(ROWS, ROW)
    ids = sb("ids", [P, 2 * ROWS], I32)
    xs = take(RING, UNITS, C)
    xsT = take(RING, KT, P)
    w_cur = take(RING, KT, C)
    oT = sb("oT", [P, 2, P])
    orow = sb("orow", [P, ROWS, C])
    turned = [[ctx.enter_context(nc.psum_tensor(f"turned{i}{n}", [P, 512], F32)) for n in "ab"] for i in range(2)]
    ob = [ctx.enter_context(nc.psum_tensor(f"mixed_bank{i}", [P, 512], F32)) for i in range(2)]
    rb = [ctx.enter_context(nc.psum_tensor(f"back_bank{i}", [P, 512], F32)) for i in range(2)]
    scaled, turned_a, turned_b, kept_a, kept_b, w_kept, mixed, mixed_kept, back, back_kept, ids_kept = (sem("m_" + n) for n in
        "scaled turned_a turned_b kept_a kept_b w_kept mixed mixed_kept back back_kept ids_kept".split())
    rows_in = [sem(f"m_rows_in{i}") for i in range(ROWS)]
    written = [sem(f"m_written{i}") for i in range(ROWS)]
    rows_v = rows_d.rearrange("(n p) c -> n p c", p=P)
    block = ctx.enter_context(nc.Block())

    def due(n):
        return not isinstance(n, int) or n > 0

    def there(m):
        return not isinstance(m, int) or 0 <= m < PAIRS

    def steps_of(eng, step, skew):
        for m in range(PEELED * TURN):
            step(m // TURN, m % TURN)
        with eng.Fori(PEELED, TURNS) as k:
            for j in range(TURN):
                step(k, j)
        for m in range(PAIRS, PAIRS + skew):
            step(m // TURN, m % TURN)

    @block.sync
    def _(sp):
        def load(k, i):
            b = ROWS * k + i
            if due(b - ROWS + 1):
                sp.wait_ge(scaled, b - ROWS + 1)
                sp.wait_ge(turned_b, b - ROWS + 1)
                sp.wait_ge(ids_kept, b - ROWS + 1)
            src = rows_v[b, :, :] if isinstance(b, int) else rows_v[bass.ds(b, 1), :, :].rearrange("o p c -> (o p) c")
            sp.dma_start(rows[:, i, :], src).then_inc(rows_in[i], 16)
        for i in range(ROWS):
            load(0, i)
        with sp.Fori(1, TURNS) as k:
            for i in range(ROWS):
                load(k, i)

    @block.vector
    def _(v):
        d = nc.vector

        def step(k, j):
            m = TURN * k + j
            for h in range(2):
                if there(m):
                    b, i = 2 * m + h, 2 * j + h
                    v.wait_ge(rows_in[i], 16 * (k + 1))
                    if due(b - RING + 1):
                        v.wait_ge(turned_a, b - RING + 1)
                        v.wait_ge(turned_b, b - RING + 1)
                    d.tensor_tensor(xs[:, i % RING, :, :], rows[:, i, X0:X0 + C].rearrange("p (o c) -> p o c", o=1).broadcast_to([P, UNITS, C]),
                                    rows[:, i, P0:P0 + UNITS].rearrange("p (u o) -> p u o", o=1).broadcast_to([P, UNITS, C]), ALU.mult).then_inc(scaled, 1)
                if there(m - 1):
                    b, i = 2 * m - 2 + h, (2 * j - 2 + h) % ROWS
                    v.wait_ge(turned_b, b + 1)
                    if due(m - 2):
                        v.wait_ge(mixed, m - 2)
                    d.tensor_copy(xsT[:, i % RING, 4:KT, :], turned[h][1][:, 0:3 * P].rearrange("p (u n) -> p u n", u=3)).then_inc(kept_b, 1)
            if there(m - 2):
                v.wait_ge(mixed, m - 1)
                if due(m - 3):
                    v.wait_ge(back, m - 3)
                d.tensor_copy(oT[:, j % 2, :], ob[j % 2][:, 0:P]).then_inc(mixed_kept, 1)
        steps_of(v, step, 2)

    @block.scalar
    def _(act):
        a = nc.scalar

        def step(k, j):
            m = TURN * k + j
            for h in range(2):
                if there(m):
                    b, i = 2 * m + h, 2 * j + h
                    g = act.value_load(gid[0:1, b:b + 1] if isinstance(b, int) else gid[0:1, bass.ds(b, 1)], min_val=0, max_val=GRP - 1)
                    if due(m - 1):
                        act.wait_ge(mixed, m - 1)
                    a.activation(w_cur[:, i % RING, :, :], wt[:, bass.ds(g, 1), :, :].rearrange("p o k c -> p (o k) c"), ACT.Copy).then_inc(w_kept, 1)
                    act.wait_ge(turned_a, b + 1)
                    a.activation(xsT[:, i % RING, 0:4, :], turned[h][0][:, :].rearrange("p (u n) -> p u n", u=4), ACT.Copy).then_inc(kept_a, 1)
            if there(m - 2):
                i = (2 * j - 4) % ROWS
                act.wait_ge(back, m - 1)
                q = k if j >= 2 else k - 1
                if due(q):
                    act.wait_ge(written[i], 16 * q)
                    act.wait_ge(written[i + 1], 16 * q)
                a.activation(orow[:, i:i + 2, :], rb[j % 2][:, 0:P].rearrange("p (b c) -> p b c", b=2), ACT.Copy).then_inc(back_kept, 1)
        steps_of(act, step, 2)

    @block.tensor
    def _(pe):
        mm = nc.tensor.matmul

        def step(k, j):
            m = TURN * k + j
            for h in range(2):
                if there(m):
                    b, i = 2 * m + h, 2 * j + h
                    pe.wait_ge(scaled, b + 1)
                    if due(b - 1):
                        pe.wait_ge(kept_a, b - 1)
                    for u in range(4):
                        t = nc.tensor.transpose(turned[h][0][:, P * u:P * u + P], xs[:, i % RING, 2 * u:2 * u + 2, :].rearrange("p a c -> p (a c)"), ident[:, :])
                    t.then_inc(turned_a, 1)
                    if due(b - 1):
                        pe.wait_ge(kept_b, b - 1)
                    for u in range(2):
                        nc.tensor.transpose(turned[h][1][:, P * u:P * u + P], xs[:, i % RING, 8 + 2 * u:10 + 2 * u, :].rearrange("p a c -> p (a c)"), ident[:, :])
                    pe.wait_ge(rows_in[i], 16 * (k + 1))
                    nc.tensor.transpose(turned[h][1][:, 2 * P:3 * P], rows[:, i, 16:ROW], ident[:, :]).then_inc(turned_b, 1)
            if there(m - 1):
                i = (2 * j - 2) % RING
                pe.wait_ge(kept_a, 2 * m)
                pe.wait_ge(kept_b, 2 * m)
                pe.wait_ge(w_kept, 2 * m)
                if due(m - 2):
                    pe.wait_ge(mixed_kept, m - 2)
                for u in range(KT):
                    for h in range(2):
                        t = mm(ob[(j + 1) % 2][C * h:C * h + C, 0:P], w_cur[:, i + h, u, :], xsT[:, i + h, u, :], start=u == 0, stop=u == KT - 1)
                t.then_inc(mixed, 1)
            if there(m - 2):
                pe.wait_ge(mixed_kept, m - 1)
                if due(m - 3):
                    pe.wait_ge(back_kept, m - 3)
                nc.tensor.transpose(rb[j % 2][:, 0:P], oT[:, j % 2, :], ident[:, :]).then_inc(back, 1)
        steps_of(pe, step, 2)

    @block.gpsimd
    def _(pool):
        def take_ids(b):
            pool.wait_ge(rows_in[b % ROWS], 16 * (b // ROWS + 1))
            if b >= 2 * ROWS:
                pool.wait_ge(written[b % ROWS], 16 * (b // ROWS - 1))
            nc.gpsimd.tensor_copy(ids[:, b % (2 * ROWS):b % (2 * ROWS) + 1], rows[:, b % ROWS, ID0:ID0 + 1].bitcast(I32)).then_inc(ids_kept, 1)
        for b in range(LOOKAHEAD):
            take_ids(b)
        for b in range(NBLK):
            if b + LOOKAHEAD < NBLK:
                take_ids(b + LOOKAHEAD)
            pool.wait_ge(ids_kept, b + 1)
            pool.wait_ge(back_kept, b // 2 + 1)
            nc.gpsimd.indirect_dma_start(out_d, bass.IndirectOffsetOnAxis(ap=ids[:, b % (2 * ROWS):b % (2 * ROWS) + 1], axis=0), orow[:, b % ROWS, :], None,
                                         bounds_check=TOKENS - 1, oob_is_err=False).then_inc(written[b % ROWS], 16)
        for i in range(ROWS):
            pool.wait_ge(written[i], 16 * TURNS)


def program(nc, A, out):
    rows_d = nc.dram_tensor("rows_sorted", (NBLK * BLK, ROW), F32, kind="Internal").ap()
    with ExitStack() as top:
        h1 = top.enter_context(nc.sbuf_tensor("h1", [P, TILES * TOK], F32))
        with ExitStack() as ctx:
            tokenizer(nc, ctx, A, h1)
        pay = top.enter_context(nc.sbuf_tensor("pay", [P, NT, ROW], F32))
        lg = top.enter_context(nc.sbuf_tensor("lg", [P, NT, 256], F32))
        with ExitStack() as ctx:
            scan_and_logits(nc, ctx, A, h1, pay, lg)
        bits = top.enter_context(nc.sbuf_tensor("bits", [P, LEVELS - 1, NT], F32))
        wt = top.enter_context(nc.sbuf_tensor("wt", [P, GRP, KT, C], F32))
        gid = top.enter_context(nc.sbuf_tensor("gid", [1, P], I32))
        ident = top.enter_context(nc.sbuf_tensor("ident3", [P, P], F32))
        with ExitStack() as ctx:
            paths_and_slots(nc, ctx, A, h1, pay, lg, bits, wt, gid, ident, rows_d)
        with ExitStack() as ctx:
            mix_blocks(nc, ctx, lg, wt, gid, ident, rows_d, out)


def preorder(node=0, level=0):
    if level == LEVELS - 1:
        return [node]
    return [node] + preorder(2 * node + 1, level + 1) + preorder(2 * node + 2, level + 1)


_INS = ["x", "L0_attn_Wy", "L0_attn_by", "L0_ffn_b2s"]


def kernel(**inputs):
    import concourse.bacc as bacc
    from concourse.bass_utils import run_bass_kernel_spmd

    arrays = {n: np.ascontiguousarray(inputs[n]) for n in _INS}
    order = preorder()
    arrays["tok_weights"] = np.ascontiguousarray(np.concatenate([np.asarray(inputs["L0_tok_" + n]) for n in ("Wq", "Wkv", "proj_w")]).T)
    arrays["tok_vectors"] = np.ascontiguousarray(np.stack([np.asarray(inputs["L0_tok_" + n]) for n in ("ln_q_w", "ln_q_b", "ln_kv_w", "ln_kv_b", "proj_b")], axis=1))
    arrays["scan_weights"] = np.ascontiguousarray(np.concatenate([np.asarray(inputs["L0_attn_" + n]) for n in ("Wx", "Wbc", "Wd")], axis=1))
    arrays["scan_biases"] = np.ascontiguousarray(np.concatenate([np.asarray(inputs["L0_attn_" + n]) for n in ("bx", "bbc", "bd")]).reshape(4, N_ST).T)
    arrays["w1T"] = np.ascontiguousarray(np.asarray(inputs["L0_ffn_w1s"])[order].T)
    arrays["b1r"] = np.ascontiguousarray(np.asarray(inputs["L0_ffn_b1s"])[order].reshape(1, NODES))
    arrays["w2T"] = np.ascontiguousarray(np.asarray(inputs["L0_ffn_w2s"]).transpose(1, 0, 2))

    nc = bacc.Bacc("TRN2", target_bir_lowering=False, num_devices=1)
    A = {n: nc.dram_tensor("in_" + n, a.shape, mybir.dt.from_np(a.dtype), kind="ExternalInput").ap() for n, a in arrays.items()}
    out = nc.dram_tensor("out", (TOKENS, C), F32, kind="ExternalOutput").ap()
    program(nc, A, out)
    r = run_bass_kernel_spmd(nc, [{"in_" + n: a for n, a in arrays.items()}], core_ids=[0])
    return r.results[0]["out"].reshape(B, TOK, C)
```
